# Optimizing a Trainium2 kernel written in Bass

```python
import numpy as np
import jax
import jax.numpy as jnp

def _softmax(x, axis=-1):
    return jax.nn.softmax(x, axis=axis)

def _gelu(x):
    return jax.nn.gelu(x, approximate=True)

def _silu(x):
    return jax.nn.silu(x)

def _sigmoid(x):
    return jax.nn.sigmoid(x)

def _layernorm(x, axis=-1, eps=1e-05):
    m = jnp.mean(x, axis=axis, keepdims=True)
    v = jnp.var(x, axis=axis, keepdims=True)
    return (x - m) / jnp.sqrt(v + eps)

def _scatter_add(tgt, idx, src, axis=0):
    return tgt.at[idx].add(src)

def _segment_sum(src, seg, n):
    return jax.ops.segment_sum(src, seg, n)
kernel_name = 'mk_xattn_ffn_d1_seqx_r4_21e250'

def setup_inputs(seed: int=0):
    np.random.seed(seed)
    _w = jnp.asarray

    def _rec_inputs():
        import jax
        import jax.numpy as jnp
        _rk = jax.random.key(seed)
        x = -0.000125 + 0.9999 * jax.random.normal(jax.random.fold_in(_rk, 1), (16, 256, 256), jnp.float32)
        _lenS = 256 - jax.random.randint(jax.random.fold_in(_rk, 7), (16,), 0, max(1, 256 // 4) + 1, jnp.int32)
        _lenS2 = 77 - jax.random.randint(jax.random.fold_in(_rk, 8), (16,), 0, max(1, 77 // 4) + 1, jnp.int32)
        _ctx_768P = jax.random.normal(jax.random.fold_in(_rk, 11), (16, 16, 192), jnp.float32)
        _ctx_768c = jax.random.dirichlet(jax.random.fold_in(_rk, 511), 0.3 * jnp.ones((16,), jnp.float32), (16, 77))
        _ctx_768t = jnp.einsum('bsk,bkd->bsd', _ctx_768c, _ctx_768P)
        _ctx_768t = _ctx_768t * jax.lax.rsqrt(jnp.mean(jnp.square(_ctx_768t)) + 1e-12) * 0.953939
        ctx_768 = 0.00243539 + 0.99952 * (_ctx_768t + 0.3 * jax.random.normal(jax.random.fold_in(_rk, 611), (16, 77, 192), jnp.float32))
        return (x, ctx_768)
    x, ctx_768 = _rec_inputs()

    def _L0_xattn_setup():
        import jax, jax.numpy as jnp
        import numpy as np
        HEADS = 16
        DIM_HEAD = 64
        RANK = 32
        LORA_W = 1.0
        IPA_SCALE = 1.0
        IPA_TOKENS = 4
        SCALE = DIM_HEAD ** (-0.5)

        def _split_heads(t):
            b, n, _ = t.shape
            return t.reshape(b, n, HEADS, DIM_HEAD).transpose(0, 2, 1, 3)

        def _merge_heads(t):
            b, h, n, d = t.shape
            return t.transpose(0, 2, 1, 3).reshape(b, n, h * d)

        def _attention(q_in, k_in, v_in):
            q = _split_heads(q_in)
            k = _split_heads(k_in)
            v = _split_heads(v_in)
            s = jnp.einsum('bhid,bhjd->bhij', q, k) * SCALE
            p = jax.nn.softmax(s, axis=-1)
            o = jnp.einsum('bhij,bhjd->bhid', p, v)
            return _merge_heads(o)

        def _lora(t, down, up, alpha):
            return t @ down @ up * (LORA_W * alpha[0] / RANK)
        key = jax.random.key(seed)
        ks = jax.random.split(key, 20)
        B, N, QD, CD, ID = (8, 1024, 256, 192, HEADS * DIM_HEAD)
        CTX = 77 + IPA_TOKENS
        s = 0.02
        return {'x': jax.random.normal(ks[0], (B, N, QD), jnp.float32), 'context': jax.random.normal(ks[1], (B, CTX, CD), jnp.float32), 'Wq': jax.random.normal(ks[2], (QD, ID), jnp.float32) * s, 'Wk': jax.random.normal(ks[3], (CD, ID), jnp.float32) * s, 'Wv': jax.random.normal(ks[4], (CD, ID), jnp.float32) * s, 'Wo': jax.random.normal(ks[5], (ID, QD), jnp.float32) * s, 'bo': jnp.zeros((QD,), jnp.float32), 'q_down': jax.random.normal(ks[6], (QD, RANK), jnp.float32) * s, 'q_up': jax.random.normal(ks[7], (RANK, ID), jnp.float32) * s, 'q_alpha': jnp.ones((1,), jnp.float32) * RANK, 'k_down': jax.random.normal(ks[8], (CD, RANK), jnp.float32) * s, 'k_up': jax.random.normal(ks[9], (RANK, ID), jnp.float32) * s, 'k_alpha': jnp.ones((1,), jnp.float32) * RANK, 'v_down': jax.random.normal(ks[10], (CD, RANK), jnp.float32) * s, 'v_up': jax.random.normal(ks[11], (RANK, ID), jnp.float32) * s, 'v_alpha': jnp.ones((1,), jnp.float32) * RANK, 'o_down': jax.random.normal(ks[12], (ID, RANK), jnp.float32) * s, 'o_up': jax.random.normal(ks[13], (RANK, QD), jnp.float32) * s, 'o_alpha': jnp.ones((1,), jnp.float32) * RANK, 'Wk_ipa': jax.random.normal(ks[14], (CD, ID), jnp.float32) * s, 'Wv_ipa': jax.random.normal(ks[15], (CD, ID), jnp.float32) * s}
    _L0_xattn_all = _L0_xattn_setup()
    _L0_xattn_in = {k: v for k, v in _L0_xattn_all.items() if k in ('Wq', 'Wk', 'Wv', 'Wo', 'bo', 'q_down', 'q_up', 'q_alpha', 'k_down', 'k_up', 'k_alpha', 'v_down', 'v_up', 'v_alpha', 'o_down', 'o_up', 'o_alpha', 'Wk_ipa', 'Wv_ipa')}
    del _L0_xattn_all

    def _L0_ffn_setup():
        import jax, jax.numpy as jnp
        import numpy as np
        D_MODEL, D_FF, N_EXPERTS, TOP_K = (256, 512, 8, 2)
        B, S = (2, 512)
        key = jax.random.key(seed)
        k1, k2, k3, k4 = jax.random.split(key, 4)
        scale = 0.02
        return {'x': jax.random.normal(k1, (B, S, D_MODEL), dtype=jnp.float32), 'gate_w': jax.random.normal(k2, (D_MODEL, N_EXPERTS), dtype=jnp.float32) * scale, 'w1': jax.random.normal(k3, (N_EXPERTS, D_MODEL, D_FF), dtype=jnp.float32) * scale, 'w2': jax.random.normal(k4, (N_EXPERTS, D_FF, D_MODEL), dtype=jnp.float32) * scale}
    _L0_ffn_all = _L0_ffn_setup()
    _L0_ffn_in = {k: v for k, v in _L0_ffn_all.items() if k in ('gate_w', 'w1', 'w2')}
    del _L0_ffn_all
    return {'x': x, 'ctx_768': ctx_768, 'L0_xattn_Wq': _L0_xattn_in['Wq'], 'L0_xattn_Wk': _L0_xattn_in['Wk'], 'L0_xattn_Wv': _L0_xattn_in['Wv'], 'L0_xattn_Wo': _L0_xattn_in['Wo'], 'L0_xattn_bo': _L0_xattn_in['bo'], 'L0_xattn_q_down': _L0_xattn_in['q_down'], 'L0_xattn_q_up': _L0_xattn_in['q_up'], 'L0_xattn_q_alpha': _L0_xattn_in['q_alpha'], 'L0_xattn_k_down': _L0_xattn_in['k_down'], 'L0_xattn_k_up': _L0_xattn_in['k_up'], 'L0_xattn_k_alpha': _L0_xattn_in['k_alpha'], 'L0_xattn_v_down': _L0_xattn_in['v_down'], 'L0_xattn_v_up': _L0_xattn_in['v_up'], 'L0_xattn_v_alpha': _L0_xattn_in['v_alpha'], 'L0_xattn_o_down': _L0_xattn_in['o_down'], 'L0_xattn_o_up': _L0_xattn_in['o_up'], 'L0_xattn_o_alpha': _L0_xattn_in['o_alpha'], 'L0_xattn_Wk_ipa': _L0_xattn_in['Wk_ipa'], 'L0_xattn_Wv_ipa': _L0_xattn_in['Wv_ipa'], 'L0_ffn_gate_w': _L0_ffn_in['gate_w'], 'L0_ffn_w1': _L0_ffn_in['w1'], 'L0_ffn_w2': _L0_ffn_in['w2']}

def reference(x, ctx_768, L0_xattn_Wq, L0_xattn_Wk, L0_xattn_Wv, L0_xattn_Wo, L0_xattn_bo, L0_xattn_q_down, L0_xattn_q_up, L0_xattn_q_alpha, L0_xattn_k_down, L0_xattn_k_up, L0_xattn_k_alpha, L0_xattn_v_down, L0_xattn_v_up, L0_xattn_v_alpha, L0_xattn_o_down, L0_xattn_o_up, L0_xattn_o_alpha, L0_xattn_Wk_ipa, L0_xattn_Wv_ipa, L0_ffn_gate_w, L0_ffn_w1, L0_ffn_w2):
    import jax
    import jax.numpy as jnp

    def _L0_xattn_ref(x, context, Wq, Wk, Wv, Wo, bo, q_down, q_up, q_alpha, k_down, k_up, k_alpha, v_down, v_up, v_alpha, o_down, o_up, o_alpha, Wk_ipa, Wv_ipa):
        import jax, jax.numpy as jnp
        import numpy as np
        HEADS = 16
        DIM_HEAD = 64
        RANK = 32
        LORA_W = 1.0
        IPA_SCALE = 1.0
        IPA_TOKENS = 4
        SCALE = DIM_HEAD ** (-0.5)

        def _split_heads(t):
            b, n, _ = t.shape
            return t.reshape(b, n, HEADS, DIM_HEAD).transpose(0, 2, 1, 3)

        def _merge_heads(t):
            b, h, n, d = t.shape
            return t.transpose(0, 2, 1, 3).reshape(b, n, h * d)

        def _attention(q_in, k_in, v_in):
            q = _split_heads(q_in)
            k = _split_heads(k_in)
            v = _split_heads(v_in)
            s = jnp.einsum('bhid,bhjd->bhij', q, k) * SCALE
            p = jax.nn.softmax(s, axis=-1)
            o = jnp.einsum('bhij,bhjd->bhid', p, v)
            return _merge_heads(o)

        def _lora(t, down, up, alpha):
            return t @ down @ up * (LORA_W * alpha[0] / RANK)
        q_in = x @ Wq + _lora(x, q_down, q_up, q_alpha)
        end = context.shape[1] - IPA_TOKENS
        org_ctx = context[:, :end, :]
        ipa_ctx = context[:, end:, :]
        k_in = org_ctx @ Wk + _lora(org_ctx, k_down, k_up, k_alpha)
        v_in = org_ctx @ Wv + _lora(org_ctx, v_down, v_up, v_alpha)
        out = _attention(q_in, k_in, v_in)
        ipa_k = ipa_ctx @ Wk_ipa
        ipa_v = ipa_ctx @ Wv_ipa
        out_ipa = _attention(q_in, ipa_k, ipa_v)
        out = out + IPA_SCALE * out_ipa
        return out @ Wo + bo + _lora(out, o_down, o_up, o_alpha)

    def _L0_ffn_ref(x, gate_w, w1, w2):
        import jax, jax.numpy as jnp
        import numpy as np
        D_MODEL, D_FF, N_EXPERTS, TOP_K = (256, 512, 8, 2)
        B, S = (2, 512)
        router_logits = jnp.einsum('bsd,de->bse', x, gate_w)
        top_logits, top_idx = jax.lax.top_k(router_logits, TOP_K)
        top_w = jax.nn.softmax(top_logits, axis=-1)
        combine = jnp.sum(jax.nn.one_hot(top_idx, N_EXPERTS, dtype=x.dtype) * top_w[..., None], axis=-2)
        h = jax.nn.silu(jnp.einsum('bsd,edf->ebsf', x, w1))
        y = jnp.einsum('ebsf,efd->ebsd', h, w2)
        out = jnp.einsum('ebsd,bse->bsd', y, combine)
        return out
    x = x + _L0_xattn_ref(_layernorm(x, axis=-1), ctx_768, L0_xattn_Wq, L0_xattn_Wk, L0_xattn_Wv, L0_xattn_Wo, L0_xattn_bo, L0_xattn_q_down, L0_xattn_q_up, L0_xattn_q_alpha, L0_xattn_k_down, L0_xattn_k_up, L0_xattn_k_alpha, L0_xattn_v_down, L0_xattn_v_up, L0_xattn_v_alpha, L0_xattn_o_down, L0_xattn_o_up, L0_xattn_o_alpha, L0_xattn_Wk_ipa, L0_xattn_Wv_ipa)
    x = x + _L0_ffn_ref(_layernorm(x, axis=-1), L0_ffn_gate_w, L0_ffn_w1, L0_ffn_w2)
    return x

_drawn_inputs = setup_inputs


def setup_inputs(seed=0):
    import zlib

    import numpy as np

    out = dict(_drawn_inputs(seed))
    spreads = {'L0_xattn_bo': (0.0, 0.1)}
    factors = {'L0_xattn_Wq': 7.95,
     'L0_xattn_Wk': 8.0,
     'L0_xattn_q_down': 8.0,
     'L0_xattn_q_up': 8.0,
     'L0_xattn_k_down': 8.0,
     'L0_xattn_k_up': 8.0,
     'L0_xattn_v_down': 5.34,
     'L0_xattn_v_up': 5.219,
     'L0_xattn_o_down': 3.134,
     'L0_xattn_o_up': 3.148,
     'L0_xattn_Wk_ipa': 8.0}
    for name, (base, spread) in spreads.items():
        noise = np.random.default_rng([zlib.crc32(name.encode()), seed]).standard_normal(out[name].shape)
        drawn = base * np.exp(spread * noise) if base else spread * noise
        out[name] = jnp.asarray(drawn.astype(out[name].dtype))
    for name, factor in factors.items():
        out[name] = (out[name] * factor).astype(out[name].dtype)
    return out
```

```python
from contextlib import ExitStack

import concourse.bass as bass
from concourse import mybir

F32 = mybir.dt.float32
F16 = mybir.dt.float16
U32 = mybir.dt.uint32
ALU = mybir.AluOpType
ACT = mybir.ActivationFunctionType
AX = mybir.AxisListType.X

P = 128
BATCH, SEQ, DM = 16, 256, 256
HEADS, DH = 16, 64
ID = HEADS * DH
CD, CTX, IPA = 192, 77, 4
ORG = CTX - IPA
RANK = 32
EXPERTS, DFF = 8, 512
PAIRS = HEADS // 2
KD = DM // P
CDR = CD - P
TILES = BATCH * SEQ // P
TPB = SEQ // P
KEYS = HEADS * CTX
WSCALE = 64.0
PSCALE = 64.0
LN_EPS = 1e-5
HPB = 4
FW = 1024
GT = 4
GTOK = GT * P
GROUPS = TILES // GT


def build(nc, x, ctx_t, wq, wk, wv, wo, bo, q_down_t, q_up, q_alpha, k_down_t, k_up, k_alpha,
          v_down_t, v_up, v_alpha, o_down_t, o_up, o_alpha, wk_ipa, wv_ipa, gate_w, ffn_w, out):
    stack = ExitStack()
    with stack:
        def sb(name, shape, dt):
            return stack.enter_context(nc.sbuf_tensor(name, shape, dt))

        def sem(name):
            return stack.enter_context(nc.semaphore(name))

        x_sb = sb("x_sb", [P, TILES, DM], F32)
        ffnw = sb("ffnw", [P, 2, 2 * EXPERTS, FW], F16)
        wq_s = sb("wq_s", [P, 2, KD, ID], F16)
        wk_s = sb("wk_s", [P, 2, KD, ID], F16)
        wv_s = sb("wv_s", [P, 2, KD, ID], F16)
        wo_s = sb("wo_s", [P, 2, PAIRS, DM], F16)
        ctx_s = sb("ctx_s", [P, 2, KD, BATCH * CTX], F16)
        kipa_s = sb("kipa_s", [P, 2, PAIRS, BATCH, IPA], F16)
        kbd = sb("kbd", [P, 2, PAIRS, 2 * CTX], F16)
        v_s = sb("v_s", [P, 2, ID], F16)
        q_s = sb("q_s", [P, 2, PAIRS, SEQ], F16)
        xn = sb("xn", [P, TPB, DM], F32)
        xt_s = sb("xt_s", [P, 2, KD, SEQ], F16)
        prob = sb("prob", [P, TPB, KEYS], F32)
        pt_s = sb("pt_s", [P, 2, HEADS, SEQ], F16)
        ot_s = sb("ot_s", [P, 2, PAIRS, SEQ], F16)
        wstage = sb("wstage", [P, FW], F32)
        bo_sb = sb("bo_sb", [P, DM], F32)
        gate_f = sb("gate_f", [P, KD, EXPERTS], F32)
        gate_s = sb("gate_s", [P, 2, KD, EXPERTS], F16)
        ident = sb("ident", [P, P], F32)
        iota8 = sb("iota8", [P, EXPERTS], F32)
        alphas = sb("alphas", [RANK, 4], F32)
        stats = sb("stats", [P, TILES, 6], F32)
        ln_tmp = sb("ln_tmp", [P, 6, TILES], F32)
        ln_mean = sb("ln_mean", [P, TILES], F32)
        ln_std = sb("ln_std", [P, TILES], F32)
        ln_rstd = sb("ln_rstd", [P, TILES], F32)
        mx = sb("mx", [P, TPB, 2, HEADS], F32)
        sm = sb("sm", [P, TPB, 2, HEADS], F32)
        rc = sb("rc", [P, TPB, 2, HEADS], F32)

        pstage = pt_s[:, :, :, :].rearrange("p a h n -> p (a h n)").bitcast(F32).rearrange(
            "p (s n) -> p s n", s=2)
        cstage = ot_s[:, :, :, :].rearrange("p a h n -> p (a h n)").bitcast(F32)
        early = ffnw[:, :, :, :].rearrange("p a e n -> p (a e n)")
        kipaw = early[:, 0:4096].rearrange("p (a k n) -> p a k n", a=2, k=KD)
        vipaw = early[:, 4096:8192].rearrange("p (a k n) -> p a k n", a=2, k=KD)
        vipa_s = early[0:BATCH * IPA, 8192:8192 + 2 * ID].rearrange("p (a n) -> p a n", a=2)
        lora = early[0:RANK, 12288:12288 + 2 * 9216].bitcast(F32)
        ups = {"q": lora[:, 0:1024], "k": lora[:, 1024:2048], "v": lora[:, 2048:3072], "o": lora[:, 3072:3328]}
        downs = {"q": lora[:, 3328:3584], "k": lora[:, 3584:3776], "v": lora[:, 3776:3968],
                 "o": lora[:, 3968:4992]}

        lg = sb("lg", [P, GT, EXPERTS], F32)
        top = sb("top", [P, GT, EXPERTS], F32)
        top_i = sb("top_i", [P, GT, EXPERTS], U32)
        top_f = sb("top_f", [P, GT, EXPERTS], F32)
        oh_a = sb("oh_a", [P, GT, EXPERTS], F32)
        oh_b = sb("oh_b", [P, GT, EXPERTS], F32)
        comb = sb("comb", [P, GT, EXPERTS], F32)
        gap = sb("gap", [P, GT], F32)
        gap_exp = sb("gap_exp", [P, GT], F32)
        hold = sb("hold", [P, 1], F32)
        w_sum = sb("w_sum", [P, GT], F32)
        w_a = sb("w_a", [P, GT], F32)
        w_b = sb("w_b", [P, GT], F32)

        ps_s = stack.enter_context(nc.psum_tensor("ps_s", [P, 3, 512], F32))
        ps_a = stack.enter_context(nc.psum_tensor("ps_a", [P, 3, 512], F32))
        ps_b = stack.enter_context(nc.psum_tensor("ps_b", [P, 2, 512], F32))

        vipa_dram = nc.dram_tensor("vipa_dram", (BATCH, IPA, 2, ID), F16, kind="Internal").ap()

        S = {}
        x_in = [sem(f"x_in{c}") for c in range(4)]
        lora_in = sem("lora_in")
        misc_in = sem("misc_in")
        ctx_in = sem("ctx_in")
        pst_in = [sem(f"pst_in{s}") for s in range(2)]
        consts = sem("consts")
        zeroed = sem("zeroed")
        rows_zeroed = sem("rows_zeroed")
        pt_zeroed = sem("pt_zeroed")
        downs_ok = sem("downs_ok")
        lora_mm = sem("lora_mm")
        lora_add = sem("lora_add")
        w_hi = sem("w_hi")
        w_split = sem("w_split")
        c_hi = sem("c_hi")
        c_split = sem("c_split")
        g_hi = sem("g_hi")
        g_split = sem("g_split")
        ipa_mm = sem("ipa_mm")
        ipa_hi = sem("ipa_hi")
        ipa_split = sem("ipa_split")
        vipa_out = sem("vipa_out")
        ln_link = sem("ln_link")
        ln_var = sem("ln_var")
        ln_sqrt = sem("ln_sqrt")
        ln_done = sem("ln_done")
        xn_done = sem("xn_done")
        xt_mm = sem("xt_mm")
        xt_hi = sem("xt_hi")
        xt_split = sem("xt_split")
        q_mm = sem("q_mm")
        q_hi = sem("q_hi")
        q_split = sem("q_split")
        k_mm = sem("k_mm")
        k_hi = sem("k_hi")
        k_split = sem("k_split")
        kipa_put = sem("kipa_put")
        v_mm = sem("v_mm")
        v_hi = sem("v_hi")
        v_split = sem("v_split")
        vipa_in = sem("vipa_in")
        s_mm = sem("s_mm")
        s_copied = sem("s_copied")
        mx_done = sem("mx_done")
        shifted = sem("shifted")
        exp_done = sem("exp_done")
        sum_done = sem("sum_done")
        rc_done = sem("rc_done")
        p_ready = sem("p_ready")
        t_mm = sem("t_mm")
        pt_hi = sem("pt_hi")
        pt_split = sem("pt_split")
        pv_mm = sem("pv_mm")
        ot_hi = sem("ot_hi")
        ot_split = sem("ot_split")
        wo_mm = sem("wo_mm")
        bo_added = sem("bo_added")
        x1_done = sem("x1_done")
        st_done = sem("st_done")
        fw_in = sem("fw_in")
        fw_hi = sem("fw_hi")
        fw_split = sem("fw_split")

        for n in ("xg_done", "gx_mm", "gx_hi", "gx_split", "lg_mm", "lg_copied", "route_step", "gap_done", "gap_expd",
                  "h_mm", "silu_done", "h_hi", "h_split", "y_mm", "y_done", "out_done"):
            S[n] = sem(n)
        (xg_done, gx_mm, gx_hi, gx_split, lg_mm, lg_copied, route_step, gap_done, gap_expd, h_mm, silu_done, h_hi,
         h_split, y_mm, y_done, out_done) = S.values()

        jobs = ["q", "k", "v", "ki", "vi", "o"]
        job_src = {"q": wq, "k": wk, "v": wv, "ki": wk_ipa, "vi": wv_ipa, "o": wo}
        job_dst = {"q": wq_s, "k": wk_s, "v": wv_s, "ki": kipaw, "vi": vipaw, "o": wo_s}
        lora_jobs = ["q", "k", "v", "o"]
        x_view = x.rearrange("b (t p) d -> p (b t) d", p=P)
        out_view = out.rearrange("b (t p) d -> p (b t) d", p=P)

        def job_parts(j):
            if j in ("q", "o"):
                return [(P, 0, 2048)]
            return [(P, 0, 1024), (CDR, 1024, 2048)]

        def dst_flat(j, part):
            return job_dst[j][:, part].rearrange("p k n -> p (k n)")

        prob_f = prob[:].rearrange("p t n -> p (t n)")
        xg = prob_f[:, 0:GT * DM].rearrange("p (t d) -> p t d", t=GT)
        h32 = prob_f[:, GT * DM:GT * DM + 2 * GTOK].rearrange("p (s n) -> p s n", s=2)
        x2t = q_s[:].rearrange("p a m n -> p (a m n)")[:, 0:2 * KD * GTOK].rearrange("p (a k n) -> p a k n", a=2, k=KD)
        hs = pt_s[:].rearrange("p a h n -> p (a h n)").rearrange("p (s a f n) -> p s a f n", s=2, a=2, f=4)
        FT = DFF // P

        def w1(part, e, kk, m):
            return ffnw[:, part, 2 * e, kk * DFF + m * P:kk * DFF + m * P + P]

        def w2(part, e, f):
            return ffnw[:, part, 2 * e + 1, f * DM:f * DM + DM]

        def hbank(m):
            return ps_a[:, m, :] if m < 3 else ps_s[:, 2, :]

        def ffn_sp(sp):
            def group(g):
                sp.wait_ge(y_done, 2 * EXPERTS * g + 2 * EXPERTS)
                sp.dma_start(out_view[:, bass.ds(g * GT, GT), :], x_sb[:, bass.ds(g * GT, GT), :]).then_inc(out_done, 16)

            group(0)
            with sp.Fori(1, GROUPS) as g:
                group(g)
            sp.wait_ge(out_done, 16 * GROUPS)

        def ffn_pe(pe, product):
            def hidden(g, e):
                for m in range(FT):
                    if e == 0:
                        pe.wait_ge(silu_done, 32 * g)
                    else:
                        pe.wait_ge(silu_done, 32 * g + 4 * (e - 1) + m + 1)
                    product(hbank(m), lambda a, n: w1(a, e, n, m), lambda a, n: x2t[:, a, n, :], KD).then_inc(h_mm, 1)

            def down(g, e):
                pe.wait_ge(h_split, 32 * g + 4 * e + 4)
                for yk in (0, 1):
                    pe.wait_ge(y_done, 16 * g + (2 * (e - 1) + yk + 1 if e else 0))
                    for c in (0, 1):
                        t = 2 * yk + c
                        last = product(ps_b[:, yk, c * DM:c * DM + DM],
                                       lambda a, n: hs[:, e % 2, a, n, t * P:t * P + P],
                                       lambda a, n: w2(a, e, n), FT)
                    last.then_inc(y_mm, 1)

            pe.wait_ge(fw_split, 2 * EXPERTS)
            pe.wait_ge(g_split, 1)
            def group(g):
                pe.wait_ge(xg_done, g + 1)
                pe.wait_ge(lg_copied, g)
                for kk in range(KD):
                    for t in range(GT):
                        last = pe.transpose(ps_s[:, kk, t * P:t * P + P], xg[:, t, kk * P:kk * P + P], ident[:])
                    last.then_inc(gx_mm, 1)
                pe.wait_ge(gx_split, 2 * g + 2)
                for t in range(GT):
                    last = product(ps_s[:, 0, t * EXPERTS:t * EXPERTS + EXPERTS],
                                   lambda a, n: x2t[:, a, n, t * P:t * P + P], lambda a, n: gate_s[:, a, n, :], KD)
                last.then_inc(lg_mm, 1)
                hidden(g, 0)
                for e in range(EXPERTS):
                    if e + 1 < EXPERTS:
                        hidden(g, e + 1)
                    down(g, e)

            group(0)
            with pe.Fori(1, GROUPS) as g:
                group(g)

        def ffn_act(act):
            act.wait_ge(ln_var, 2)
            act.activation(ln_std[:], ln_tmp[:, 5, :], ACT.Sqrt).then_inc(ln_sqrt, 1)
            def group(g):
                for kk in range(KD):
                    act.wait_ge(gx_mm, 2 * g + kk + 1)
                    act.activation(x2t[:, 0, kk, :], ps_s[:, kk, :], ACT.Copy).then_inc(gx_hi, 1)
                act.wait_ge(gap_done, g + 1)
                act.activation(gap_exp[:], gap[:], ACT.Exp, scale=1 / WSCALE).then_inc(gap_expd, 1)
                for e in range(EXPERTS):
                    for m in range(FT):
                        u = 32 * g + 4 * e + m
                        act.wait_ge(h_mm, u + 1)
                        act.wait_ge(h_split, 32 * g if e == 0 and m < 2 else u - 1)
                        act.activation(h32[:, m % 2, :], hbank(m), ACT.Silu, scale=1 / WSCALE).then_inc(silu_done, 1)
                        act.wait_ge(silu_done, u + 1)
                        act.wait_ge(y_mm, 16 * g + (2 * (e - 1) if e else 0))
                        act.activation(hs[:, e % 2, 0, m, :], h32[:, m % 2, :], ACT.Copy).then_inc(h_hi, 1)

            group(0)
            with act.Fori(1, GROUPS) as g:
                group(g)

        def ffn_dve(dve):
            count = [0]
            NLINK = 11

            def group(g):
                count[0] = 0

                def step(ins):
                    count[0] += 1
                    ins.then_inc(route_step, 1)
                    dve.wait_ge(route_step, g * NLINK + count[0])

                for t in range(GT):
                    tile = g * GT + t
                    last = dve.tensor_scalar(
                        xg[:, t, :], x_sb[:, bass.ds(tile, 1), :].rearrange("p t d -> p (t d)"),
                        ln_mean[:, bass.ds(tile, 1)], ln_rstd[:, bass.ds(tile, 1)], ALU.subtract, ALU.mult)
                last.then_inc(xg_done, 1)
                for kk in range(KD):
                    dve.wait_ge(gx_hi, 2 * g + kk + 1)
                    dve.tensor_tensor(x2t[:, 1, kk, :], ps_s[:, kk, :], x2t[:, 0, kk, :], ALU.subtract
                                      ).then_inc(gx_split, 1)
                dve.wait_ge(lg_mm, g + 1)
                dve.tensor_copy(lg[:].rearrange("p t e -> p (t e)"), ps_s[:, 0, 0:GT * EXPERTS]).then_inc(lg_copied, 1)
                dve.wait_ge(lg_copied, g + 1)
                dve.memset(hold[:], 0.0)
                for t in range(GT):
                    last = dve.max(top[:, t, :], lg[:, t, :])
                step(last)
                dve.memset(hold[:], 0.0)
                for t in range(GT):
                    last = dve.max_index(top_i[:, t, :], top[:, t, :], lg[:, t, :])
                step(last)
                step(dve.tensor_copy(top_f[:], top_i[:]))
                dve.tensor_tensor(gap[:], top[:, :, 1], top[:, :, 0], ALU.subtract).then_inc(gap_done, 1)
                dve.wait_ge(gap_expd, g + 1)
                step(dve.tensor_scalar(w_sum[:], gap_exp[:], 1.0, WSCALE, ALU.add, ALU.mult))
                step(dve.reciprocal(w_a[:], w_sum[:]))
                step(dve.tensor_tensor(w_b[:], w_a[:], gap_exp[:], ALU.mult))
                io = iota8[:].unsqueeze(1).to_broadcast([P, GT, EXPERTS])
                step(dve.tensor_tensor(oh_a[:], io, top_f[:, :, 0:1].to_broadcast([P, GT, EXPERTS]), ALU.is_equal))
                step(dve.tensor_tensor(oh_b[:], io, top_f[:, :, 1:2].to_broadcast([P, GT, EXPERTS]), ALU.is_equal))
                step(dve.tensor_tensor(oh_a[:], oh_a[:], w_a[:].unsqueeze(2).to_broadcast([P, GT, EXPERTS]), ALU.mult))
                step(dve.tensor_tensor(oh_b[:], oh_b[:], w_b[:].unsqueeze(2).to_broadcast([P, GT, EXPERTS]), ALU.mult))
                step(dve.tensor_tensor(comb[:], oh_a[:], oh_b[:], ALU.add))

                def low(e):
                    for m in range(FT):
                        dve.wait_ge(h_hi, 32 * g + 4 * e + m + 1)
                        dve.tensor_tensor(hs[:, e % 2, 1, m, :], h32[:, m % 2, :], hs[:, e % 2, 0, m, :], ALU.subtract
                                          ).then_inc(h_split, 1)

                low(0)
                for e in range(EXPERTS):
                    if e + 1 < EXPERTS:
                        low(e + 1)
                    for yk in (0, 1):
                        dve.wait_ge(y_mm, 16 * g + 2 * e + yk + 1)
                        if e:
                            dve.wait_ge(y_done, 16 * g + 2 * e + yk - 1)
                        for c in (0, 1):
                            t = 2 * yk + c
                            xt_ = x_sb[:, bass.ds(g * GT + t, 1), :].rearrange("p t d -> p (t d)")
                            last = dve.scalar_tensor_tensor(out=xt_, in0=ps_b[:, yk, c * DM:c * DM + DM],
                                                            scalar=comb[:, t, e:e + 1], in1=xt_, op0=ALU.mult,
                                                            op1=ALU.add)
                        last.then_inc(y_done, 1)

            group(0)
            with dve.Fori(1, GROUPS) as g:
                group(g)
            assert count[0] == NLINK

        block = stack.enter_context(nc.Block())

        @block.sync
        def _(sp):
            for j, (dn, up) in {"q": (q_down_t, q_up), "k": (k_down_t, k_up), "v": (v_down_t, v_up),
                                "o": (o_down_t, o_up)}.items():
                sp.dma_start(downs[j], dn).then_inc(lora_in, 16)
                sp.dma_start(ups[j], up).then_inc(lora_in, 16)
            for n, a in enumerate((q_alpha, k_alpha, v_alpha, o_alpha)):
                sp.dma_start(alphas[:, n:n + 1], a.rearrange("(a b) -> a b", a=1).to_broadcast([RANK, 1])
                             ).then_inc(lora_in, 16)

            def load_job(n):
                j, slot = jobs[n], n % 2
                if n >= 2:
                    sp.wait_ge(w_split, n - 1)
                if j in ("q", "o"):
                    nk = KD if j == "q" else PAIRS
                    dst = pstage[:, slot, :].rearrange("p (k n) -> p k n", k=nk)
                    src = job_src[j].rearrange("(k p) n -> p k n", p=P)
                    for c in (0, 1):
                        ks = slice(c * nk // 2, (c + 1) * nk // 2)
                        sp.dma_start(dst[:, ks], src[:, ks]).then_inc(pst_in[slot], 16)
                else:
                    sp.dma_start(pstage[:, slot, 0:ID], job_src[j][0:P, :]).then_inc(pst_in[slot], 16)
                    sp.dma_start(pstage[0:CDR, slot, ID:2 * ID], job_src[j][P:CD, :]).then_inc(pst_in[slot], 16)

            load_job(0)
            load_job(1)
            for c in range(4):
                sp.dma_start(x_sb[:, c * 8:c * 8 + 8, :], x_view[:, c * 8:c * 8 + 8, :]).then_inc(x_in[c], 16)
            sp.dma_start(cstage[:, 0:BATCH * CTX], ctx_t[0:P, :]).then_inc(ctx_in, 16)
            sp.dma_start(bo_sb[:], bo.rearrange("(a n) -> a n", a=1).to_broadcast([P, DM])).then_inc(misc_in, 16)
            sp.dma_start(gate_f[:], gate_w.rearrange("(k p) e -> p k e", p=P)).then_inc(misc_in, 16)
            sp.wait_ge(c_split, 1)
            sp.dma_start(cstage[0:CDR, 0:BATCH * CTX], ctx_t[P:CD, :]).then_inc(ctx_in, 16)
            for n in range(2, 6):
                load_job(n)
            sp.wait_ge(ipa_split, 4)
            sp.dma_start(vipa_dram.rearrange("b i a n -> (b i) a n"), vipa_s).then_inc(vipa_out, 16)
            sp.wait_ge(vipa_out, 16)
            sp.wait_ge(zeroed, 2)
            sp.dma_start(v_s[ORG:CTX, :, :], vipa_dram[0]).then_inc(vipa_in, 16)

            def body(b, last):
                if not (isinstance(b, int) and b == 0):
                    sp.wait_ge(fw_split, b)
                else:
                    sp.wait_ge(ipa_split, 4)
                sp.dma_start(wstage[:], ffn_w[b]).then_inc(fw_in, 16)
                if not last:
                    sp.wait_ge(pv_mm, 4 * b + 4)
                    sp.dma_start(v_s[ORG:CTX, :, :], vipa_dram[bass.ds(b + 1, 1)].rearrange("a i h n -> (a i) h n")
                                 ).then_inc(vipa_in, 16)

            body(0, False)
            with sp.Fori(1, BATCH - 1) as b:
                body(b, False)
            body(BATCH - 1, True)
            ffn_sp(sp)

        @block.gpsimd
        def _(pool):
            pool.memset(ident[:], 0.0).then_inc(consts, 1)
            pool.iota(iota8[:], [[1, EXPERTS]], base=0, channel_multiplier=0,
                      allow_small_or_imprecise_dtypes=True).then_inc(consts, 1)
            pool.wait_ge(consts, 2)
            pool.affine_select(out=ident[:], in_=ident[:], compare_op=ALU.not_equal, fill=1.0, base=0,
                               pattern=[[-1, P]], channel_multiplier=1).then_inc(consts, 1)
            pool.memset(kbd[:], 0.0).then_inc(zeroed, 1)
            pool.memset(v_s[:], 0.0).then_inc(zeroed, 1)

            def keys(t):
                v = prob[:, t, :].rearrange("p (h j) -> p h j", j=CTX)
                return [(v[:, :, 0:ORG], 0, ORG), (v[:, :, ORG:CTX], 1, IPA)]

            def shift(b, t):
                pool.wait_ge(mx_done, 2 * b + t + 1)
                for v, w, n in keys(t):
                    last = pool.tensor_tensor(v, v, mx[:, t, w, :].unsqueeze(2).to_broadcast([P, HEADS, n]),
                                              ALU.subtract)
                last.then_inc(shifted, 1)

            def normalise(b, t):
                pool.wait_ge(rc_done, 2 * b + t + 1)
                for v, w, n in keys(t):
                    last = pool.tensor_tensor(v, v, rc[:, t, w, :].unsqueeze(2).to_broadcast([P, HEADS, n]),
                                              ALU.mult)
                last.then_inc(p_ready, 1)

            def body(b, last):
                shift(b, 0)
                pool.wait_ge(xn_done, b + 1)
                xb = x_sb[:, bass.ds(b * TPB, TPB), :]
                pool.tensor_tensor(xb, xb, bo_sb[:].unsqueeze(1).to_broadcast([P, TPB, DM]), ALU.add
                                   ).then_inc(bo_added, 1)
                normalise(b, 0)
                shift(b, 1)
                normalise(b, 1)

            pool.wait_ge(misc_in, 32)
            body(0, False)
            with pool.Fori(1, BATCH - 1) as b:
                body(b, False)
            body(BATCH - 1, True)

        def ipa_k_hi(act):
            act.wait_ge(ipa_mm, 1)
            act.activation(kipa_s[:, 0].rearrange("p m b i -> p (m b i)"), ps_s[:, 0, :], ACT.Copy,
                           scale=1 / WSCALE).then_inc(ipa_hi, 1)

        def ipa_v_hi(act):
            act.wait_ge(ipa_mm, 2)
            act.activation(vipa_s[:, 0, :], ps_s[0:BATCH * IPA, 1:3, :].rearrange("p c n -> p (c n)"), ACT.Copy,
                           scale=1 / WSCALE).then_inc(ipa_hi, 1)

        @block.scalar
        def _(act):
            def split_job(n):
                j, slot = jobs[n], n % 2
                if j in lora_jobs:
                    act.wait_ge(lora_add, 4 * lora_jobs.index(j) + 4)
                else:
                    act.wait_ge(pst_in[slot], 32 * (n // 2 + 1))
                for rows, lo, hi in job_parts(j):
                    last = act.activation(dst_flat(j, 0)[0:rows, lo:hi], pstage[0:rows, slot, lo:hi], ACT.Copy,
                                          scale=WSCALE)
                last.then_inc(w_hi, 1)

            split_job(0)
            split_job(1)
            act.wait_ge(ln_var, 1)
            act.activation(ln_std[:], ln_tmp[:, 5, :], ACT.Sqrt).then_inc(ln_sqrt, 1)
            for kk, rows in enumerate((P, CDR)):
                act.wait_ge(ctx_in, 16 * (kk + 1))
                act.activation(ctx_s[0:rows, 0, kk, :], cstage[0:rows, 0:BATCH * CTX], ACT.Copy).then_inc(c_hi, 1)
            act.wait_ge(misc_in, 32)
            act.activation(gate_s[:, 0], gate_f[:], ACT.Copy, scale=WSCALE).then_inc(g_hi, 1)
            for n in range(2, 6):
                split_job(n)
                if n == 3:
                    ipa_k_hi(act)
                if n == 4:
                    ipa_v_hi(act)

            def hi_of(dst, src, scale, ready, n, done):
                act.wait_ge(ready, n)
                act.activation(dst, src, ACT.Copy, scale=scale).then_inc(done, 1)

            def xt(b):
                hi_of(xt_s[:, 0].rearrange("p k n -> p (k n)"), ps_b[:, 1, :], 1.0, xt_mm, b + 1, xt_hi)

            def q(b, k):
                hi_of(q_s[:, 0, 2 * k:2 * k + 2, :].rearrange("p m n -> p (m n)"), ps_a[:, k % 3, :],
                      1 / WSCALE, q_mm, 4 * b + k + 1, q_hi)

            def k_(b, k):
                act.wait_ge(k_mm, 2 * b + k + 1)
                for half in (0, 1):
                    o = half * DH
                    last = act.activation(
                        kbd[o:o + DH, 0, 4 * k:4 * k + 4, half * CTX:half * CTX + ORG],
                        ps_b[o:o + DH, k, 0:4 * ORG].rearrange("p (m j) -> p m j", m=4), ACT.Copy,
                        scale=1 / WSCALE)
                last.then_inc(k_hi, 1)

            def put_kipa(b):
                for half in (0, 1):
                    o = half * DH
                    last = act.activation(
                        kbd[o:o + DH, :, :, half * CTX + ORG:half * CTX + CTX].rearrange("p a m j -> p (a m) j"),
                        kipa_s[o:o + DH, :, :, bass.ds(b, 1), :].rearrange("p a m b j -> p (a m) (b j)"), ACT.Copy)
                last.then_inc(kipa_put, 1)

            def v(b, k):
                hi_of(v_s[0:ORG, 0, k * 512:k * 512 + 512], ps_b[0:ORG, k, :], 1 / WSCALE, v_mm, 2 * b + k + 1, v_hi)

            def copy_scores(b, t):
                act.wait_ge(s_mm, 2 * b + t + 1)
                for c in range(3):
                    w = min(3, PAIRS - 3 * c) * 2 * CTX
                    last = act.activation(prob[:, t, c * 6 * CTX:c * 6 * CTX + w], ps_s[:, c, 0:w], ACT.Copy)
                last.then_inc(s_copied, 1)

            def exp(b, t):
                act.wait_ge(shifted, 2 * b + t + 1)
                act.activation(prob[:, t, :], prob[:, t, :], ACT.Exp, scale=DH ** -0.5).then_inc(exp_done, 1)

            def pt(b, k):
                t, h = k // 4, HPB * (k % 4)
                hi_of(pt_s[0:CTX, 0, h:h + HPB, t * P:t * P + P],
                      ps_a[0:CTX, (k + 1) % 3, :].rearrange("p (h n) -> p h n", h=HPB), PSCALE, t_mm, 8 * b + k + 1,
                      pt_hi)

            def ot(b, k):
                hi_of(ot_s[:, 0, 2 * k:2 * k + 2, :].rearrange("p m n -> p (m n)"), ps_b[:, k % 2, :],
                      1 / (PSCALE), pv_mm, 4 * b + k + 1, ot_hi)

            def body(b, last):
                copy_scores(b, 0)
                exp(b, 0)
                copy_scores(b, 1)
                if not last:
                    xt(b + 1)
                    q(b + 1, 0)
                    q(b + 1, 1)
                exp(b, 1)
                if not last:
                    q(b + 1, 2)
                    q(b + 1, 3)
                    k_(b + 1, 0)
                    k_(b + 1, 1)
                    put_kipa(b + 1)
                act.wait_ge(fw_in, 16 * b + 16)
                act.activation(ffnw[:, 0, bass.ds(b, 1), :].rearrange("p e n -> p (e n)"), wstage[:], ACT.Copy,
                               scale=WSCALE).then_inc(fw_hi, 1)
                for k in range(8):
                    pt(b, k)
                for k in range(4):
                    ot(b, k)
                if not last:
                    v(b + 1, 0)
                    v(b + 1, 1)

            xt(0)
            act.wait_ge(zeroed, 2)
            act.wait_ge(ipa_split, 4)
            k_(0, 0)
            k_(0, 1)
            put_kipa(0)
            for k in range(4):
                q(0, k)
            v(0, 0)
            v(0, 1)
            body(0, False)
            with act.Fori(1, BATCH - 1) as b:
                body(b, False)
            body(BATCH - 1, True)
            ffn_act(act)

        @block.vector
        def _(dve):
            links = [0]

            def link(ins):
                links[0] += 1
                ins.then_inc(ln_link, 1)
                dve.wait_ge(ln_link, links[0])

            def layer_stats(n):
                me, mo, cve, cvo = (stats[:, :, c] for c in (1, 4, 2, 5))
                tmp = [ln_tmp[:, c, :] for c in range(6)]
                link(dve.tensor_tensor(tmp[0], me, mo, ALU.add))
                link(dve.tensor_tensor(tmp[1], me, mo, ALU.subtract))
                link(dve.tensor_tensor(tmp[2], cve, cvo, ALU.add))
                link(dve.tensor_scalar(ln_mean[:], tmp[0], 0.5, None, ALU.mult))
                link(dve.tensor_tensor(tmp[3], tmp[1], tmp[1], ALU.mult))
                link(dve.tensor_scalar(tmp[4], tmp[2], 1.0 / DM, LN_EPS, ALU.mult, ALU.add))
                dve.scalar_tensor_tensor(out=tmp[5], in0=tmp[3], scalar=0.25, in1=tmp[4], op0=ALU.mult,
                                         op1=ALU.add).then_inc(ln_var, 1)
                dve.wait_ge(ln_sqrt, n)
                link(dve.reciprocal(ln_rstd[:], ln_std[:]))

            def lo_of(dst, src, scale, hi, ready, n, done):
                dve.wait_ge(ready, n)
                dve.scalar_tensor_tensor(out=dst, in0=src, scalar=scale, in1=hi, op0=ALU.mult, op1=ALU.subtract
                                         ).then_inc(done, 1)

            def job_adds(n):
                j, slot = jobs[n], n % 2
                dve.wait_ge(pst_in[slot], 32 * (n // 2 + 1))
                li = lora_jobs.index(j)
                for u in range(4):
                    rows = P if u < 2 or j in ("q", "o") else CDR
                    dve.wait_ge(lora_mm, 4 * li + u + 1)
                    piece = pstage[0:rows, slot, u * 512:u * 512 + 512]
                    dve.tensor_tensor(piece, ps_s[0:rows, (4 * li + u) % 3, :], piece, ALU.add
                                      ).then_inc(lora_add, 1)

            def job_lo(n):
                j, slot = jobs[n], n % 2
                dve.wait_ge(w_hi, n + 1)
                for rows, lo, hi in job_parts(j):
                    last = dve.scalar_tensor_tensor(
                        out=dst_flat(j, 1)[0:rows, lo:hi], in0=pstage[0:rows, slot, lo:hi], scalar=WSCALE,
                        in1=dst_flat(j, 0)[0:rows, lo:hi], op0=ALU.mult, op1=ALU.subtract)
                last.then_inc(w_split, 1)

            for w in (wk_s, wv_s, kipaw, vipaw, ctx_s):
                for part in (0, 1):
                    last = dve.memset(w[CDR:P, part, 1, :].bitcast(F32), 0.0)
            last.then_inc(rows_zeroed, 1)
            dve.wait_ge(lora_in, 16 * 12)
            for n, j in enumerate(lora_jobs):
                link(dve.tensor_scalar(downs[j], downs[j], alphas[:, n:n + 1], 1.0 / RANK, ALU.mult, ALU.mult))
            dve.wait_ge(ln_link, 4)
            dve.memset(ln_tmp[0:1, 0, 0:1], 0.0).then_inc(downs_ok, 1)
            job_adds(0)
            job_lo(0)
            job_adds(1)
            job_lo(1)
            for c in range(4):
                dve.wait_ge(x_in[c], 16)
                with dve.Fori(8 * c, 8 * c + 8) as t:
                    dve.bn_stats(stats[:, bass.ds(t, 1), :].rearrange("p t s -> p (t s)"),
                                 x_sb[:, bass.ds(t, 1), :].rearrange("p t d -> p (t d)")).then_inc(st_done, 1)
            dve.wait_ge(st_done, TILES)
            layer_stats(1)

            def normalise_x(b):
                for t in range(TPB):
                    tile = b * TPB + t
                    last = dve.tensor_scalar(
                        xn[:, t, :], x_sb[:, bass.ds(tile, 1), :].rearrange("p t d -> p (t d)"),
                        ln_mean[:, bass.ds(tile, 1)], ln_rstd[:, bass.ds(tile, 1)], ALU.subtract, ALU.mult)
                last.then_inc(xn_done, 1)

            normalise_x(0)
            for kk, rows in enumerate((P, CDR)):
                lo_of(ctx_s[0:rows, 1, kk, :], cstage[0:rows, 0:BATCH * CTX], 1.0, ctx_s[0:rows, 0, kk, :],
                      c_hi, kk + 1, c_split)
            lo_of(gate_s[:, 1], gate_f[:], WSCALE, gate_s[:, 0], g_hi, 1, g_split)
            for n in range(2, 6):
                if jobs[n] in lora_jobs:
                    job_adds(n)
                job_lo(n)
                if n == 3:
                    dve.wait_ge(ipa_hi, 1)
                    dve.scalar_tensor_tensor(
                        out=kipa_s[:, 1].rearrange("p m b i -> p (m b i)"), in0=ps_s[:, 0, :], scalar=1 / WSCALE,
                        in1=kipa_s[:, 0].rearrange("p m b i -> p (m b i)"), op0=ALU.mult, op1=ALU.subtract
                    ).then_inc(ipa_split, 2)
                if n == 4:
                    dve.wait_ge(ipa_hi, 2)
                    dve.scalar_tensor_tensor(
                        out=vipa_s[:, 1, :], in0=ps_s[0:BATCH * IPA, 1:3, :].rearrange("p c n -> p (c n)"),
                        scalar=1 / WSCALE, in1=vipa_s[:, 0, :], op0=ALU.mult, op1=ALU.subtract
                    ).then_inc(ipa_split, 2)

            def xt(b):
                lo_of(xt_s[:, 1].rearrange("p k n -> p (k n)"), ps_b[:, 1, :], 1.0,
                      xt_s[:, 0].rearrange("p k n -> p (k n)"), xt_hi, b + 1, xt_split)

            def q(b, k):
                lo_of(q_s[:, 1, 2 * k:2 * k + 2, :].rearrange("p m n -> p (m n)"), ps_a[:, k % 3, :], 1 / WSCALE,
                      q_s[:, 0, 2 * k:2 * k + 2, :].rearrange("p m n -> p (m n)"), q_hi, 4 * b + k + 1, q_split)

            def k_(b, k):
                dve.wait_ge(k_hi, 2 * b + k + 1)
                for half in (0, 1):
                    o = half * DH
                    last = dve.scalar_tensor_tensor(
                        out=kbd[o:o + DH, 1, 4 * k:4 * k + 4, half * CTX:half * CTX + ORG],
                        in0=ps_b[o:o + DH, k, 0:4 * ORG].rearrange("p (m j) -> p m j", m=4), scalar=1 / WSCALE,
                        in1=kbd[o:o + DH, 0, 4 * k:4 * k + 4, half * CTX:half * CTX + ORG], op0=ALU.mult,
                        op1=ALU.subtract)
                last.then_inc(k_split, 1)

            def v(b, k):
                lo_of(v_s[0:ORG, 1, k * 512:k * 512 + 512], ps_b[0:ORG, k, :], 1 / WSCALE,
                      v_s[0:ORG, 0, k * 512:k * 512 + 512], v_hi, 2 * b + k + 1, v_split)

            def keys(t):
                vw = prob[:, t, :].rearrange("p (h j) -> p h j", j=CTX)
                return [(vw[:, :, 0:ORG], 0), (vw[:, :, ORG:CTX], 1)]

            def maxima(b, t):
                dve.wait_ge(s_copied, 2 * b + t + 1)
                for vw, w in keys(t):
                    last = dve.tensor_reduce(mx[:, t, w, :], vw, AX, ALU.max)
                last.then_inc(mx_done, 1)

            def sums(b, t):
                dve.wait_ge(exp_done, 2 * b + t + 1)
                for vw, w in keys(t):
                    last = dve.tensor_reduce(sm[:, t, w, :], vw, AX, ALU.add)
                last.then_inc(sum_done, 1)
                dve.wait_ge(sum_done, 2 * b + t + 1)
                dve.reciprocal(rc[:, t], sm[:, t]).then_inc(rc_done, 1)

            def pt(b, k):
                t, h = k // 4, HPB * (k % 4)
                lo_of(pt_s[0:CTX, 1, h:h + HPB, t * P:t * P + P],
                      ps_a[0:CTX, (k + 1) % 3, :].rearrange("p (h n) -> p h n", h=HPB), PSCALE,
                      pt_s[0:CTX, 0, h:h + HPB, t * P:t * P + P], pt_hi, 8 * b + k + 1, pt_split)

            def ot(b, k):
                lo_of(ot_s[:, 1, 2 * k:2 * k + 2, :].rearrange("p m n -> p (m n)"), ps_b[:, k % 2, :],
                      1 / (PSCALE), ot_s[:, 0, 2 * k:2 * k + 2, :].rearrange("p m n -> p (m n)"), ot_hi,
                      4 * b + k + 1, ot_split)

            def residual(b):
                dve.wait_ge(wo_mm, b + 1)
                dve.wait_ge(bo_added, b + 1)
                xb = x_sb[:, bass.ds(b * TPB, TPB), :].rearrange("p t d -> p (t d)")
                dve.scalar_tensor_tensor(out=xb, in0=ps_b[:, 0, :], scalar=1 / WSCALE, in1=xb, op0=ALU.mult,
                                         op1=ALU.add).then_inc(x1_done, 1)
                dve.wait_ge(x1_done, b + 1)
                for t in range(TPB):
                    tile = b * TPB + t
                    last = dve.bn_stats(stats[:, bass.ds(tile, 1), :].rearrange("p t s -> p (t s)"),
                                        x_sb[:, bass.ds(tile, 1), :].rearrange("p t d -> p (t d)"))
                last.then_inc(st_done, 1)

            def body(b, first, last):
                if not last:
                    normalise_x(b + 1)
                maxima(b, 0)
                sums(b, 0)
                if not first:
                    residual(b - 1)
                maxima(b, 1)
                if not last:
                    xt(b + 1)
                    q(b + 1, 0)
                    q(b + 1, 1)
                sums(b, 1)
                if not last:
                    q(b + 1, 2)
                    q(b + 1, 3)
                    k_(b + 1, 0)
                    k_(b + 1, 1)
                dve.wait_ge(fw_hi, b + 1)
                fw = [ffnw[:, part, bass.ds(b, 1), :].rearrange("p e n -> p (e n)") for part in (0, 1)]
                dve.scalar_tensor_tensor(out=fw[1], in0=wstage[:], scalar=WSCALE, in1=fw[0], op0=ALU.mult,
                                         op1=ALU.subtract).then_inc(fw_split, 1)
                for k in range(8):
                    pt(b, k)
                for k in range(4):
                    ot(b, k)
                if not last:
                    v(b + 1, 0)
                    v(b + 1, 1)

            dve.wait_ge(w_split, 6)
            dve.memset(pt_s[DH:P].rearrange("p a h n -> p (a h n)").bitcast(F32), 0.0).then_inc(pt_zeroed, 1)
            xt(0)
            k_(0, 0)
            k_(0, 1)
            for k in range(4):
                q(0, k)
            v(0, 0)
            v(0, 1)
            body(0, True, False)
            with dve.Fori(1, BATCH - 1) as b:
                body(b, False, False)
            body(BATCH - 1, False, True)
            residual(BATCH - 1)
            dve.wait_ge(st_done, TILES + BATCH)
            layer_stats(2)
            ffn_dve(dve)

        THREE = ((0, 0), (0, 1), (1, 0))

        @block.tensor
        def _(pe):
            def product(o, lhs, rhs, terms):
                steps = [(n, a, c) for n in range(terms) for a, c in THREE]
                for i, (n, a, c) in enumerate(steps):
                    last = pe.matmul(o, lhs(a, n), rhs(c, n), start=(i == 0), stop=(i == len(steps) - 1))
                return last

            def lora_products(j):
                li = lora_jobs.index(j)
                for u in range(4):
                    if 4 * li + u >= 3:
                        pe.wait_ge(lora_add, 4 * li + u - 2)
                    bank = (4 * li + u) % 3
                    if j == "o":
                        for c in (0, 1):
                            p = 2 * u + c
                            last = pe.matmul(ps_s[:, bank, c * DM:c * DM + DM], downs[j][:, p * P:p * P + P], ups[j],
                                             start=True, stop=True)
                    else:
                        kk, n = u // 2, u % 2
                        rows = P if kk == 0 or j == "q" else CDR
                        last = pe.matmul(ps_s[0:rows, bank, :], downs[j][:, kk * P:kk * P + rows],
                                         ups[j][:, n * 512:n * 512 + 512], start=True, stop=True)
                    last.then_inc(lora_mm, 1)

            def transpose_x(b):
                pe.wait_ge(xn_done, b + 1)
                for kk in range(KD):
                    for t in range(TPB):
                        c = kk * SEQ + t * P
                        last = pe.transpose(ps_b[:, 1, c:c + P], xn[:, t, kk * P:kk * P + P], ident[:])
                last.then_inc(xt_mm, 1)

            def queries(b, k):
                for m in (2 * k, 2 * k + 1):
                    o = (m % 2) * SEQ
                    last = product(ps_a[:, k % 3, o:o + SEQ], lambda a, n: wq_s[:, a, n, m * P:m * P + P],
                                   lambda a, n: xt_s[:, a, n, :], KD)
                last.then_inc(q_mm, 1)

            def context(part, kk, b):
                return ctx_s[:, part, kk, bass.ds(b * ORG, ORG)]

            def new_keys(b, k):
                for m in range(4 * k, 4 * k + 4):
                    o = (m % 4) * ORG
                    last = product(ps_b[:, k, o:o + ORG], lambda a, n: wk_s[:, a, n, m * P:m * P + P],
                                   lambda a, n: context(a, n, b), KD)
                last.then_inc(k_mm, 1)

            def new_values(b, k):
                product(ps_b[0:ORG, k, :], lambda a, n: context(a, n, b),
                        lambda a, n: wv_s[:, a, n, k * 512:k * 512 + 512], KD).then_inc(v_mm, 1)

            def scores(b, t):
                pe.wait_ge(s_copied, 2 * b + t)
                if t == 0:
                    pe.wait_ge(q_split, 4 * b + 4)
                    pe.wait_ge(k_split, 2 * b + 2)
                    pe.wait_ge(kipa_put, b + 1)
                for p in range(PAIRS):
                    o = (p % 3) * 2 * CTX
                    last = product(ps_s[:, p // 3, o:o + 2 * CTX], lambda a, n: q_s[:, a, p, t * P:t * P + P],
                                   lambda a, n: kbd[:, a, p, :], 1)
                last.then_inc(s_mm, 1)

            def transpose_probs(b, k):
                t, h = k // 4, HPB * (k % 4)
                if k % 4 == 0:
                    pe.wait_ge(p_ready, 2 * b + t + 1)
                for c in range(HPB):
                    last = pe.transpose(ps_a[0:CTX, (k + 1) % 3, c * P:c * P + P],
                                        prob[:, t, (h + c) * CTX:(h + c + 1) * CTX], ident[:])
                last.then_inc(t_mm, 1)

            def attend(b, k):
                for p in (2 * k, 2 * k + 1):
                    o = (p % 2) * SEQ
                    for i, (a, c) in enumerate(THREE):
                        for half in (0, 1):
                            h = 2 * p + half
                            last = pe.matmul(ps_b[half * DH:half * DH + DH, k % 2, o:o + SEQ],
                                             v_s[:, a, h * DH:h * DH + DH], pt_s[:, c, h, :],
                                             start=(i == 0), stop=(i == 2))
                last.then_inc(pv_mm, 1)

            def project(b):
                pe.wait_ge(ot_split, 4 * b + 4)
                for t in range(TPB):
                    last = product(ps_b[:, 0, t * DM:t * DM + DM], lambda a, n: ot_s[:, a, n, t * P:t * P + P],
                                   lambda a, n: wo_s[:, a, n, :], PAIRS)
                last.then_inc(wo_mm, 1)

            pe.wait_ge(consts, 3)
            pe.wait_ge(downs_ok, 1)
            lora_products("q")
            lora_products("k")
            transpose_x(0)
            lora_products("v")
            pe.wait_ge(rows_zeroed, 1)
            pe.wait_ge(c_split, 2)
            pe.wait_ge(w_split, 4)
            pe.wait_ge(lora_add, 12)
            for m in range(PAIRS):
                last = product(ps_s[:, 0, m * 64:m * 64 + 64], lambda a, n: kipaw[:, a, n, m * P:m * P + P],
                               lambda a, n: ctx_s[:, a, n, BATCH * ORG:BATCH * CTX], KD)
            last.then_inc(ipa_mm, 1)
            pe.wait_ge(w_split, 5)
            for c in (0, 1):
                last = product(ps_s[0:BATCH * IPA, 1 + c, :], lambda a, n: ctx_s[:, a, n, BATCH * ORG:BATCH * CTX],
                               lambda a, n: vipaw[:, a, n, c * 512:c * 512 + 512], KD)
            last.then_inc(ipa_mm, 1)
            pe.wait_ge(ipa_split, 4)
            lora_products("o")
            new_keys(0, 0)
            pe.wait_ge(xt_split, 1)
            new_keys(0, 1)
            for k in range(4):
                if k == 3:
                    pe.wait_ge(q_split, 1)
                queries(0, k)
            pe.wait_ge(k_split, 1)
            new_values(0, 0)
            pe.wait_ge(k_split, 2)
            new_values(0, 1)
            pe.wait_ge(w_split, 6)
            pe.wait_ge(lora_add, 16)
            pe.wait_ge(pt_zeroed, 1)

            def body(b, first, last):
                scores(b, 0)
                if not first:
                    pe.wait_ge(v_split, 2 * b + 1)
                    project(b - 1)
                scores(b, 1)
                if not last:
                    pe.wait_ge(v_split, 2 * b + 2)
                    transpose_x(b + 1)
                    pe.wait_ge(xt_split, b + 2)
                    pe.wait_ge(pt_split, 8 * b)
                    for k in range(4):
                        if k == 3:
                            pe.wait_ge(q_split, 4 * b + 5)
                        queries(b + 1, k)
                    pe.wait_ge(x1_done, b)
                    new_keys(b + 1, 0)
                    new_keys(b + 1, 1)
                for k in range(8):
                    if k >= 3:
                        pe.wait_ge(pt_split, 8 * b + k - 2)
                    elif not last:
                        pe.wait_ge(q_split, 4 * b + 6 + k)
                    else:
                        pe.wait_ge(pt_split, 8 * b)
                    transpose_probs(b, k)
                pe.wait_ge(pt_split, 8 * b + 8)
                pe.wait_ge(v_split, 2 * b + 2)
                pe.wait_ge(vipa_in, 16 * b + 16)
                for k in range(4):
                    if k >= 2:
                        pe.wait_ge(ot_split, 4 * b + k - 1)
                    elif not last:
                        pe.wait_ge(k_split, 2 * b + 3 + k)
                    else:
                        pe.wait_ge(x1_done, b)
                    attend(b, k)
                if not last:
                    for k in (0, 1):
                        pe.wait_ge(ot_split, 4 * b + 3 + k)
                        new_values(b + 1, k)

            body(0, True, False)
            with pe.Fori(1, BATCH - 1) as b:
                body(b, False, False)
            body(BATCH - 1, False, True)
            project(BATCH - 1)
            ffn_pe(pe, product)



def kernel(**inputs):
    import numpy as _np
    import concourse.bacc as _bacc
    from concourse.bass_utils import run_bass_kernel_spmd as _run

    i = {n.replace("L0_xattn_", "").replace("L0_ffn_", ""): _np.asarray(a) for n, a in inputs.items()}
    c = i["ctx_768"]
    ctx_t = _np.concatenate([c[:, :ORG].reshape(-1, CD), c[:, ORG:].reshape(-1, CD)]).T
    w1 = i["w1"].reshape(EXPERTS, KD, P, DFF).transpose(0, 2, 1, 3).reshape(EXPERTS, 1, P, FW)
    w2 = i["w2"].reshape(EXPERTS, DFF // P, P, DM).transpose(0, 2, 1, 3).reshape(EXPERTS, 1, P, FW)
    ffn_w = _np.concatenate([w1, w2], axis=1).reshape(2 * EXPERTS, P, FW)
    laid = {
        "x": i["x"], "ctx_t": ctx_t, "wq": i["Wq"], "wk": i["Wk"], "wv": i["Wv"], "wo": i["Wo"], "bo": i["bo"],
        "q_down_t": i["q_down"].T, "q_up": i["q_up"], "q_alpha": i["q_alpha"],
        "k_down_t": i["k_down"].T, "k_up": i["k_up"], "k_alpha": i["k_alpha"],
        "v_down_t": i["v_down"].T, "v_up": i["v_up"], "v_alpha": i["v_alpha"],
        "o_down_t": i["o_down"].T, "o_up": i["o_up"], "o_alpha": i["o_alpha"],
        "wk_ipa": i["Wk_ipa"], "wv_ipa": i["Wv_ipa"], "gate_w": i["gate_w"], "ffn_w": ffn_w,
    }
    nc = _bacc.Bacc("TRN2", target_bir_lowering=False, num_devices=1)
    arrays, args = {}, {}
    for name, a in laid.items():
        a = _np.ascontiguousarray(a)
        arrays[f"in_{name}"] = a
        args[name] = nc.dram_tensor(f"in_{name}", a.shape, mybir.dt.from_np(a.dtype), kind="ExternalInput").ap()
    args["out"] = nc.dram_tensor("out_x", (BATCH, SEQ, DM), F32, kind="ExternalOutput").ap()
    build(nc, **args)
    return _run(nc, [arrays], core_ids=[0]).results[0]["out_x"]
```

```python
from contextlib import ExitStack

import concourse.bass as bass
from concourse import mybir

F32 = mybir.dt.float32
F16 = mybir.dt.float16
U32 = mybir.dt.uint32
I32 = mybir.dt.int32
ALU = mybir.AluOpType
ACT = mybir.ActivationFunctionType
AX = mybir.AxisListType.X

P = 128
BATCH, SEQ, DM = 16, 256, 256
HEADS, DH = 16, 64
ID = HEADS * DH
CD, CTX, IPA = 192, 77, 4
ORG = CTX - IPA
RANK = 32
EXPERTS, DFF = 8, 512
PAIRS = HEADS // 2
KD = DM // P
CDR = CD - P
TILES = BATCH * SEQ // P
TPB = SEQ // P
KEYS = HEADS * CTX
WSCALE = 64.0
PSCALE = 64.0
LN_EPS = 1e-5
HPB = 4
FW = 1024
TOKENS = BATCH * SEQ
TOPK = 2
FT = DFF // P
RT = 256
SUB = RT // P
NT = (TOPK * TOKENS + EXPERTS * (RT - 1)) // RT
REGION = TOKENS + RT
ROW = 2 * DM + 8 + 8
META = 2 * DM
UNROLL = 4


def build(nc, x, ctx_t, wq, wk, wv, wo, bo, q_down_t, q_up, q_alpha, k_down_t, k_up, k_alpha,
          v_down_t, v_up, v_alpha, o_down_t, o_up, o_alpha, wk_ipa, wv_ipa, gate_w, ffn_w, out):
    stack = ExitStack()
    with stack:
        def sb(name, shape, dt):
            return stack.enter_context(nc.sbuf_tensor(name, shape, dt))

        def sem(name):
            return stack.enter_context(nc.semaphore(name))

        x_sb = sb("x_sb", [P, TILES, DM], F32)
        ffnw = sb("ffnw", [P, 2, 2 * EXPERTS, FW], F16)
        wq_s = sb("wq_s", [P, 2, KD, ID], F16)
        wk_s = sb("wk_s", [P, 2, KD, ID], F16)
        wv_s = sb("wv_s", [P, 2, KD, ID], F16)
        wo_s = sb("wo_s", [P, 2, PAIRS, DM], F16)
        ctx_s = sb("ctx_s", [P, 2, KD, BATCH * CTX], F16)
        kipa_s = sb("kipa_s", [P, 2, PAIRS, BATCH, IPA], F16)
        kbd = sb("kbd", [P, 2, PAIRS, 2 * CTX], F16)
        v_s = sb("v_s", [P, 2, ID], F16)
        q_s = sb("q_s", [P, 2, PAIRS, SEQ], F16)
        xn = sb("xn", [P, TPB, DM], F32)
        xt_s = sb("xt_s", [P, 2, KD, SEQ], F16)
        prob = sb("prob", [P, TPB, KEYS], F32)
        pt_s = sb("pt_s", [P, 2, HEADS, SEQ], F16)
        ot_s = sb("ot_s", [P, 2, PAIRS, SEQ], F16)
        wstage = sb("wstage", [P, FW], F32)
        bo_sb = sb("bo_sb", [P, DM], F32)
        gate_f = sb("gate_f", [P, KD, EXPERTS], F32)
        ident = sb("ident", [P, P], F32)
        iota8 = sb("iota8", [P, EXPERTS], F32)
        alphas = sb("alphas", [RANK, 4], F32)
        ln_mean = sb("ln_mean", [P, TILES], F32)
        ln_std = sb("ln_std", [P, TILES], F32)
        ln_rstd = sb("ln_rstd", [P, TILES], F32)
        mx = sb("mx", [P, TPB, 2, HEADS], F32)
        sm = sb("sm", [P, TPB, 2, HEADS], F32)
        rc = sb("rc", [P, TPB, 2, HEADS], F32)

        pstage = pt_s[:, :, :, :].rearrange("p a h n -> p (a h n)").bitcast(F32).rearrange(
            "p (s n) -> p s n", s=2)
        cstage = ot_s[:, :, :, :].rearrange("p a h n -> p (a h n)").bitcast(F32)
        prob_flat = prob[:].rearrange("p t n -> p (t n)")
        stats = prob_flat[:, 0:6 * TILES].rearrange("p (t s) -> p t s", s=6)
        ln_tmp = prob_flat[:, 6 * TILES:12 * TILES].rearrange("p (s t) -> p s t", s=6)
        early = ffnw[:, :, :, :].rearrange("p a e n -> p (a e n)")
        kipaw = early[:, 0:4096].rearrange("p (a k n) -> p a k n", a=2, k=KD)
        vipaw = early[:, 4096:8192].rearrange("p (a k n) -> p a k n", a=2, k=KD)
        vipa_s = early[0:BATCH * IPA, 8192:8192 + 2 * ID].rearrange("p (a n) -> p a n", a=2)
        lora = early[0:RANK, 12288:12288 + 2 * 9216].bitcast(F32)
        ups = {"q": lora[:, 0:1024], "k": lora[:, 1024:2048], "v": lora[:, 2048:3072], "o": lora[:, 3072:3328]}
        downs = {"q": lora[:, 3328:3584], "k": lora[:, 3584:3776], "v": lora[:, 3776:3968],
                 "o": lora[:, 3968:4992]}

        hold = sb("hold", [P, 1], F32)
        hold_p = sb("hold_p", [P, 2], F32)
        ident_h = sb("ident_h", [P, P], F16)
        before = sb("before", [P, P], F16)
        ones = sb("ones", [P, P], F16)
        ln2 = sb("ln2", [P, TPB, 2], F32)
        ln2_s = sb("ln2_s", [P, 3, TPB], F32)
        st2 = sb("st2", [P, TPB, 6], F32)
        x2n = xn
        x2t = sb("x2t", [P, KD, SEQ], F32)
        row_words = sb("row_words", [P, TPB, ROW // 2], I32)
        row = row_words[:].bitcast(F16)
        tok = sb("tok", [P, TILES], I32)
        lg = sb("lg", [P, TPB, EXPERTS], F32)
        top = sb("top", [P, TPB, EXPERTS], F32)
        top_i = sb("top_i", [P, TPB, EXPERTS], U32)
        top_f = sb("top_f", [P, TPB, EXPERTS], F32)
        gap = sb("gap", [P, TPB], F32)
        gap_exp = sb("gap_exp", [P, TPB], F32)
        w_sum = sb("w_sum", [P, TPB], F32)
        w_a = sb("w_a", [P, TPB], F32)
        picks = sb("picks", [P, TOPK, TPB, EXPERTS], F32)
        both = sb("both", [P, TPB, EXPERTS], F16)
        place = sb("place", [P, TPB, EXPERTS], F32)
        picked = sb("picked", [P, TOPK, TPB, EXPERTS], F32)
        slot_f = sb("slot_f", [P, TOPK, TPB], F32)
        slot_i = sb("slot_i", [P, TOPK, TPB], I32)
        counts = sb("counts", [P, EXPERTS], F32)
        reg0 = sb("reg0", [P, EXPERTS], F32)
        steps_of = sb("steps_of", [P, TOKENS // RT], F32)
        tiles_e = sb("tiles_e", [P, EXPERTS], F32)
        zero8 = sb("zero8", [P, EXPERTS], F32)
        ends = sb("ends", [P, EXPERTS], F32)
        tnum = sb("tnum", [P, NT], F32)
        e_of = sb("e_of", [P, NT], F32)
        wt = sb("wt", [P, UNROLL, SUB], F32)
        token_of = sb("token_of", [P, UNROLL, SUB], I32)
        table = sb("table", [1, 2, NT], I32)
        pads = sb("pads", [1, EXPERTS], I32)

        ps_s = stack.enter_context(nc.psum_tensor("ps_s", [P, 3, 512], F32))
        ps_a = stack.enter_context(nc.psum_tensor("ps_a", [P, 3, 512], F32))
        ps_b = stack.enter_context(nc.psum_tensor("ps_b", [P, 2, 512], F32))

        rows_dram = nc.dram_tensor("rows_dram", (EXPERTS * REGION + RT, ROW // 2), I32, kind="Internal").ap()
        vipa_dram = nc.dram_tensor("vipa_dram", (BATCH, IPA, 2, ID), F16, kind="Internal").ap()

        S = {}
        x_in = [sem(f"x_in{c}") for c in range(4)]
        lora_in = sem("lora_in")
        misc_in = sem("misc_in")
        ctx_in = sem("ctx_in")
        pst_in = [sem(f"pst_in{s}") for s in range(2)]
        consts = sem("consts")
        zeroed = sem("zeroed")
        rows_zeroed = sem("rows_zeroed")
        pt_zeroed = sem("pt_zeroed")
        downs_ok = sem("downs_ok")
        lora_mm = sem("lora_mm")
        lora_add = sem("lora_add")
        w_hi = sem("w_hi")
        w_split = sem("w_split")
        c_hi = sem("c_hi")
        c_split = sem("c_split")
        ipa_mm = sem("ipa_mm")
        ipa_hi = sem("ipa_hi")
        ipa_split = sem("ipa_split")
        vipa_out = sem("vipa_out")
        ln_link = sem("ln_link")
        ln_var = sem("ln_var")
        ln_sqrt = sem("ln_sqrt")
        ln_done = sem("ln_done")
        xn_done = sem("xn_done")
        xt_mm = sem("xt_mm")
        xt_hi = sem("xt_hi")
        xt_split = sem("xt_split")
        q_mm = sem("q_mm")
        q_hi = sem("q_hi")
        q_split = sem("q_split")
        k_mm = sem("k_mm")
        k_hi = sem("k_hi")
        k_split = sem("k_split")
        kipa_put = sem("kipa_put")
        v_mm = sem("v_mm")
        v_hi = sem("v_hi")
        v_split = sem("v_split")
        vipa_in = sem("vipa_in")
        s_mm = sem("s_mm")
        s_copied = sem("s_copied")
        mx_done = sem("mx_done")
        shifted = sem("shifted")
        exp_done = sem("exp_done")
        sum_done = sem("sum_done")
        rc_done = sem("rc_done")
        p_ready = sem("p_ready")
        t_mm = sem("t_mm")
        pt_hi = sem("pt_hi")
        pt_split = sem("pt_split")
        pv_mm = sem("pv_mm")
        ot_hi = sem("ot_hi")
        ot_split = sem("ot_split")
        wo_mm = sem("wo_mm")
        bo_added = sem("bo_added")
        x1_done = sem("x1_done")
        st_done = sem("st_done")
        fw_in = sem("fw_in")
        fw_hi = sem("fw_hi")
        fw_split = sem("fw_split")

        for n in ("st2_done", "ag2_done", "var2", "std2", "rstd2", "x2n_done", "row_hi", "row_lo", "row_meta", "x2_mm",
                  "x2_copied", "lg_mm", "lg_copied", "route", "gap_done", "gap_expd", "both_done", "rank_mm",
                  "placed", "slots", "scattered", "acc_in", "pad_in", "pad_made", "held", "tab", "tab_done", "tx_mm",
                  "tx_copied", "h_mm", "silu_done", "h_hi", "h_split", "wt_done", "y_mm", "y_done", "added",
                  "out_done", "consts2"):
            S[n] = sem(n)
        (st2_done, ag2_done, var2, std2, rstd2, x2n_done, row_hi, row_lo, row_meta, x2_mm, x2_copied, lg_mm, lg_copied,
         route, gap_done, gap_expd, both_done, rank_mm, placed, slots, scattered, acc_in, pad_in, pad_made, held, tab, tab_done,
         tx_mm, tx_copied, h_mm, silu_done, h_hi, h_split, wt_done, y_mm, y_done, added, out_done,
         consts2) = S.values()

        tile_in = [sem(f"tile_in{n}") for n in range(UNROLL)]

        jobs = ["q", "k", "v", "ki", "vi", "o"]
        job_src = {"q": wq, "k": wk, "v": wv, "ki": wk_ipa, "vi": wv_ipa, "o": wo}
        job_dst = {"q": wq_s, "k": wk_s, "v": wv_s, "ki": kipaw, "vi": vipaw, "o": wo_s}
        lora_jobs = ["q", "k", "v", "o"]
        x_view = x.rearrange("b (t p) d -> p (b t) d", p=P)
        out_rows = out.rearrange("b n d -> (b n) d")

        def job_parts(j):
            if j in ("q", "o"):
                return [(P, 0, 2048)]
            return [(P, 0, 1024), (CDR, 1024, 2048)]

        def dst_flat(j, part):
            return job_dst[j][:, part].rearrange("p k n -> p (k n)")

        xg_words = prob[:].rearrange("p t n -> p (t n)").bitcast(I32)[:, 0:UNROLL * SUB * ROW // 2].rearrange(
            "p (s c n) -> p s c n", s=UNROLL, c=SUB)
        xg = prob[:].rearrange("p t n -> p (t n)").bitcast(F16)[:, 0:UNROLL * SUB * ROW].rearrange(
            "p (s c n) -> p s c n", s=UNROLL, c=SUB)
        q_flat = q_s[:].rearrange("p a m n -> p (a m n)")
        tx = q_flat[:, 0:2 * 2 * KD * RT].rearrange("p (s a k n) -> p s a k n", s=2, a=2, k=KD)
        h32 = q_flat[:, 2048:4096].bitcast(F32).rearrange("p (j n) -> p j n", j=2)
        hs = ot_s[:].rearrange("p a m n -> p (a m n)").rearrange("p (s a f n) -> p s a f n", s=2, a=2, f=FT)
        y_sb = pt_s[:].rearrange("p a h n -> p (a h n)").bitcast(F32)[:, 0:UNROLL * SUB * DM].rearrange(
            "p (s c n) -> p s c n", s=UNROLL, c=SUB)
        xn_flat = xn[:].rearrange("p t d -> p (t d)")
        past = xn_flat[:, 0:NT * EXPERTS].rearrange("p (t e) -> p t e", t=NT)
        ge = xn_flat[:, NT * EXPERTS:NT * EXPERTS + 128].rearrange("p (e n) -> p e n", e=EXPERTS)
        start_of = bo_sb[:, 0:NT]
        row_of = bo_sb[:, NT:2 * NT]
        past_n = x2t[:].rearrange("p k n -> p (k n)")[:, 0:NT * EXPERTS].rearrange("p (t e) -> p t e", t=NT)
        pad_rows = wstage[:].bitcast(I32)[:, 0:SUB * ROW // 2].rearrange("p (c n) -> p c n", c=SUB)
        tx_ps = [ps_s[:, s, :].bitcast(F16) for s in (0, 1)]

        def probs_bank(k):
            return (ps_s[:, 0, :], ps_s[:, 1, :], ps_a[:, 1, :], ps_a[:, 2, :], ps_a[:, 0, :])[k % 5]

        def h_ps(t, j):
            n = 2 * (t % 2) + j
            return ps_a[:, n, :] if n < 3 else ps_s[:, 2, :]

        def run_tiles(eng, step):
            for t in range(UNROLL):
                step(t, t)
            loops = (NT - UNROLL) // UNROLL
            with eng.Fori(1, loops) as i:
                for j in range(UNROLL):
                    step(i * UNROLL + j, j)
            for t in range(loops * UNROLL, NT):
                step(t, t)

        def fill_up(eng, experts):
            eng.wait_ge(pad_made, 4)
            eng.wait_ge(tab_done, 1)
            for e in experts:
                r = eng.value_load(pads[0:1, e:e + 1], min_val=0, max_val=EXPERTS * REGION - RT)
                eng.dma_start(rows_dram[bass.ds(r, RT), :].rearrange("(c p) n -> p c n", p=P), pad_rows
                              ).then_inc(pad_in, 16)

        def ffn_sp(sp):
            fill_up(sp, range(0, EXPERTS, 2))
            sp.wait_ge(tab_done, 2)
            sp.wait_ge(scattered, 16 + 16 * TOPK * TILES)
            sp.wait_ge(pad_in, 16 * EXPERTS)

            def load(t, slot):
                r = sp.value_load(table[0:1, 0, bass.ds(t, 1)], min_val=0, max_val=EXPERTS * REGION)
                sp.dma_start(xg_words[:, slot], rows_dram[bass.ds(r, RT), :].rearrange("(c p) n -> p c n", p=P)
                             ).then_inc(tile_in[slot], 16)

            def step(t, j):
                if isinstance(t, int) and t + UNROLL >= NT:
                    return
                sp.wait_ge(wt_done, 2 * t + 2)
                load(t + UNROLL, j % UNROLL)

            for t in range(UNROLL):
                load(t, t)
            run_tiles(sp, step)
            sp.wait_ge(added, 16 * SUB * NT)

        def ffn_pool(pool):
            pool.wait_ge(acc_in, 16 * BATCH)

            def step(t, j):
                pool.wait_ge(y_done, t + 1)
                if not (isinstance(t, int) and t == 0):
                    pool.wait_ge(added, 16 * SUB * t)
                    pool.wait_ge(held, t)
                pool.tensor_tensor(hold_p[:, 1:2], zero8[:, 0:1], zero8[:, 1:2], ALU.add).then_inc(held, 1)
                for c in range(SUB):
                    pool.indirect_dma_start(
                        out_rows, bass.IndirectOffsetOnAxis(ap=token_of[:, j % UNROLL, c:c + 1], axis=0),
                        y_sb[:, j % UNROLL, c, :], None, bounds_check=TOKENS - 1, oob_is_err=False,
                        compute_op=ALU.add).then_inc(added, 16)

            run_tiles(pool, step)

        def ffn_pe(pe, product):
            def weights_of(t):
                return pe.value_load(table[0:1, 1, bass.ds(t, 1)], min_val=0, max_val=EXPERTS - 1)

            def transposes(t, j):
                pe.wait_ge(tile_in[j % UNROLL], 16 * (t // UNROLL + 1) if isinstance(t, int) else tile_wait(t, j))
                if not (isinstance(t, int) and t < 2):
                    pe.wait_ge(tx_copied, t - 1)
                for part in (0, 1):
                    for kk in range(KD):
                        for c in range(SUB):
                            o = (part * KD + kk) * RT + c * P
                            s = part * DM + kk * P
                            last = pe.transpose(tx_ps[j % 2][:, o:o + P], xg[:, j % UNROLL, c, s:s + P], ident_h[:])
                last.then_inc(tx_mm, 1)

            def tile_wait(t, j):
                return (t - (j % UNROLL)) * (16 // UNROLL) + 16

            def hidden(t, j):
                e = weights_of(t)
                pe.wait_ge(tx_copied, t + 1)
                for half in (0, 1):
                    if not (isinstance(t, int) and t < 2):
                        pe.wait_ge(silu_done, 2 * t - 3 + half)
                    for m in (2 * half, 2 * half + 1):
                        o = (m % 2) * RT
                        last = product(h_ps(j, half)[:, o:o + RT],
                                       lambda a, n: ffnw[:, a, bass.ds(2 * e, 1), n * DFF + m * P:n * DFF + m * P + P]
                                       .rearrange("p e n -> p (e n)"),
                                       lambda a, n: tx[:, j % 2, a, n, :], KD)
                    last.then_inc(h_mm, 1)

            def down(t, j):
                e = weights_of(t)
                pe.wait_ge(h_split, 2 * t + 2)
                if not (isinstance(t, int) and t < 2):
                    pe.wait_ge(y_done, t - 1)
                for c in range(SUB):
                    last = product(ps_b[:, j % 2, c * DM:c * DM + DM],
                                   lambda a, n: hs[:, j % 2, a, n, c * P:c * P + P],
                                   lambda a, n: ffnw[:, a, bass.ds(2 * e + 1, 1), n * DM:n * DM + DM]
                                   .rearrange("p e n -> p (e n)"), FT)
                last.then_inc(y_mm, 1)

            def step(t, j):
                if not (isinstance(t, int) and t + 2 >= NT):
                    transposes(t + 2, j + 2)
                if not (isinstance(t, int) and t + 1 >= NT):
                    hidden(t + 1, j + 1)
                down(t, j)

            pe.wait_ge(fw_split, 2 * EXPERTS)
            pe.wait_ge(tab_done, 1)
            transposes(0, 0)
            transposes(1, 1)
            hidden(0, 0)
            run_tiles(pe, step)

        def ffn_act(act):
            def hidden(t, j):
                for half in (0, 1):
                    act.wait_ge(h_mm, 2 * t + half + 1)
                    if not (isinstance(t, int) and t < 1):
                        act.wait_ge(h_split, 2 * t - 1 + half)
                    act.activation(h32[:, half, :], h_ps(j, half), ACT.Silu, scale=1 / WSCALE).then_inc(silu_done, 1)
                    act.wait_ge(silu_done, 2 * t + half + 1)
                    if not (isinstance(t, int) and t < 2):
                        act.wait_ge(y_mm, t - 1)
                    act.activation(hs[:, j % 2, 0, 2 * half:2 * half + 2, :].rearrange("p f n -> p (f n)"),
                                   h32[:, half, :], ACT.Copy).then_inc(h_hi, 1)

            def step(t, j):
                if not (isinstance(t, int) and t + 1 >= NT):
                    hidden(t + 1, j + 1)

            fill_up(act, range(1, EXPERTS, 2))
            hidden(0, 0)
            run_tiles(act, step)

        def ffn_dve(dve):
            n = [0]

            def step_tab(ins):
                n[0] += 1
                ins.then_inc(tab, 1)
                dve.wait_ge(tab, n[0])

            dve.tensor_tensor(pads[:], reg0[0:1, :], counts[0:1, :], ALU.add).then_inc(tab_done, 1)
            dve.wait_ge(row_lo, BATCH + 1)
            step_tab(dve.tensor_tensor(ge, counts[:].unsqueeze(2).to_broadcast([P, EXPERTS, TOKENS // RT]),
                                       steps_of[:].unsqueeze(1).to_broadcast([P, EXPERTS, TOKENS // RT]), ALU.is_gt))
            step_tab(dve.tensor_reduce(tiles_e[:], ge, AX, ALU.add))
            step_tab(dve.tensor_tensor_scan(ends[:], tiles_e[:], zero8[:], 0.0, ALU.add, ALU.add))
            step_tab(dve.tensor_tensor(past, ends[:].unsqueeze(1).to_broadcast([P, NT, EXPERTS]),
                                       tnum[:].unsqueeze(2).to_broadcast([P, NT, EXPERTS]), ALU.is_le))
            step_tab(dve.tensor_reduce(e_of[:], past, AX, ALU.add))
            step_tab(dve.tensor_tensor(past_n, past, tiles_e[:].unsqueeze(1).to_broadcast([P, NT, EXPERTS]),
                                       ALU.mult))
            step_tab(dve.tensor_reduce(start_of, past_n, AX, ALU.add))
            step_tab(dve.tensor_tensor(row_of, tnum[:], start_of, ALU.subtract))
            step_tab(dve.tensor_scalar(row_of, row_of, float(RT), None, ALU.mult))
            step_tab(dve.scalar_tensor_tensor(out=row_of, in0=e_of[:], scalar=float(REGION), in1=row_of,
                                              op0=ALU.mult, op1=ALU.add))
            dve.tensor_scalar(table[:, 0, :], row_of[0:1, :], float(EXPERTS * REGION), None, ALU.min)
            dve.tensor_scalar(table[:, 1, :], e_of[0:1, :], float(EXPERTS - 1), None, ALU.min).then_inc(tab_done, 1)

            def rows_in(t, j):
                dve.wait_ge(tx_mm, t + 1)
                if not (isinstance(t, int) and t < 2):
                    dve.wait_ge(h_mm, 2 * t - 2)
                dve.tensor_copy(tx[:, j % 2].rearrange("p a k n -> p (a k n)"), tx_ps[j % 2]).then_inc(tx_copied, 1)
                if not (isinstance(t, int) and t < UNROLL):
                    dve.wait_ge(added, 16 * SUB * (t - UNROLL + 1))
                dve.tensor_copy(token_of[:, j % UNROLL, :], xg_words[:, j % UNROLL, :, META // 2])
                meta = xg[:, j % UNROLL, :, META:META + 8].bitcast(F32)
                dve.scalar_tensor_tensor(out=wt[:, j % UNROLL, :], in0=meta[:, :, 1], scalar=e_of[:, bass.ds(t, 1)],
                                         in1=meta[:, :, 2], op0=ALU.is_equal, op1=ALU.mult).then_inc(wt_done, 1)
                dve.wait_ge(wt_done, 2 * t + 1)
                dve.tensor_tensor(wt[:, j % UNROLL, :], wt[:, j % UNROLL, :], meta[:, :, 3], ALU.add
                                  ).then_inc(wt_done, 1)

            def low(t, j):
                for half in (0, 1):
                    dve.wait_ge(h_hi, 2 * t + half + 1)
                    dve.tensor_tensor(hs[:, j % 2, 1, 2 * half:2 * half + 2, :].rearrange("p f n -> p (f n)"),
                                      h32[:, half, :],
                                      hs[:, j % 2, 0, 2 * half:2 * half + 2, :].rearrange("p f n -> p (f n)"),
                                      ALU.subtract).then_inc(h_split, 1)

            def result(t, j):
                dve.wait_ge(y_mm, t + 1)
                dve.wait_ge(wt_done, 2 * t + 2)
                for c in range(SUB):
                    last = dve.tensor_scalar(y_sb[:, j % UNROLL, c, :], ps_b[:, j % 2, c * DM:c * DM + DM],
                                             wt[:, j % UNROLL, c:c + 1], 1 / WSCALE, ALU.mult, ALU.mult)
                last.then_inc(y_done, 1)

            def step(t, j):
                if not (isinstance(t, int) and t + 2 >= NT):
                    rows_in(t + 2, j + 2)
                if not (isinstance(t, int) and t + 1 >= NT):
                    low(t + 1, j + 1)
                result(t, j)

            rows_in(0, 0)
            rows_in(1, 1)
            low(0, 0)
            run_tiles(dve, step)

        block = stack.enter_context(nc.Block())

        @block.sync
        def _(sp):
            for j, (dn, up) in {"q": (q_down_t, q_up), "k": (k_down_t, k_up), "v": (v_down_t, v_up),
                                "o": (o_down_t, o_up)}.items():
                sp.dma_start(downs[j], dn).then_inc(lora_in, 16)
                sp.dma_start(ups[j], up).then_inc(lora_in, 16)
            for n, a in enumerate((q_alpha, k_alpha, v_alpha, o_alpha)):
                sp.dma_start(alphas[:, n:n + 1], a.rearrange("(a b) -> a b", a=1).to_broadcast([RANK, 1])
                             ).then_inc(lora_in, 16)

            def load_job(n):
                j, slot = jobs[n], n % 2
                if n >= 2:
                    sp.wait_ge(w_split, n - 1)
                if j in ("q", "o"):
                    nk = KD if j == "q" else PAIRS
                    dst = pstage[:, slot, :].rearrange("p (k n) -> p k n", k=nk)
                    src = job_src[j].rearrange("(k p) n -> p k n", p=P)
                    for c in (0, 1):
                        ks = slice(c * nk // 2, (c + 1) * nk // 2)
                        sp.dma_start(dst[:, ks], src[:, ks]).then_inc(pst_in[slot], 16)
                else:
                    sp.dma_start(pstage[:, slot, 0:ID], job_src[j][0:P, :]).then_inc(pst_in[slot], 16)
                    sp.dma_start(pstage[0:CDR, slot, ID:2 * ID], job_src[j][P:CD, :]).then_inc(pst_in[slot], 16)

            load_job(0)
            load_job(1)
            for c in range(4):
                sp.dma_start(x_sb[:, c * 8:c * 8 + 8, :], x_view[:, c * 8:c * 8 + 8, :]).then_inc(x_in[c], 16)
            sp.dma_start(cstage[:, 0:BATCH * CTX], ctx_t[0:P, :]).then_inc(ctx_in, 16)
            sp.dma_start(bo_sb[:], bo.rearrange("(a n) -> a n", a=1).to_broadcast([P, DM])).then_inc(misc_in, 16)
            sp.dma_start(gate_f[:], gate_w.rearrange("(k p) e -> p k e", p=P)).then_inc(misc_in, 16)
            sp.wait_ge(c_split, 1)
            sp.dma_start(cstage[0:CDR, 0:BATCH * CTX], ctx_t[P:CD, :]).then_inc(ctx_in, 16)
            for n in range(2, 6):
                load_job(n)
            sp.wait_ge(ipa_split, 4)
            sp.dma_start(vipa_dram.rearrange("b i a n -> (b i) a n"), vipa_s).then_inc(vipa_out, 16)
            sp.wait_ge(vipa_out, 16)
            sp.wait_ge(zeroed, 2)
            sp.dma_start(v_s[ORG:CTX, :, :], vipa_dram[0]).then_inc(vipa_in, 16)

            def store_x1(b):
                sp.wait_ge(x1_done, b + 1)
                sp.dma_start(out_rows[bass.ds(b * SEQ, SEQ), :].rearrange("(t p) d -> p t d", p=P),
                             x_sb[:, bass.ds(b * TPB, TPB), :]).then_inc(acc_in, 16)

            def body(b, first, last):
                if not first:
                    store_x1(b - 1)
                if not first:
                    sp.wait_ge(fw_split, b)
                else:
                    sp.wait_ge(ipa_split, 4)
                sp.dma_start(wstage[:], ffn_w[b]).then_inc(fw_in, 16)
                if not last:
                    sp.wait_ge(pv_mm, 4 * b + 4)
                    sp.dma_start(v_s[ORG:CTX, :, :], vipa_dram[bass.ds(b + 1, 1)].rearrange("a i h n -> (a i) h n")
                                 ).then_inc(vipa_in, 16)

            body(0, True, False)
            with sp.Fori(1, BATCH - 1) as b:
                body(b, False, False)
            body(BATCH - 1, False, True)
            store_x1(BATCH - 1)
            ffn_sp(sp)

        @block.gpsimd
        def _(pool):
            pool.memset(ident[:], 0.0).then_inc(consts, 1)
            pool.iota(iota8[:], [[1, EXPERTS]], base=0, channel_multiplier=0,
                      allow_small_or_imprecise_dtypes=True).then_inc(consts, 1)
            pool.wait_ge(consts, 2)
            pool.affine_select(out=ident[:], in_=ident[:], compare_op=ALU.not_equal, fill=1.0, base=0,
                               pattern=[[-1, P]], channel_multiplier=1).then_inc(consts, 1)
            pool.memset(row_words[:], 0).then_inc(pad_made, 1)
            pool.wait_ge(pad_made, 1)
            pool.iota(row_words[:, :, META // 2:META // 2 + 1], [[0, SUB], [0, 1]], base=TOKENS,
                      channel_multiplier=0).then_inc(pad_made, 1)
            pool.wait_ge(pad_made, 2)
            pool.dma_start(rows_dram[EXPERTS * REGION:EXPERTS * REGION + RT, :].rearrange("(c p) n -> p c n", p=P),
                           row_words[:]).then_inc(scattered, 16)
            pool.memset(ident_h[:], 0.0).then_inc(consts2, 1)
            pool.memset(before[:], 0.0).then_inc(consts2, 1)
            pool.memset(ones[:], 1.0).then_inc(consts2, 1)
            pool.memset(counts[:], 0.0).then_inc(consts2, 1)
            pool.memset(zero8[:], 0.0).then_inc(consts2, 1)
            pool.iota(tok[:], [[P, TILES]], base=0, channel_multiplier=1).then_inc(consts2, 1)
            pool.iota(reg0[:], [[REGION, EXPERTS]], base=0, channel_multiplier=0,
                      allow_small_or_imprecise_dtypes=True).then_inc(consts2, 1)
            pool.iota(steps_of[:], [[RT, TOKENS // RT]], base=0, channel_multiplier=0,
                      allow_small_or_imprecise_dtypes=True).then_inc(consts2, 1)
            pool.iota(tnum[:], [[1, NT]], base=0, channel_multiplier=0,
                      allow_small_or_imprecise_dtypes=True).then_inc(consts2, 1)
            pool.wait_ge(consts2, 9)
            pool.affine_select(out=ident_h[:], in_=ident_h[:], compare_op=ALU.not_equal, fill=1.0, base=0,
                               pattern=[[-1, P]], channel_multiplier=1).then_inc(consts2, 1)
            pool.affine_select(out=before[:], in_=before[:], compare_op=ALU.is_ge, fill=1.0, base=0,
                               pattern=[[-1, P]], channel_multiplier=1).then_inc(consts2, 1)
            pool.memset(kbd[:], 0.0).then_inc(zeroed, 1)
            pool.memset(v_s[:], 0.0).then_inc(zeroed, 1)

            def keys(t):
                v = prob[:, t, :].rearrange("p (h j) -> p h j", j=CTX)
                return [(v[:, :, 0:ORG], 0, ORG), (v[:, :, ORG:CTX], 1, IPA)]

            def shift(b, t):
                pool.wait_ge(mx_done, 2 * b + t + 1)
                for v, w, n in keys(t):
                    last = pool.tensor_tensor(v, v, mx[:, t, w, :].unsqueeze(2).to_broadcast([P, HEADS, n]),
                                              ALU.subtract)
                last.then_inc(shifted, 1)

            def normalise(b, t):
                pool.wait_ge(rc_done, 2 * b + t + 1)
                for v, w, n in keys(t):
                    last = pool.tensor_tensor(v, v, rc[:, t, w, :].unsqueeze(2).to_broadcast([P, HEADS, n]),
                                              ALU.mult)
                last.then_inc(p_ready, 1)

            def row_low(b):
                pool.wait_ge(row_hi, b + 1)
                pool.tensor_tensor(row[:, :, DM:2 * DM], x2n[:], row[:, :, 0:DM], ALU.subtract).then_inc(row_lo, 1)

            def scatter(b):
                pool.wait_ge(slots, b + 2)
                pool.wait_ge(row_meta, b + 1)
                pool.wait_ge(row_lo, b + 2)
                pool.tensor_tensor(hold_p[:, 0:1], zero8[:, 0:1], zero8[:, 1:2], ALU.add)
                for pick in range(TOPK):
                    for t in range(TPB):
                        pool.indirect_dma_start(
                            rows_dram, bass.IndirectOffsetOnAxis(ap=slot_i[:, pick, t:t + 1], axis=0), row_words[:, t, :],
                            None).then_inc(scattered, 16)

            def body(b, first, last):
                shift(b, 0)
                shift(b, 1)
                normalise(b, 0)
                normalise(b, 1)
                if not first:
                    row_low(b - 1)
                pool.wait_ge(xn_done, b + 1)
                xb = x_sb[:, bass.ds(b * TPB, TPB), :]
                pool.tensor_tensor(xb, xb, bo_sb[:].unsqueeze(1).to_broadcast([P, TPB, DM]), ALU.add
                                   ).then_inc(bo_added, 1)
                if not first:
                    scatter(b - 1)

            pool.wait_ge(misc_in, 32)
            body(0, True, False)
            with pool.Fori(1, BATCH - 1) as b:
                body(b, False, False)
            body(BATCH - 1, False, True)
            pool.wait_ge(fw_split, BATCH)
            pool.memset(pad_rows, 0).then_inc(pad_made, 1)
            pool.wait_ge(pad_made, 3)
            pool.iota(pad_rows[:, :, META // 2:META // 2 + 1], [[0, SUB], [0, 1]], base=TOKENS,
                      channel_multiplier=0).then_inc(pad_made, 1)
            row_low(BATCH - 1)
            scatter(BATCH - 1)
            ffn_pool(pool)

        def ipa_k_hi(act):
            act.wait_ge(ipa_mm, 1)
            act.activation(kipa_s[:, 0].rearrange("p m b i -> p (m b i)"), ps_s[:, 0, :], ACT.Copy,
                           scale=1 / WSCALE).then_inc(ipa_hi, 1)

        def ipa_v_hi(act):
            act.wait_ge(ipa_mm, 2)
            act.activation(vipa_s[:, 0, :], ps_s[0:BATCH * IPA, 1:3, :].rearrange("p c n -> p (c n)"), ACT.Copy,
                           scale=1 / WSCALE).then_inc(ipa_hi, 1)

        @block.scalar
        def _(act):
            def split_job(n):
                j, slot = jobs[n], n % 2
                if j in lora_jobs:
                    act.wait_ge(lora_add, 4 * lora_jobs.index(j) + 4)
                else:
                    act.wait_ge(pst_in[slot], 32 * (n // 2 + 1))
                for rows, lo, hi in job_parts(j):
                    last = act.activation(dst_flat(j, 0)[0:rows, lo:hi], pstage[0:rows, slot, lo:hi], ACT.Copy,
                                          scale=WSCALE)
                last.then_inc(w_hi, 1)

            split_job(0)
            split_job(1)
            act.wait_ge(ln_var, 1)
            act.activation(ln_std[:], ln_tmp[:, 5, :], ACT.Sqrt).then_inc(ln_sqrt, 1)
            for kk, rows in enumerate((P, CDR)):
                act.wait_ge(ctx_in, 16 * (kk + 1))
                act.activation(ctx_s[0:rows, 0, kk, :], cstage[0:rows, 0:BATCH * CTX], ACT.Copy).then_inc(c_hi, 1)
            for n in range(2, 6):
                split_job(n)
                if n == 3:
                    ipa_k_hi(act)
                if n == 4:
                    ipa_v_hi(act)

            def hi_of(dst, src, scale, ready, n, done):
                act.wait_ge(ready, n)
                act.activation(dst, src, ACT.Copy, scale=scale).then_inc(done, 1)

            def xt(b):
                hi_of(xt_s[:, 0].rearrange("p k n -> p (k n)"), ps_b[:, 1, :], 1.0, xt_mm, b + 1, xt_hi)

            def q(b, k):
                hi_of(q_s[:, 0, 2 * k:2 * k + 2, :].rearrange("p m n -> p (m n)"), ps_a[:, k % 3, :],
                      1 / WSCALE, q_mm, 4 * b + k + 1, q_hi)

            def k_(b, k):
                act.wait_ge(k_mm, 2 * b + k + 1)
                for half in (0, 1):
                    o = half * DH
                    last = act.activation(
                        kbd[o:o + DH, 0, 4 * k:4 * k + 4, half * CTX:half * CTX + ORG],
                        ps_b[o:o + DH, 1 - k, 0:4 * ORG].rearrange("p (m j) -> p m j", m=4), ACT.Copy,
                        scale=1 / WSCALE)
                last.then_inc(k_hi, 1)

            def put_kipa(b):
                for half in (0, 1):
                    o = half * DH
                    last = act.activation(
                        kbd[o:o + DH, :, :, half * CTX + ORG:half * CTX + CTX].rearrange("p a m j -> p (a m) j"),
                        kipa_s[o:o + DH, :, :, bass.ds(b, 1), :].rearrange("p a m b j -> p (a m) (b j)"), ACT.Copy)
                last.then_inc(kipa_put, 1)

            def v(b, k):
                hi_of(v_s[0:ORG, 0, k * 512:k * 512 + 512], ps_b[0:ORG, 1 - k, :], 1 / WSCALE, v_mm, 2 * b + k + 1, v_hi)

            def copy_scores(b, t):
                act.wait_ge(s_mm, 2 * b + t + 1)
                for c in range(3):
                    w = min(3, PAIRS - 3 * c) * 2 * CTX
                    last = act.activation(prob[:, t, c * 6 * CTX:c * 6 * CTX + w], ps_s[:, c, 0:w], ACT.Copy)
                last.then_inc(s_copied, 1)

            def exp(b, t):
                act.wait_ge(shifted, 2 * b + t + 1)
                act.activation(prob[:, t, :], prob[:, t, :], ACT.Exp, scale=DH ** -0.5).then_inc(exp_done, 1)

            def pt(b, k):
                t, h = k // 4, HPB * (k % 4)
                hi_of(pt_s[0:CTX, 0, h:h + HPB, t * P:t * P + P],
                      probs_bank(k)[0:CTX, :].rearrange("p (h n) -> p h n", h=HPB), PSCALE, t_mm, 8 * b + k + 1,
                      pt_hi)

            def ot(b, k):
                hi_of(ot_s[:, 0, 2 * k:2 * k + 2, :].rearrange("p m n -> p (m n)"), ps_b[:, (k + 1) % 2, :],
                      1 / (PSCALE), pv_mm, 4 * b + k + 1, ot_hi)

            def std_2(b):
                act.wait_ge(var2, b + 1)
                act.activation(ln2_s[:, 1, :], ln2_s[:, 0, :], ACT.Sqrt).then_inc(std2, 1)

            def row_high(b):
                act.wait_ge(x2n_done, b + 1)
                act.wait_ge(scattered, 64 * b + 16)
                act.activation(row[:, :, 0:DM], x2n[:], ACT.Copy).then_inc(row_hi, 1)

            def x2t_copy(b):
                act.wait_ge(x2_mm, b + 1)
                act.activation(x2t[:].rearrange("p k n -> p (k n)"), ps_b[:, 0, :], ACT.Copy).then_inc(x2_copied, 1)

            def gap_e(b):
                act.wait_ge(gap_done, b + 1)
                act.activation(gap_exp[:], gap[:], ACT.Exp).then_inc(gap_expd, 1)

            def body(b, first, last):
                copy_scores(b, 0)
                if not last:
                    xt(b + 1)
                copy_scores(b, 1)
                exp(b, 0)
                if not last:
                    q(b + 1, 0)
                    q(b + 1, 1)
                exp(b, 1)
                if not first:
                    std_2(b - 1)
                if not last:
                    q(b + 1, 2)
                pt(b, 0)
                pt(b, 1)
                if not last:
                    q(b + 1, 3)
                if not first:
                    row_high(b - 1)
                pt(b, 2)
                pt(b, 3)
                if not first:
                    x2t_copy(b - 1)
                if not last:
                    k_(b + 1, 0)
                    k_(b + 1, 1)
                    put_kipa(b + 1)
                for k in range(4, 8):
                    pt(b, k)
                    if k == 5 and not first:
                        gap_e(b - 1)
                act.wait_ge(fw_in, 16 * b + 16)
                act.activation(ffnw[:, 0, bass.ds(b, 1), :].rearrange("p e n -> p (e n)"), wstage[:], ACT.Copy,
                               scale=WSCALE).then_inc(fw_hi, 1)
                for k in range(4):
                    ot(b, k)
                if not last:
                    v(b + 1, 0)
                    v(b + 1, 1)

            xt(0)
            act.wait_ge(zeroed, 2)
            act.wait_ge(ipa_split, 4)
            k_(0, 0)
            k_(0, 1)
            put_kipa(0)
            for k in range(4):
                q(0, k)
            v(0, 0)
            v(0, 1)
            body(0, True, False)
            with act.Fori(1, BATCH - 1) as b:
                body(b, False, False)
            body(BATCH - 1, False, True)
            std_2(BATCH - 1)
            row_high(BATCH - 1)
            x2t_copy(BATCH - 1)
            gap_e(BATCH - 1)
            ffn_act(act)

        @block.vector
        def _(dve):
            links = [0]

            def link(ins):
                links[0] += 1
                ins.then_inc(ln_link, 1)
                dve.wait_ge(ln_link, links[0])

            def layer_stats(n):
                me, mo, cve, cvo = (stats[:, :, c] for c in (1, 4, 2, 5))
                tmp = [ln_tmp[:, c, :] for c in range(6)]
                link(dve.tensor_tensor(tmp[0], me, mo, ALU.add))
                link(dve.tensor_tensor(tmp[1], me, mo, ALU.subtract))
                link(dve.tensor_tensor(tmp[2], cve, cvo, ALU.add))
                link(dve.tensor_scalar(ln_mean[:], tmp[0], 0.5, None, ALU.mult))
                link(dve.tensor_tensor(tmp[3], tmp[1], tmp[1], ALU.mult))
                link(dve.tensor_scalar(tmp[4], tmp[2], 1.0 / DM, LN_EPS, ALU.mult, ALU.add))
                dve.scalar_tensor_tensor(out=tmp[5], in0=tmp[3], scalar=0.25, in1=tmp[4], op0=ALU.mult,
                                         op1=ALU.add).then_inc(ln_var, 1)
                dve.wait_ge(ln_sqrt, n)
                link(dve.reciprocal(ln_rstd[:], ln_std[:]))

            def lo_of(dst, src, scale, hi, ready, n, done):
                dve.wait_ge(ready, n)
                dve.scalar_tensor_tensor(out=dst, in0=src, scalar=scale, in1=hi, op0=ALU.mult, op1=ALU.subtract
                                         ).then_inc(done, 1)

            def job_adds(n):
                j, slot = jobs[n], n % 2
                dve.wait_ge(pst_in[slot], 32 * (n // 2 + 1))
                li = lora_jobs.index(j)
                for u in range(4):
                    rows = P if u < 2 or j in ("q", "o") else CDR
                    dve.wait_ge(lora_mm, 4 * li + u + 1)
                    piece = pstage[0:rows, slot, u * 512:u * 512 + 512]
                    dve.tensor_tensor(piece, ps_s[0:rows, (4 * li + u) % 3, :], piece, ALU.add
                                      ).then_inc(lora_add, 1)

            def job_lo(n):
                j, slot = jobs[n], n % 2
                dve.wait_ge(w_hi, n + 1)
                for rows, lo, hi in job_parts(j):
                    last = dve.scalar_tensor_tensor(
                        out=dst_flat(j, 1)[0:rows, lo:hi], in0=pstage[0:rows, slot, lo:hi], scalar=WSCALE,
                        in1=dst_flat(j, 0)[0:rows, lo:hi], op0=ALU.mult, op1=ALU.subtract)
                last.then_inc(w_split, 1)

            dve.memset(hold[:], 0.0).then_inc(slots, 1)
            dve.memset(gap[:], 0.0).then_inc(row_lo, 1)
            for w in (wk_s, wv_s, kipaw, vipaw, ctx_s):
                for part in (0, 1):
                    last = dve.memset(w[CDR:P, part, 1, :].bitcast(F32), 0.0)
            last.then_inc(rows_zeroed, 1)
            dve.wait_ge(lora_in, 16 * 12)
            for n, j in enumerate(lora_jobs):
                link(dve.tensor_scalar(downs[j], downs[j], alphas[:, n:n + 1], 1.0 / RANK, ALU.mult, ALU.mult))
            dve.wait_ge(ln_link, 4)
            dve.memset(ln_tmp[0:1, 0, 0:1], 0.0).then_inc(downs_ok, 1)
            job_adds(0)
            job_lo(0)
            job_adds(1)
            job_lo(1)
            for c in range(4):
                dve.wait_ge(x_in[c], 16)
                with dve.Fori(8 * c, 8 * c + 8) as t:
                    dve.bn_stats(stats[:, bass.ds(t, 1), :].rearrange("p t s -> p (t s)"),
                                 x_sb[:, bass.ds(t, 1), :].rearrange("p t d -> p (t d)")).then_inc(st_done, 1)
            dve.wait_ge(st_done, TILES)
            layer_stats(1)

            def normalise_x(b):
                for t in range(TPB):
                    tile = b * TPB + t
                    last = dve.tensor_scalar(
                        xn[:, t, :], x_sb[:, bass.ds(tile, 1), :].rearrange("p t d -> p (t d)"),
                        ln_mean[:, bass.ds(tile, 1)], ln_rstd[:, bass.ds(tile, 1)], ALU.subtract, ALU.mult)
                last.then_inc(xn_done, 1)

            normalise_x(0)
            for kk, rows in enumerate((P, CDR)):
                lo_of(ctx_s[0:rows, 1, kk, :], cstage[0:rows, 0:BATCH * CTX], 1.0, ctx_s[0:rows, 0, kk, :],
                      c_hi, kk + 1, c_split)
            for n in range(2, 6):
                if jobs[n] in lora_jobs:
                    job_adds(n)
                job_lo(n)
                if n == 3:
                    dve.wait_ge(ipa_hi, 1)
                    dve.scalar_tensor_tensor(
                        out=kipa_s[:, 1].rearrange("p m b i -> p (m b i)"), in0=ps_s[:, 0, :], scalar=1 / WSCALE,
                        in1=kipa_s[:, 0].rearrange("p m b i -> p (m b i)"), op0=ALU.mult, op1=ALU.subtract
                    ).then_inc(ipa_split, 2)
                if n == 4:
                    dve.wait_ge(ipa_hi, 2)
                    dve.scalar_tensor_tensor(
                        out=vipa_s[:, 1, :], in0=ps_s[0:BATCH * IPA, 1:3, :].rearrange("p c n -> p (c n)"),
                        scalar=1 / WSCALE, in1=vipa_s[:, 0, :], op0=ALU.mult, op1=ALU.subtract
                    ).then_inc(ipa_split, 2)

            def xt(b):
                lo_of(xt_s[:, 1].rearrange("p k n -> p (k n)"), ps_b[:, 1, :], 1.0,
                      xt_s[:, 0].rearrange("p k n -> p (k n)"), xt_hi, b + 1, xt_split)

            def q(b, k):
                lo_of(q_s[:, 1, 2 * k:2 * k + 2, :].rearrange("p m n -> p (m n)"), ps_a[:, k % 3, :], 1 / WSCALE,
                      q_s[:, 0, 2 * k:2 * k + 2, :].rearrange("p m n -> p (m n)"), q_hi, 4 * b + k + 1, q_split)

            def k_(b, k):
                dve.wait_ge(k_hi, 2 * b + k + 1)
                for half in (0, 1):
                    o = half * DH
                    last = dve.scalar_tensor_tensor(
                        out=kbd[o:o + DH, 1, 4 * k:4 * k + 4, half * CTX:half * CTX + ORG],
                        in0=ps_b[o:o + DH, 1 - k, 0:4 * ORG].rearrange("p (m j) -> p m j", m=4), scalar=1 / WSCALE,
                        in1=kbd[o:o + DH, 0, 4 * k:4 * k + 4, half * CTX:half * CTX + ORG], op0=ALU.mult,
                        op1=ALU.subtract)
                last.then_inc(k_split, 1)

            def v(b, k):
                lo_of(v_s[0:ORG, 1, k * 512:k * 512 + 512], ps_b[0:ORG, 1 - k, :], 1 / WSCALE,
                      v_s[0:ORG, 0, k * 512:k * 512 + 512], v_hi, 2 * b + k + 1, v_split)

            def keys(t):
                vw = prob[:, t, :].rearrange("p (h j) -> p h j", j=CTX)
                return [(vw[:, :, 0:ORG], 0), (vw[:, :, ORG:CTX], 1)]

            def maxima(b, t):
                dve.wait_ge(s_copied, 2 * b + t + 1)
                for vw, w in keys(t):
                    last = dve.tensor_reduce(mx[:, t, w, :], vw, AX, ALU.max)
                last.then_inc(mx_done, 1)

            def sums(b, t):
                dve.wait_ge(exp_done, 2 * b + t + 1)
                for vw, w in keys(t):
                    last = dve.tensor_reduce(sm[:, t, w, :], vw, AX, ALU.add)
                last.then_inc(sum_done, 1)
                dve.wait_ge(sum_done, 2 * b + t + 1)
                dve.reciprocal(rc[:, t], sm[:, t]).then_inc(rc_done, 1)

            def pt(b, k):
                t, h = k // 4, HPB * (k % 4)
                lo_of(pt_s[0:CTX, 1, h:h + HPB, t * P:t * P + P],
                      probs_bank(k)[0:CTX, :].rearrange("p (h n) -> p h n", h=HPB), PSCALE,
                      pt_s[0:CTX, 0, h:h + HPB, t * P:t * P + P], pt_hi, 8 * b + k + 1, pt_split)

            def ot(b, k):
                lo_of(ot_s[:, 1, 2 * k:2 * k + 2, :].rearrange("p m n -> p (m n)"), ps_b[:, (k + 1) % 2, :],
                      1 / (PSCALE), ot_s[:, 0, 2 * k:2 * k + 2, :].rearrange("p m n -> p (m n)"), ot_hi,
                      4 * b + k + 1, ot_split)

            def residual(b):
                dve.wait_ge(wo_mm, b + 1)
                dve.wait_ge(bo_added, b + 1)
                xb = x_sb[:, bass.ds(b * TPB, TPB), :].rearrange("p t d -> p (t d)")
                dve.scalar_tensor_tensor(out=xb, in0=ps_b[:, 0, :], scalar=1 / WSCALE, in1=xb, op0=ALU.mult,
                                         op1=ALU.add).then_inc(x1_done, 1)
                dve.wait_ge(x1_done, b + 1)
                dve.memset(hold[:], 0.0)
                for t in range(TPB):
                    tile = b * TPB + t
                    last = dve.bn_stats(st2[:, t, :], x_sb[:, bass.ds(tile, 1), :].rearrange("p t d -> p (t d)"))
                last.then_inc(st2_done, 1)
                dve.wait_ge(st2_done, b + 1)
                dve.memset(hold[:], 0.0)
                for t in range(TPB):
                    last = dve.bn_aggr(ln2[:, t, :], st2[:, t, :])
                last.then_inc(ag2_done, 1)
                dve.wait_ge(ag2_done, b + 1)
                dve.tensor_scalar(ln2_s[:, 0, :], ln2[:, :, 1], LN_EPS, None, ALU.add).then_inc(var2, 1)

            def normalise_2(b):
                dve.wait_ge(std2, b + 1)
                dve.reciprocal(ln2_s[:, 2, :], ln2_s[:, 1, :]).then_inc(rstd2, 1)
                dve.wait_ge(rstd2, b + 1)
                for t in range(TPB):
                    last = dve.tensor_scalar(
                        x2n[:, t, :], x_sb[:, bass.ds(b * TPB + t, 1), :].rearrange("p t d -> p (t d)"),
                        ln2[:, t, 0:1], ln2_s[:, 2, t:t + 1], ALU.subtract, ALU.mult)
                last.then_inc(x2n_done, 1)

            class Chain:

                def __init__(self, b, per):
                    self.b, self.per, self.n = b, per, 0

                def step(self, ins):
                    self.n += 1
                    ins.then_inc(route, 1)
                    dve.wait_ge(route, self.b * self.per + self.n)

            ROUTE = 14

            def pick_experts(b):
                c = Chain(b, ROUTE)
                dve.wait_ge(lg_mm, b + 1)
                c.step(dve.tensor_copy(lg[:].rearrange("p t e -> p (t e)"), ps_s[:, 2, 320:320 + TPB * EXPERTS]))
                dve.memset(hold[:], 0.0)
                for t in range(TPB):
                    last = dve.max(top[:, t, :], lg[:, t, :])
                c.step(last)
                dve.tensor_tensor(gap[:], top[:, :, 1], top[:, :, 0], ALU.subtract).then_inc(gap_done, 1)
                for t in range(TPB):
                    last = dve.max_index(top_i[:, t, :], top[:, t, :], lg[:, t, :])
                c.step(last)
                c.step(dve.tensor_copy(top_f[:], top_i[:]))
                io = iota8[:].unsqueeze(1).to_broadcast([P, TPB, EXPERTS])
                for pick in range(TOPK):
                    last = dve.tensor_tensor(
                        picks[:, pick], io, top_f[:, :, pick:pick + 1].to_broadcast([P, TPB, EXPERTS]), ALU.is_equal)
                c.step(last)
                dve.tensor_tensor(both[:], picks[:, 0], picks[:, 1], ALU.add).then_inc(both_done, 1)
                return c

            def weigh_and_place(b, c):
                dve.wait_ge(gap_expd, b + 1)
                c.step(dve.tensor_scalar(w_sum[:], gap_exp[:], 1.0, None, ALU.add))
                meta = row[:, :, META:META + 8].bitcast(F32)
                dve.wait_ge(scattered, 64 * b + 16)
                c.step(dve.reciprocal(w_a[:], w_sum[:]))
                c.step(dve.tensor_tensor(meta[:, :, 3], w_a[:], gap_exp[:], ALU.mult))
                dve.tensor_tensor(meta[:, :, 2], w_a[:], meta[:, :, 3], ALU.subtract)
                dve.tensor_copy(meta[:, :, 1], top_f[:, :, 0])
                dve.tensor_copy(row[:, :, META:META + 8].bitcast(I32)[:, :, 0], tok[:, bass.ds(b * TPB, TPB)]
                                ).then_inc(row_meta, 1)
                dve.wait_ge(rank_mm, b + 1)
                rank = ps_s[:, 2, 352:352 + TPB * EXPERTS].rearrange("p (t e) -> p t e", t=TPB)
                base = counts[:].unsqueeze(1).to_broadcast([P, TPB, EXPERTS])
                c.step(dve.tensor_tensor(place[:], rank, base, ALU.add))
                c.step(dve.tensor_tensor(place[:], place[:], reg0[:].unsqueeze(1).to_broadcast([P, TPB, EXPERTS]),
                                         ALU.add))
                c.step(dve.tensor_tensor(counts[:], ps_s[:, 2, 368:368 + EXPERTS], counts[:], ALU.add))
                for pick in range(TOPK):
                    last = dve.tensor_tensor(picked[:, pick], picks[:, pick], place[:], ALU.mult)
                c.step(last)
                c.step(dve.tensor_reduce(slot_f[:].rearrange("p k t -> p (k t)"),
                                         picked[:].rearrange("p k t e -> p (k t) e"), AX, ALU.add))
                dve.tensor_copy(slot_i[:], slot_f[:]).then_inc(slots, 1)
                c.step(dve.memset(hold[:], 0.0))
                assert c.n == ROUTE, c.n

            def body(b, first, last, x_left):
                maxima(b, 0)
                if not last:
                    xt(b + 1)
                maxima(b, 1)
                sums(b, 0)
                if not first:
                    residual(b - 1)
                if not last:
                    q(b + 1, 0)
                    q(b + 1, 1)
                sums(b, 1)
                if not first:
                    normalise_2(b - 1)
                if not last:
                    q(b + 1, 2)
                pt(b, 0)
                pt(b, 1)
                if not last:
                    q(b + 1, 3)
                pt(b, 2)
                pt(b, 3)
                if not last:
                    k_(b + 1, 0)
                    k_(b + 1, 1)
                if not first:
                    chain = pick_experts(b - 1)
                for k in range(4, 8):
                    pt(b, k)
                dve.wait_ge(fw_hi, b + 1)
                fw = [ffnw[:, part, bass.ds(b, 1), :].rearrange("p e n -> p (e n)") for part in (0, 1)]
                dve.scalar_tensor_tensor(out=fw[1], in0=wstage[:], scalar=WSCALE, in1=fw[0], op0=ALU.mult,
                                         op1=ALU.subtract).then_inc(fw_split, 1)
                if not first:
                    weigh_and_place(b - 1, chain)
                if x_left:
                    dve.wait_ge(row_lo, b + 1)
                    normalise_x(b + 2)
                for k in range(4):
                    ot(b, k)
                if not last:
                    v(b + 1, 0)
                    v(b + 1, 1)

            dve.wait_ge(w_split, 6)
            dve.memset(pt_s[DH:P].rearrange("p a h n -> p (a h n)").bitcast(F32), 0.0).then_inc(pt_zeroed, 1)
            xt(0)
            k_(0, 0)
            k_(0, 1)
            normalise_x(1)
            for k in range(4):
                q(0, k)
            v(0, 0)
            v(0, 1)
            body(0, True, False, True)
            with dve.Fori(1, BATCH - 2) as b:
                body(b, False, False, True)
            body(BATCH - 2, False, False, False)
            body(BATCH - 1, False, True, False)
            residual(BATCH - 1)
            normalise_2(BATCH - 1)
            weigh_and_place(BATCH - 1, pick_experts(BATCH - 1))
            ffn_dve(dve)

        THREE = ((0, 0), (0, 1), (1, 0))

        @block.tensor
        def _(pe):
            def product(o, lhs, rhs, terms):
                steps = [(n, a, c) for n in range(terms) for a, c in THREE]
                for i, (n, a, c) in enumerate(steps):
                    last = pe.matmul(o, lhs(a, n), rhs(c, n), start=(i == 0), stop=(i == len(steps) - 1))
                return last

            def lora_products(j):
                li = lora_jobs.index(j)
                for u in range(4):
                    if 4 * li + u >= 3:
                        pe.wait_ge(lora_add, 4 * li + u - 2)
                    bank = (4 * li + u) % 3
                    if j == "o":
                        for c in (0, 1):
                            p = 2 * u + c
                            last = pe.matmul(ps_s[:, bank, c * DM:c * DM + DM], downs[j][:, p * P:p * P + P], ups[j],
                                             start=True, stop=True)
                    else:
                        kk, n = u // 2, u % 2
                        rows = P if kk == 0 or j == "q" else CDR
                        last = pe.matmul(ps_s[0:rows, bank, :], downs[j][:, kk * P:kk * P + rows],
                                         ups[j][:, n * 512:n * 512 + 512], start=True, stop=True)
                    last.then_inc(lora_mm, 1)

            def transpose_x(b):
                pe.wait_ge(xn_done, b + 1)
                for kk in range(KD):
                    for t in range(TPB):
                        c = kk * SEQ + t * P
                        last = pe.transpose(ps_b[:, 1, c:c + P], xn[:, t, kk * P:kk * P + P], ident[:])
                last.then_inc(xt_mm, 1)

            def queries(b, k):
                for m in (2 * k, 2 * k + 1):
                    o = (m % 2) * SEQ
                    last = product(ps_a[:, k % 3, o:o + SEQ], lambda a, n: wq_s[:, a, n, m * P:m * P + P],
                                   lambda a, n: xt_s[:, a, n, :], KD)
                last.then_inc(q_mm, 1)

            def context(part, kk, b):
                return ctx_s[:, part, kk, bass.ds(b * ORG, ORG)]

            def new_keys(b, k):
                for m in range(4 * k, 4 * k + 4):
                    o = (m % 4) * ORG
                    last = product(ps_b[:, 1 - k, o:o + ORG], lambda a, n: wk_s[:, a, n, m * P:m * P + P],
                                   lambda a, n: context(a, n, b), KD)
                last.then_inc(k_mm, 1)

            def new_values(b, k):
                product(ps_b[0:ORG, 1 - k, :], lambda a, n: context(a, n, b),
                        lambda a, n: wv_s[:, a, n, k * 512:k * 512 + 512], KD).then_inc(v_mm, 1)

            def scores(b, t):
                pe.wait_ge(s_copied, 2 * b + t)
                if t == 0:
                    pe.wait_ge(q_split, 4 * b + 4)
                    pe.wait_ge(k_split, 2 * b + 2)
                    pe.wait_ge(kipa_put, b + 1)
                for p in range(PAIRS):
                    o = (p % 3) * 2 * CTX
                    last = product(ps_s[:, p // 3, o:o + 2 * CTX], lambda a, n: q_s[:, a, p, t * P:t * P + P],
                                   lambda a, n: kbd[:, a, p, :], 1)
                last.then_inc(s_mm, 1)

            def transpose_probs(b, k):
                t, h = k // 4, HPB * (k % 4)
                if k % 4 == 0:
                    pe.wait_ge(p_ready, 2 * b + t + 1)
                for c in range(HPB):
                    last = pe.transpose(probs_bank(k)[0:CTX, c * P:c * P + P],
                                        prob[:, t, (h + c) * CTX:(h + c + 1) * CTX], ident[:])
                last.then_inc(t_mm, 1)

            def attend(b, k):
                for p in (2 * k, 2 * k + 1):
                    o = (p % 2) * SEQ
                    for i, (a, c) in enumerate(THREE):
                        for half in (0, 1):
                            h = 2 * p + half
                            last = pe.matmul(ps_b[half * DH:half * DH + DH, (k + 1) % 2, o:o + SEQ],
                                             v_s[:, a, h * DH:h * DH + DH], pt_s[:, c, h, :],
                                             start=(i == 0), stop=(i == 2))
                last.then_inc(pv_mm, 1)

            def project(b, t):
                pe.wait_ge(ot_split, 4 * b + 4)
                last = product(ps_b[:, 0, t * DM:t * DM + DM], lambda a, n: ot_s[:, a, n, t * P:t * P + P],
                               lambda a, n: wo_s[:, a, n, :], PAIRS)
                if t == TPB - 1:
                    last.then_inc(wo_mm, 1)

            pe.wait_ge(consts, 3)
            pe.wait_ge(consts2, 11)
            pe.wait_ge(downs_ok, 1)
            lora_products("q")
            lora_products("k")
            transpose_x(0)
            lora_products("v")
            pe.wait_ge(rows_zeroed, 1)
            pe.wait_ge(c_split, 2)
            pe.wait_ge(w_split, 4)
            pe.wait_ge(lora_add, 12)
            for m in range(PAIRS):
                last = product(ps_s[:, 0, m * 64:m * 64 + 64], lambda a, n: kipaw[:, a, n, m * P:m * P + P],
                               lambda a, n: ctx_s[:, a, n, BATCH * ORG:BATCH * CTX], KD)
            last.then_inc(ipa_mm, 1)
            pe.wait_ge(w_split, 5)
            for c in (0, 1):
                last = product(ps_s[0:BATCH * IPA, 1 + c, :], lambda a, n: ctx_s[:, a, n, BATCH * ORG:BATCH * CTX],
                               lambda a, n: vipaw[:, a, n, c * 512:c * 512 + 512], KD)
            last.then_inc(ipa_mm, 1)
            pe.wait_ge(ipa_split, 4)
            lora_products("o")
            pe.wait_ge(xt_split, 1)
            new_keys(0, 0)
            new_keys(0, 1)
            for k in range(4):
                if k == 3:
                    pe.wait_ge(q_split, 1)
                queries(0, k)
            pe.wait_ge(k_split, 1)
            new_values(0, 0)
            pe.wait_ge(k_split, 2)
            new_values(0, 1)
            pe.wait_ge(w_split, 6)
            pe.wait_ge(lora_add, 16)
            pe.wait_ge(pt_zeroed, 1)

            def transpose_2(b):
                pe.wait_ge(x2n_done, b + 1)
                for kk in range(KD):
                    for t in range(TPB):
                        c = kk * SEQ + t * P
                        last = pe.transpose(ps_b[:, 0, c:c + P], x2n[:, t, kk * P:kk * P + P], ident[:])
                last.then_inc(x2_mm, 1)

            def router(b):
                pe.wait_ge(x2_copied, b + 1)
                for t in range(TPB):
                    c = 320 + t * EXPERTS
                    for kk in range(KD):
                        last = pe.matmul(ps_s[:, 2, c:c + EXPERTS], x2t[:, kk, t * P:t * P + P], gate_f[:, kk, :],
                                         start=(kk == 0), stop=(kk == KD - 1))
                last.then_inc(lg_mm, 1)

            def rank(b):
                pe.wait_ge(both_done, b + 1)
                bank = ps_s[:, 2, :]
                pe.matmul(bank[:, 352:360], before[:], both[:, 0, :], start=True, stop=True)
                pe.matmul(bank[:, 360:368], before[:], both[:, 1, :], start=True, stop=False)
                pe.matmul(bank[:, 360:368], ones[:], both[:, 0, :], start=False, stop=True)
                pe.matmul(bank[:, 368:376], ones[:], both[:, 0, :], start=True, stop=False)
                pe.matmul(bank[:, 368:376], ones[:], both[:, 1, :], start=False, stop=True).then_inc(rank_mm, 1)

            def body(b, first, last):
                if not first:
                    pe.wait_ge(slots, b)
                scores(b, 0)
                if not last:
                    pe.wait_ge(v_split, 2 * b + 1)
                    transpose_x(b + 1)
                if not first:
                    pe.wait_ge(v_split, 2 * b + 2)
                    project(b - 1, 0)
                scores(b, 1)
                if not first:
                    project(b - 1, 1)
                if not last:
                    pe.wait_ge(xt_split, b + 2)
                    pe.wait_ge(pt_split, 8 * b)
                    queries(b + 1, 0)
                    queries(b + 1, 1)
                    queries(b + 1, 2)
                else:
                    pe.wait_ge(pt_split, 8 * b)
                pe.wait_ge(s_copied, 2 * b + 2)
                transpose_probs(b, 0)
                transpose_probs(b, 1)
                if not last:
                    pe.wait_ge(q_split, 4 * b + 5)
                    queries(b + 1, 3)
                    pe.wait_ge(q_split, 4 * b + 6)
                transpose_probs(b, 2)
                if not last:
                    pe.wait_ge(q_split, 4 * b + 7)
                transpose_probs(b, 3)
                if not first:
                    transpose_2(b - 1)
                if not last:
                    new_keys(b + 1, 0)
                if not first:
                    router(b - 1)
                if not last:
                    if first:
                        pe.wait_ge(v_split, 2)
                    new_keys(b + 1, 1)
                    pe.wait_ge(q_split, 4 * b + 8)
                for k in range(4, 8):
                    if k >= 5:
                        pe.wait_ge(pt_split, 8 * b + k - 4)
                    transpose_probs(b, k)
                if not first:
                    rank(b - 1)
                pe.wait_ge(pt_split, 8 * b + 8)
                pe.wait_ge(v_split, 2 * b + 2)
                pe.wait_ge(vipa_in, 16 * b + 16)
                for k in range(4):
                    if k >= 2:
                        pe.wait_ge(ot_split, 4 * b + k - 1)
                    elif not last:
                        pe.wait_ge(k_split, 2 * b + 3 + k)
                    attend(b, k)
                if not last:
                    for k in (0, 1):
                        pe.wait_ge(ot_split, 4 * b + 3 + k)
                        new_values(b + 1, k)

            body(0, True, False)
            with pe.Fori(1, BATCH - 1) as b:
                body(b, False, False)
            body(BATCH - 1, False, True)
            for t in range(TPB):
                project(BATCH - 1, t)
            transpose_2(BATCH - 1)
            router(BATCH - 1)
            rank(BATCH - 1)
            ffn_pe(pe, product)



def kernel(**inputs):
    import numpy as _np
    import concourse.bacc as _bacc
    from concourse.bass_utils import run_bass_kernel_spmd as _run

    i = {n.replace("L0_xattn_", "").replace("L0_ffn_", ""): _np.asarray(a) for n, a in inputs.items()}
    c = i["ctx_768"]
    ctx_t = _np.concatenate([c[:, :ORG].reshape(-1, CD), c[:, ORG:].reshape(-1, CD)]).T
    w1 = i["w1"].reshape(EXPERTS, KD, P, DFF).transpose(0, 2, 1, 3).reshape(EXPERTS, 1, P, FW)
    w2 = i["w2"].reshape(EXPERTS, DFF // P, P, DM).transpose(0, 2, 1, 3).reshape(EXPERTS, 1, P, FW)
    ffn_w = _np.concatenate([w1, w2], axis=1).reshape(2 * EXPERTS, P, FW)
    laid = {
        "x": i["x"], "ctx_t": ctx_t, "wq": i["Wq"], "wk": i["Wk"], "wv": i["Wv"], "wo": i["Wo"], "bo": i["bo"],
        "q_down_t": i["q_down"].T, "q_up": i["q_up"], "q_alpha": i["q_alpha"],
        "k_down_t": i["k_down"].T, "k_up": i["k_up"], "k_alpha": i["k_alpha"],
        "v_down_t": i["v_down"].T, "v_up": i["v_up"], "v_alpha": i["v_alpha"],
        "o_down_t": i["o_down"].T, "o_up": i["o_up"], "o_alpha": i["o_alpha"],
        "wk_ipa": i["Wk_ipa"], "wv_ipa": i["Wv_ipa"], "gate_w": i["gate_w"], "ffn_w": ffn_w,
    }
    nc = _bacc.Bacc("TRN2", target_bir_lowering=False, num_devices=1)
    arrays, args = {}, {}
    for name, a in laid.items():
        a = _np.ascontiguousarray(a)
        arrays[f"in_{name}"] = a
        args[name] = nc.dram_tensor(f"in_{name}", a.shape, mybir.dt.from_np(a.dtype), kind="ExternalInput").ap()
    args["out"] = nc.dram_tensor("out_x", (BATCH, SEQ, DM), F32, kind="ExternalOutput").ap()
    build(nc, **args)
    return _run(nc, [arrays], core_ids=[0]).results[0]["out_x"]
```

```python
from contextlib import ExitStack

import concourse.bass as bass
from concourse import mybir

F32 = mybir.dt.float32
F16 = mybir.dt.float16
U32 = mybir.dt.uint32
I32 = mybir.dt.int32
ALU = mybir.AluOpType
ACT = mybir.ActivationFunctionType
AX = mybir.AxisListType.X

P = 128
BATCH, SEQ, DM = 16, 256, 256
HEADS, DH = 16, 64
ID = HEADS * DH
CD, CTX, IPA = 192, 77, 4
ORG = CTX - IPA
RANK = 32
EXPERTS, DFF = 8, 512
PAIRS = HEADS // 2
KD = DM // P
CDR = CD - P
TILES = BATCH * SEQ // P
TPB = SEQ // P
KEYS = HEADS * CTX
WSCALE = 64.0
PSCALE = 64.0
LN_EPS = 1e-5
HPB = 4
FW = 1024
TOKENS = BATCH * SEQ
TOPK = 2
FT = DFF // P
RT = 256
SUB = RT // P
NT = (TOPK * TOKENS + EXPERTS * (RT - 1)) // RT
REGION = TOKENS + RT
ROW = 2 * DM + 8 + 8
META = 2 * DM
UNROLL = 4


def build(nc, x, ctx_t, wq, wk, wv, wo, bo, q_down_t, q_up, q_alpha, k_down_t, k_up, k_alpha,
          v_down_t, v_up, v_alpha, o_down_t, o_up, o_alpha, wk_ipa, wv_ipa, gate_w, ffn_w, out):
    stack = ExitStack()
    with stack:
        def sb(name, shape, dt):
            return stack.enter_context(nc.sbuf_tensor(name, shape, dt))

        def sem(name):
            return stack.enter_context(nc.semaphore(name))

        x_sb = sb("x_sb", [P, TILES, DM], F32)
        ffnw = sb("ffnw", [P, 2, 2 * EXPERTS, FW], F16)
        wq_s = sb("wq_s", [P, 2, KD, ID], F16)
        wk_s = sb("wk_s", [P, 2, KD, ID], F16)
        wv_s = sb("wv_s", [P, 2, KD, ID], F16)
        wo_s = sb("wo_s", [P, 2, PAIRS, DM], F16)
        ctx_s = sb("ctx_s", [P, 2, KD, BATCH * CTX], F16)
        kipa_s = sb("kipa_s", [P, 2, PAIRS, BATCH, IPA], F16)
        kbd = sb("kbd", [P, 2, PAIRS, 2 * CTX], F16)
        v_s = sb("v_s", [P, 2, ID], F16)
        q_s = sb("q_s", [P, 2, PAIRS, SEQ], F16)
        xn = sb("xn", [P, TPB, DM], F32)
        xt_s = sb("xt_s", [P, 2, KD, SEQ], F16)
        prob = sb("prob", [P, TPB, KEYS], F32)
        pt_s = sb("pt_s", [P, 2, HEADS, SEQ], F16)
        ot_s = sb("ot_s", [P, 2, PAIRS, SEQ], F16)
        wstage = sb("wstage", [P, FW], F32)
        bo_sb = sb("bo_sb", [P, DM], F32)
        gate_f = sb("gate_f", [P, KD, EXPERTS], F32)
        ident = sb("ident", [P, P], F32)
        iota8 = sb("iota8", [P, EXPERTS], F32)
        alphas = sb("alphas", [RANK, 4], F32)
        ln_mean = sb("ln_mean", [P, TILES], F32)
        ln_std = sb("ln_std", [P, TILES], F32)
        ln_rstd = sb("ln_rstd", [P, TILES], F32)
        mx = sb("mx", [P, TPB, 2, HEADS], F32)
        sm = sb("sm", [P, TPB, 2, HEADS], F32)
        rc = sb("rc", [P, TPB, 2, HEADS], F32)

        pt_stage = pt_s[:].rearrange("p a h n -> p (a h n)").bitcast(F32).rearrange("p (s n) -> p s n", s=2)
        prob_flat = prob[:].rearrange("p t n -> p (t n)")
        stage = [pt_stage[:, 0, :], pt_stage[:, 1, :], prob_flat[:, 12 * TILES:12 * TILES + 2048],
                 q_s[:].rearrange("p a m n -> p (a m n)").bitcast(F32)]
        cstage = (ot_s[:].rearrange("p a m n -> p (a m n)").bitcast(F32),
                  kbd[:].rearrange("p a m j -> p (a m j)").bitcast(F32))
        stats = prob_flat[:, 0:6 * TILES].rearrange("p (t s) -> p t s", s=6)
        ln_tmp = prob_flat[:, 6 * TILES:12 * TILES].rearrange("p (s t) -> p s t", s=6)
        early = ffnw[:, :, :, :].rearrange("p a e n -> p (a e n)")
        kipaw = early[:, 0:4096].rearrange("p (a k n) -> p a k n", a=2, k=KD)
        vipaw = early[:, 4096:8192].rearrange("p (a k n) -> p a k n", a=2, k=KD)
        vipa_s = early[0:BATCH * IPA, 8192:8192 + 2 * ID].rearrange("p (a n) -> p a n", a=2)
        lora = early[0:RANK, 12288:12288 + 2 * 9216].bitcast(F32)
        ups = {"q": lora[:, 0:1024], "k": lora[:, 1024:2048], "v": lora[:, 2048:3072], "o": lora[:, 3072:3328]}
        downs = {"q": lora[:, 3328:3584], "k": lora[:, 3584:3776], "v": lora[:, 3776:3968],
                 "o": lora[:, 3968:4992]}

        hold = sb("hold", [P, 1], F32)
        hold_p = sb("hold_p", [P, 2], F32)
        ident_h = sb("ident_h", [P, P], F16)
        before = sb("before", [P, P], F16)
        ones = sb("ones", [P, P], F16)
        ln2 = sb("ln2", [P, TPB, 2], F32)
        ln2_s = sb("ln2_s", [P, 3, TPB], F32)
        st2 = sb("st2", [P, TPB, 6], F32)
        x2n = xn
        x2t = sb("x2t", [P, KD, SEQ], F32)
        row_words = sb("row_words", [P, TPB, ROW // 2], I32)
        row = row_words[:].bitcast(F16)
        tok = sb("tok", [P, TILES], I32)
        lg = sb("lg", [P, TPB, EXPERTS], F32)
        top = sb("top", [P, TPB, EXPERTS], F32)
        top_i = sb("top_i", [P, TPB, EXPERTS], U32)
        top_f = sb("top_f", [P, TPB, EXPERTS], F32)
        gap = sb("gap", [P, TPB], F32)
        gap_exp = sb("gap_exp", [P, TPB], F32)
        w_sum = sb("w_sum", [P, TPB], F32)
        w_a = sb("w_a", [P, TPB], F32)
        picks = sb("picks", [P, TOPK, TPB, EXPERTS], F32)
        both = sb("both", [P, TPB, EXPERTS], F16)
        place = sb("place", [P, TPB, EXPERTS], F32)
        picked = sb("picked", [P, TOPK, TPB, EXPERTS], F32)
        slot_f = sb("slot_f", [P, TOPK, TPB], F32)
        slot_i = sb("slot_i", [P, TOPK, TPB], I32)
        counts = sb("counts", [P, EXPERTS], F32)
        reg0 = sb("reg0", [P, EXPERTS], F32)
        steps_of = sb("steps_of", [P, TOKENS // RT], F32)
        tiles_e = sb("tiles_e", [P, EXPERTS], F32)
        zero8 = sb("zero8", [P, EXPERTS], F32)
        ends = sb("ends", [P, EXPERTS], F32)
        tnum = sb("tnum", [P, NT], F32)
        e_of = sb("e_of", [P, NT], F32)
        wt = sb("wt", [P, UNROLL, SUB], F32)
        token_of = sb("token_of", [P, UNROLL, SUB], I32)
        table = sb("table", [1, 2, NT], I32)
        pads = sb("pads", [1, EXPERTS], I32)

        ps_s = stack.enter_context(nc.psum_tensor("ps_s", [P, 3, 512], F32))
        ps_a = stack.enter_context(nc.psum_tensor("ps_a", [P, 3, 512], F32))
        ps_b = stack.enter_context(nc.psum_tensor("ps_b", [P, 2, 512], F32))

        rows_dram = nc.dram_tensor("rows_dram", (EXPERTS * REGION + RT, ROW // 2), I32, kind="Internal").ap()
        vipa_dram = nc.dram_tensor("vipa_dram", (BATCH, IPA, 2, ID), F16, kind="Internal").ap()

        x_in = [sem(f"x_in{c}") for c in range(4)]
        lora_in = [sem(f"lora_in_{j}") for j in "qkvo"]
        misc_in = sem("misc_in")
        ctx_in = [sem(f"ctx_in{k}") for k in range(2)]
        pst_in = [sem(f"pst_in{s}") for s in range(4)]
        consts = sem("consts")
        zeroed = sem("zeroed")
        rows_zeroed = sem("rows_zeroed")
        pt_zeroed = sem("pt_zeroed")
        downs_ok = sem("downs_ok")
        lora_mm = sem("lora_mm")
        lora_add = sem("lora_add")
        w_hi = sem("w_hi")
        w_split = sem("w_split")
        w_split_p = sem("w_split_p")
        w_scaled = sem("w_scaled")
        c_hi = sem("c_hi")
        c_split = sem("c_split")
        ipa_mm = sem("ipa_mm")
        ipa_hi = sem("ipa_hi")
        ipa_split = sem("ipa_split")
        vipa_out = sem("vipa_out")
        ln_link = sem("ln_link")
        ln_var = sem("ln_var")
        ln_sqrt = sem("ln_sqrt")
        xn_done = sem("xn_done")
        xt_mm = sem("xt_mm")
        xt_hi = sem("xt_hi")
        xt_split = sem("xt_split")
        q_mm = sem("q_mm")
        q_hi = sem("q_hi")
        q_split = sem("q_split")
        k_mm = sem("k_mm")
        k_hi = sem("k_hi")
        k_split = sem("k_split")
        kipa_put = sem("kipa_put")
        v_mm = sem("v_mm")
        v_hi = sem("v_hi")
        v_split = sem("v_split")
        vipa_in = sem("vipa_in")
        s_mm = sem("s_mm")
        s_copied = sem("s_copied")
        mx_done = sem("mx_done")
        shifted = sem("shifted")
        exp_done = sem("exp_done")
        sum_done = sem("sum_done")
        rc_done = sem("rc_done")
        p_ready = sem("p_ready")
        t_mm = sem("t_mm")
        pt_hi = sem("pt_hi")
        pt_split = sem("pt_split")
        pv_mm = sem("pv_mm")
        ot_hi = sem("ot_hi")
        ot_split = sem("ot_split")
        wo_mm = sem("wo_mm")
        bo_added = sem("bo_added")
        x1_done = sem("x1_done")
        st_done = sem("st_done")
        fw_in = sem("fw_in")
        shifted_half = sem("shifted_half")
        fw_scaled = sem("fw_scaled")
        fw_hi = sem("fw_hi")
        fw_split = sem("fw_split")

        st2_done = sem("st2_done")
        ag2_done = sem("ag2_done")
        var2 = sem("var2")
        std2 = sem("std2")
        rstd2 = sem("rstd2")
        x2n_done = sem("x2n_done")
        row_hi = sem("row_hi")
        row_lo = sem("row_lo")
        row_meta = sem("row_meta")
        x2_mm = sem("x2_mm")
        x2_copied = sem("x2_copied")
        lg_mm = sem("lg_mm")
        route = sem("route")
        gap_done = sem("gap_done")
        gap_expd = sem("gap_expd")
        both_done = sem("both_done")
        rank_mm = sem("rank_mm")
        slots = sem("slots")
        scattered = sem("scattered")
        acc_in = sem("acc_in")
        pad_in = sem("pad_in")
        pad_made = sem("pad_made")
        held = sem("held")
        tab = sem("tab")
        tab_done = sem("tab_done")
        tx_mm = sem("tx_mm")
        tx_copied = sem("tx_copied")
        h_mm = sem("h_mm")
        silu_done = sem("silu_done")
        h_hi = sem("h_hi")
        h_split = sem("h_split")
        wt_done = sem("wt_done")
        y_mm = sem("y_mm")
        y_done = sem("y_done")
        added = sem("added")
        consts2 = sem("consts2")
        tile_in = [sem(f"tile_in{n}") for n in range(UNROLL)]

        jobs = ["q", "k", "ki", "v", "vi", "o"]
        POOL_JOBS = [2, 4, 5]
        SLOTS = 4
        job_src = {"q": wq, "k": wk, "v": wv, "ki": wk_ipa, "vi": wv_ipa, "o": wo}
        job_dst = {"q": wq_s, "k": wk_s, "v": wv_s, "ki": kipaw, "vi": vipaw, "o": wo_s}
        lora_jobs = ["q", "k", "v", "o"]
        x_view = x.rearrange("b (t p) d -> p (b t) d", p=P)
        out_rows = out.rearrange("b n d -> (b n) d")

        def job_parts(j):
            if j in ("q", "o"):
                return [(P, 0, 2048)]
            return [(P, 0, 1024), (CDR, 1024, 2048)]

        def dst_flat(j, part):
            return job_dst[j][:, part].rearrange("p k n -> p (k n)")

        xg_words = prob[:].rearrange("p t n -> p (t n)").bitcast(I32)[:, 0:UNROLL * SUB * ROW // 2].rearrange(
            "p (s c n) -> p s c n", s=UNROLL, c=SUB)
        xg = prob[:].rearrange("p t n -> p (t n)").bitcast(F16)[:, 0:UNROLL * SUB * ROW].rearrange(
            "p (s c n) -> p s c n", s=UNROLL, c=SUB)
        q_flat = q_s[:].rearrange("p a m n -> p (a m n)")
        tx = q_flat[:, 0:2 * 2 * KD * RT].rearrange("p (s a k n) -> p s a k n", s=2, a=2, k=KD)
        h32 = q_flat[:, 2048:4096].bitcast(F32).rearrange("p (j n) -> p j n", j=2)
        hs = ot_s[:].rearrange("p a m n -> p (a m n)").rearrange("p (s a f n) -> p s a f n", s=2, a=2, f=FT)
        y_sb = pt_s[:].rearrange("p a h n -> p (a h n)").bitcast(F32)[:, 0:UNROLL * SUB * DM].rearrange(
            "p (s c n) -> p s c n", s=UNROLL, c=SUB)
        xn_flat = xn[:].rearrange("p t d -> p (t d)")
        past = xn_flat[:, 0:NT * EXPERTS].rearrange("p (t e) -> p t e", t=NT)
        ge = xn_flat[:, NT * EXPERTS:NT * EXPERTS + 128].rearrange("p (e n) -> p e n", e=EXPERTS)
        start_of = bo_sb[:, 0:NT]
        row_of = bo_sb[:, NT:2 * NT]
        past_n = x2t[:].rearrange("p k n -> p (k n)")[:, 0:NT * EXPERTS].rearrange("p (t e) -> p t e", t=NT)
        pad_rows = wstage[:].bitcast(I32)[:, 0:SUB * ROW // 2].rearrange("p (c n) -> p c n", c=SUB)
        tx_ps = [ps_s[:, s, :].bitcast(F16) for s in (0, 1)]

        def probs_bank(k):
            return (ps_s[:, 0, :], ps_s[:, 1, :], ps_a[:, 1, :], ps_a[:, 2, :], ps_a[:, 0, :])[k % 5]

        def heads_bank(k):
            return (ps_b[:, 1, :], ps_b[:, 0, :], ps_s[:, 0, :], ps_s[:, 1, :])[k]

        def h_ps(t, j):
            n = 2 * (t % 2) + j
            return ps_a[:, n, :] if n < 3 else ps_s[:, 2, :]

        def run_tiles(eng, step):
            for t in range(UNROLL):
                step(t, t)
            loops = (NT - UNROLL) // UNROLL
            with eng.Fori(1, loops) as i:
                for j in range(UNROLL):
                    step(i * UNROLL + j, j)
            for t in range(loops * UNROLL, NT):
                step(t, t)

        def fill_up(eng, experts):
            eng.wait_ge(pad_made, 4)
            eng.wait_ge(tab_done, 1)
            for e in experts:
                r = eng.value_load(pads[0:1, e:e + 1], min_val=0, max_val=EXPERTS * REGION - RT)
                eng.dma_start(rows_dram[bass.ds(r, RT), :].rearrange("(c p) n -> p c n", p=P), pad_rows
                              ).then_inc(pad_in, 16)

        def ffn_sp(sp):
            fill_up(sp, range(0, EXPERTS, 2))
            sp.wait_ge(tab_done, 2)
            sp.wait_ge(scattered, 16 + 16 * TOPK * TILES)
            sp.wait_ge(pad_in, 16 * EXPERTS)

            def load(t, slot):
                r = sp.value_load(table[0:1, 0, bass.ds(t, 1)], min_val=0, max_val=EXPERTS * REGION)
                sp.dma_start(xg_words[:, slot], rows_dram[bass.ds(r, RT), :].rearrange("(c p) n -> p c n", p=P)
                             ).then_inc(tile_in[slot], 16)

            def step(t, j):
                if isinstance(t, int) and t + UNROLL >= NT:
                    return
                sp.wait_ge(wt_done, 2 * t + 2)
                load(t + UNROLL, j % UNROLL)

            for t in range(UNROLL):
                load(t, t)
            run_tiles(sp, step)
            sp.wait_ge(added, 16 * SUB * NT)

        def ffn_pool(pool):
            pool.wait_ge(acc_in, 16 * BATCH)

            def step(t, j):
                pool.wait_ge(y_done, t + 1)
                if not (isinstance(t, int) and t == 0):
                    pool.wait_ge(added, 16 * SUB * t)
                    pool.wait_ge(held, t)
                pool.tensor_tensor(hold_p[:, 1:2], zero8[:, 0:1], zero8[:, 1:2], ALU.add).then_inc(held, 1)
                for c in range(SUB):
                    pool.indirect_dma_start(
                        out_rows, bass.IndirectOffsetOnAxis(ap=token_of[:, j % UNROLL, c:c + 1], axis=0),
                        y_sb[:, j % UNROLL, c, :], None, bounds_check=TOKENS - 1, oob_is_err=False,
                        compute_op=ALU.add).then_inc(added, 16)

            run_tiles(pool, step)

        def ffn_pe(pe, product):
            def weights_of(t):
                return pe.value_load(table[0:1, 1, bass.ds(t, 1)], min_val=0, max_val=EXPERTS - 1)

            def transposes(t, j):
                pe.wait_ge(tile_in[j % UNROLL], 16 * (t // UNROLL + 1) if isinstance(t, int) else tile_wait(t, j))
                if not (isinstance(t, int) and t < 2):
                    pe.wait_ge(tx_copied, t - 1)
                for part in (0, 1):
                    for kk in range(KD):
                        for c in range(SUB):
                            o = (part * KD + kk) * RT + c * P
                            s = part * DM + kk * P
                            last = pe.transpose(tx_ps[j % 2][:, o:o + P], xg[:, j % UNROLL, c, s:s + P], ident_h[:])
                last.then_inc(tx_mm, 1)

            def tile_wait(t, j):
                return (t - (j % UNROLL)) * (16 // UNROLL) + 16

            def hidden(t, j):
                e = weights_of(t)
                pe.wait_ge(tx_copied, t + 1)
                for half in (0, 1):
                    if not (isinstance(t, int) and t < 2):
                        pe.wait_ge(silu_done, 2 * t - 3 + half)
                    for m in (2 * half, 2 * half + 1):
                        o = (m % 2) * RT
                        last = product(h_ps(j, half)[:, o:o + RT],
                                       lambda a, n: ffnw[:, a, bass.ds(2 * e, 1), n * DFF + m * P:n * DFF + m * P + P]
                                       .rearrange("p e n -> p (e n)"),
                                       lambda a, n: tx[:, j % 2, a, n, :], KD)
                    last.then_inc(h_mm, 1)

            def down(t, j):
                e = weights_of(t)
                pe.wait_ge(h_split, 2 * t + 2)
                if not (isinstance(t, int) and t < 2):
                    pe.wait_ge(y_done, t - 1)
                for c in range(SUB):
                    last = product(ps_b[:, j % 2, c * DM:c * DM + DM],
                                   lambda a, n: hs[:, j % 2, a, n, c * P:c * P + P],
                                   lambda a, n: ffnw[:, a, bass.ds(2 * e + 1, 1), n * DM:n * DM + DM]
                                   .rearrange("p e n -> p (e n)"), FT)
                last.then_inc(y_mm, 1)

            def step(t, j):
                if not (isinstance(t, int) and t + 2 >= NT):
                    transposes(t + 2, j + 2)
                if not (isinstance(t, int) and t + 1 >= NT):
                    hidden(t + 1, j + 1)
                down(t, j)

            pe.wait_ge(fw_split, 2 * EXPERTS)
            pe.wait_ge(tab_done, 1)
            transposes(0, 0)
            transposes(1, 1)
            hidden(0, 0)
            run_tiles(pe, step)

        def ffn_act(act):
            def hidden(t, j):
                for half in (0, 1):
                    act.wait_ge(h_mm, 2 * t + half + 1)
                    if not (isinstance(t, int) and t < 1):
                        act.wait_ge(h_split, 2 * t - 1 + half)
                    act.activation(h32[:, half, :], h_ps(j, half), ACT.Silu, scale=1 / WSCALE).then_inc(silu_done, 1)
                    act.wait_ge(silu_done, 2 * t + half + 1)
                    if not (isinstance(t, int) and t < 2):
                        act.wait_ge(y_mm, t - 1)
                    act.activation(hs[:, j % 2, 0, 2 * half:2 * half + 2, :].rearrange("p f n -> p (f n)"),
                                   h32[:, half, :], ACT.Copy).then_inc(h_hi, 1)

            def step(t, j):
                if not (isinstance(t, int) and t + 1 >= NT):
                    hidden(t + 1, j + 1)

            fill_up(act, range(1, EXPERTS, 2))
            hidden(0, 0)
            run_tiles(act, step)

        def ffn_dve(dve):
            n = [0]

            def step_tab(ins):
                n[0] += 1
                ins.then_inc(tab, 1)
                dve.wait_ge(tab, n[0])

            dve.tensor_tensor(pads[:], reg0[0:1, :], counts[0:1, :], ALU.add).then_inc(tab_done, 1)
            dve.wait_ge(row_lo, BATCH + 1)
            step_tab(dve.tensor_tensor(ge, counts[:].unsqueeze(2).to_broadcast([P, EXPERTS, TOKENS // RT]),
                                       steps_of[:].unsqueeze(1).to_broadcast([P, EXPERTS, TOKENS // RT]), ALU.is_gt))
            step_tab(dve.tensor_reduce(tiles_e[:], ge, AX, ALU.add))
            step_tab(dve.tensor_tensor_scan(ends[:], tiles_e[:], zero8[:], 0.0, ALU.add, ALU.add))
            step_tab(dve.tensor_tensor(past, ends[:].unsqueeze(1).to_broadcast([P, NT, EXPERTS]),
                                       tnum[:].unsqueeze(2).to_broadcast([P, NT, EXPERTS]), ALU.is_le))
            step_tab(dve.tensor_reduce(e_of[:], past, AX, ALU.add))
            step_tab(dve.tensor_tensor(past_n, past, tiles_e[:].unsqueeze(1).to_broadcast([P, NT, EXPERTS]),
                                       ALU.mult))
            step_tab(dve.tensor_reduce(start_of, past_n, AX, ALU.add))
            step_tab(dve.tensor_tensor(row_of, tnum[:], start_of, ALU.subtract))
            step_tab(dve.tensor_scalar(row_of, row_of, float(RT), None, ALU.mult))
            step_tab(dve.scalar_tensor_tensor(out=row_of, in0=e_of[:], scalar=float(REGION), in1=row_of,
                                              op0=ALU.mult, op1=ALU.add))
            dve.tensor_scalar(table[:, 0, :], row_of[0:1, :], float(EXPERTS * REGION), None, ALU.min)
            dve.tensor_scalar(table[:, 1, :], e_of[0:1, :], float(EXPERTS - 1), None, ALU.min).then_inc(tab_done, 1)

            def rows_in(t, j):
                dve.wait_ge(tx_mm, t + 1)
                if not (isinstance(t, int) and t < 2):
                    dve.wait_ge(h_mm, 2 * t - 2)
                dve.tensor_copy(tx[:, j % 2].rearrange("p a k n -> p (a k n)"), tx_ps[j % 2]).then_inc(tx_copied, 1)
                if not (isinstance(t, int) and t < UNROLL):
                    dve.wait_ge(added, 16 * SUB * (t - UNROLL + 1))
                dve.tensor_copy(token_of[:, j % UNROLL, :], xg_words[:, j % UNROLL, :, META // 2])
                meta = xg[:, j % UNROLL, :, META:META + 8].bitcast(F32)
                dve.scalar_tensor_tensor(out=wt[:, j % UNROLL, :], in0=meta[:, :, 1], scalar=e_of[:, bass.ds(t, 1)],
                                         in1=meta[:, :, 2], op0=ALU.is_equal, op1=ALU.mult).then_inc(wt_done, 1)
                dve.wait_ge(wt_done, 2 * t + 1)
                dve.tensor_tensor(wt[:, j % UNROLL, :], wt[:, j % UNROLL, :], meta[:, :, 3], ALU.add
                                  ).then_inc(wt_done, 1)

            def low(t, j):
                for half in (0, 1):
                    dve.wait_ge(h_hi, 2 * t + half + 1)
                    dve.tensor_tensor(hs[:, j % 2, 1, 2 * half:2 * half + 2, :].rearrange("p f n -> p (f n)"),
                                      h32[:, half, :],
                                      hs[:, j % 2, 0, 2 * half:2 * half + 2, :].rearrange("p f n -> p (f n)"),
                                      ALU.subtract).then_inc(h_split, 1)

            def result(t, j):
                dve.wait_ge(y_mm, t + 1)
                dve.wait_ge(wt_done, 2 * t + 2)
                for c in range(SUB):
                    last = dve.tensor_scalar(y_sb[:, j % UNROLL, c, :], ps_b[:, j % 2, c * DM:c * DM + DM],
                                             wt[:, j % UNROLL, c:c + 1], 1 / WSCALE, ALU.mult, ALU.mult)
                last.then_inc(y_done, 1)

            def step(t, j):
                if not (isinstance(t, int) and t + 2 >= NT):
                    rows_in(t + 2, j + 2)
                if not (isinstance(t, int) and t + 1 >= NT):
                    low(t + 1, j + 1)
                result(t, j)

            rows_in(0, 0)
            rows_in(1, 1)
            low(0, 0)
            run_tiles(dve, step)

        block = stack.enter_context(nc.Block())

        @block.sync
        def _(sp):
            def load_lora(n, dn, up, alpha):
                j = lora_jobs[n]
                sp.dma_start(downs[j], dn).then_inc(lora_in[n], 16)
                sp.dma_start(alphas[:, n:n + 1], alpha.rearrange("(a b) -> a b", a=1).to_broadcast([RANK, 1])
                             ).then_inc(lora_in[n], 16)
                sp.dma_start(ups[j], up).then_inc(lora_in[n], 16)

            def load_job(n):
                j, slot = jobs[n], n % SLOTS
                if n >= SLOTS:
                    sp.wait_ge(w_split, n - SLOTS + 1)
                if j in ("q", "o"):
                    nk = KD if j == "q" else PAIRS
                    dst = stage[slot].rearrange("p (k n) -> p k n", k=nk)
                    src = job_src[j].rearrange("(k p) n -> p k n", p=P)
                    for c in (0, 1):
                        ks = slice(c * nk // 2, (c + 1) * nk // 2)
                        sp.dma_start(dst[:, ks], src[:, ks]).then_inc(pst_in[slot], 16)
                else:
                    sp.dma_start(stage[slot][:, 0:ID], job_src[j][0:P, :]).then_inc(pst_in[slot], 16)
                    sp.dma_start(stage[slot][0:CDR, ID:2 * ID], job_src[j][P:CD, :]).then_inc(pst_in[slot], 16)

            def load_x(c):
                sp.dma_start(x_sb[:, c * 8:c * 8 + 8, :], x_view[:, c * 8:c * 8 + 8, :]).then_inc(x_in[c], 16)

            load_lora(0, q_down_t, q_up, q_alpha)
            load_job(0)
            load_lora(1, k_down_t, k_up, k_alpha)
            load_job(1)
            load_lora(2, v_down_t, v_up, v_alpha)
            load_x(0)
            load_job(3)
            load_lora(3, o_down_t, o_up, o_alpha)
            load_x(1)
            for kk, rows in enumerate((P, CDR)):
                sp.dma_start(cstage[kk][0:rows, 0:BATCH * CTX], ctx_t[kk * P:kk * P + rows, :]
                             ).then_inc(ctx_in[kk], 16)
            load_x(2)
            load_job(2)
            load_x(3)
            sp.dma_start(bo_sb[:], bo.rearrange("(a n) -> a n", a=1).to_broadcast([P, DM])).then_inc(misc_in, 16)
            sp.dma_start(gate_f[:], gate_w.rearrange("(k p) e -> p k e", p=P)).then_inc(misc_in, 16)
            load_job(4)
            load_job(5)
            sp.wait_ge(ipa_split, 4)
            sp.dma_start(vipa_dram.rearrange("b i a n -> (b i) a n"), vipa_s).then_inc(vipa_out, 16)
            sp.wait_ge(vipa_out, 16)
            sp.wait_ge(zeroed, 2)
            sp.dma_start(v_s[ORG:CTX, :, :], vipa_dram[0]).then_inc(vipa_in, 16)

            def store_x1(b):
                sp.wait_ge(x1_done, b + 1)
                sp.dma_start(out_rows[bass.ds(b * SEQ, SEQ), :].rearrange("(t p) d -> p t d", p=P),
                             x_sb[:, bass.ds(b * TPB, TPB), :]).then_inc(acc_in, 16)

            def body(b, first, last):
                if not first:
                    sp.wait_ge(fw_split, b)
                else:
                    sp.wait_ge(ipa_split, 4)
                sp.dma_start(wstage[:], ffn_w[b]).then_inc(fw_in, 16)
                if not first:
                    store_x1(b - 1)
                if not last:
                    sp.wait_ge(pv_mm, 4 * b + 4)
                    sp.dma_start(v_s[ORG:CTX, :, :], vipa_dram[bass.ds(b + 1, 1)].rearrange("a i h n -> (a i) h n")
                                 ).then_inc(vipa_in, 16)

            body(0, True, False)
            with sp.Fori(1, BATCH - 1) as b:
                body(b, False, False)
            body(BATCH - 1, False, True)
            store_x1(BATCH - 1)
            ffn_sp(sp)

        @block.gpsimd
        def _(pool):
            pool.memset(ident[:], 0.0).then_inc(consts, 1)
            pool.iota(iota8[:], [[1, EXPERTS]], base=0, channel_multiplier=0,
                      allow_small_or_imprecise_dtypes=True).then_inc(consts, 1)
            pool.wait_ge(consts, 2)
            pool.affine_select(out=ident[:], in_=ident[:], compare_op=ALU.not_equal, fill=1.0, base=0,
                               pattern=[[-1, P]], channel_multiplier=1).then_inc(consts, 1)
            pool.memset(row_words[:], 0).then_inc(pad_made, 1)
            pool.wait_ge(pad_made, 1)
            pool.iota(row_words[:, :, META // 2:META // 2 + 1], [[0, SUB], [0, 1]], base=TOKENS,
                      channel_multiplier=0).then_inc(pad_made, 1)
            pool.wait_ge(pad_made, 2)
            pool.dma_start(rows_dram[EXPERTS * REGION:EXPERTS * REGION + RT, :].rearrange("(c p) n -> p c n", p=P),
                           row_words[:]).then_inc(scattered, 16)
            pool.memset(ident_h[:], 0.0).then_inc(consts2, 1)
            pool.memset(before[:], 0.0).then_inc(consts2, 1)
            pool.memset(ones[:], 1.0).then_inc(consts2, 1)
            pool.memset(counts[:], 0.0).then_inc(consts2, 1)
            pool.memset(zero8[:], 0.0).then_inc(consts2, 1)
            pool.iota(tok[:], [[P, TILES]], base=0, channel_multiplier=1).then_inc(consts2, 1)
            pool.iota(reg0[:], [[REGION, EXPERTS]], base=0, channel_multiplier=0,
                      allow_small_or_imprecise_dtypes=True).then_inc(consts2, 1)
            pool.iota(steps_of[:], [[RT, TOKENS // RT]], base=0, channel_multiplier=0,
                      allow_small_or_imprecise_dtypes=True).then_inc(consts2, 1)
            pool.iota(tnum[:], [[1, NT]], base=0, channel_multiplier=0,
                      allow_small_or_imprecise_dtypes=True).then_inc(consts2, 1)
            pool.wait_ge(consts2, 9)
            pool.affine_select(out=ident_h[:], in_=ident_h[:], compare_op=ALU.not_equal, fill=1.0, base=0,
                               pattern=[[-1, P]], channel_multiplier=1).then_inc(consts2, 1)
            pool.affine_select(out=before[:], in_=before[:], compare_op=ALU.is_ge, fill=1.0, base=0,
                               pattern=[[-1, P]], channel_multiplier=1).then_inc(consts2, 1)
            pool.memset(v_s[:], 0.0).then_inc(zeroed, 1)
            for n in POOL_JOBS:
                if n == 4:
                    pool.wait_ge(c_split, 2)
                    pool.memset(kbd[:], 0.0).then_inc(zeroed, 1)
                slot = n % SLOTS
                pool.wait_ge(w_hi, n + 1)
                for rows, lo, hi in job_parts(jobs[n]):
                    last = pool.tensor_tensor(dst_flat(jobs[n], 1)[0:rows, lo:hi], stage[slot][0:rows, lo:hi],
                                              dst_flat(jobs[n], 0)[0:rows, lo:hi], ALU.subtract)
                last.then_inc(w_split_p, 1)
            pool.wait_ge(w_split_p, 3)
            pool.memset(pt_s[:].rearrange("p a h n -> p (a h n)").bitcast(F32), 0.0).then_inc(pt_zeroed, 1)

            def keys(t):
                v = prob[:, t, :].rearrange("p (h j) -> p h j", j=CTX)
                return [(v[:, :, 0:ORG], 0, ORG), (v[:, :, ORG:CTX], 1, IPA)]

            def shift(b, t):
                pool.wait_ge(mx_done, 2 * b + t + 1)
                heads = HEADS // 2 if t == 0 else HEADS
                for v, w, n in keys(t):
                    last = pool.tensor_tensor(
                        v[:, 0:heads, :], v[:, 0:heads, :],
                        mx[:, t, w, 0:heads].unsqueeze(2).to_broadcast([P, heads, n]), ALU.subtract)
                last.then_inc(shifted, 1)

            def normalise(b, t):
                pool.wait_ge(rc_done, 2 * b + t + 1)
                for v, w, n in keys(t):
                    last = pool.tensor_tensor(v, v, rc[:, t, w, :].unsqueeze(2).to_broadcast([P, HEADS, n]),
                                              ALU.mult)
                last.then_inc(p_ready, 1)

            def row_low(b):
                pool.wait_ge(row_hi, b + 1)
                pool.tensor_tensor(row[:, :, DM:2 * DM], x2n[:], row[:, :, 0:DM], ALU.subtract).then_inc(row_lo, 1)

            def scatter(b):
                pool.wait_ge(slots, b + 2)
                pool.wait_ge(row_meta, b + 1)
                pool.wait_ge(row_lo, b + 2)
                pool.tensor_tensor(hold_p[:, 0:1], zero8[:, 0:1], zero8[:, 1:2], ALU.add)
                scatter_pick(0)

            def scatter_pick(pick):
                for t in range(TPB):
                    pool.indirect_dma_start(
                        rows_dram, bass.IndirectOffsetOnAxis(ap=slot_i[:, pick, t:t + 1], axis=0),
                        row_words[:, t, :], None).then_inc(scattered, 16)

            def body(b, first, last):
                shift(b, 1)
                normalise(b, 0)
                normalise(b, 1)
                if not first:
                    row_low(b - 1)
                pool.wait_ge(xn_done, b + 1)
                xb = x_sb[:, bass.ds(b * TPB, TPB), :]
                pool.tensor_tensor(xb, xb, bo_sb[:].unsqueeze(1).to_broadcast([P, TPB, DM]), ALU.add
                                   ).then_inc(bo_added, 1)
                pool.wait_ge(fw_hi, b + 1)
                fw = [ffnw[:, part, bass.ds(b, 1), :].rearrange("p e n -> p (e n)") for part in (0, 1)]
                pool.tensor_tensor(fw[1], wstage[:], fw[0], ALU.subtract).then_inc(fw_split, 1)
                if not first:
                    scatter(b - 1)
                if not last:
                    shift(b + 1, 0)
                if not first:
                    scatter_pick(1)

            pool.wait_ge(misc_in, 32)
            shift(0, 0)
            body(0, True, False)
            with pool.Fori(1, BATCH - 1) as b:
                body(b, False, False)
            body(BATCH - 1, False, True)
            pool.wait_ge(fw_split, BATCH)
            pool.memset(pad_rows, 0).then_inc(pad_made, 1)
            pool.wait_ge(pad_made, 3)
            pool.iota(pad_rows[:, :, META // 2:META // 2 + 1], [[0, SUB], [0, 1]], base=TOKENS,
                      channel_multiplier=0).then_inc(pad_made, 1)
            row_low(BATCH - 1)
            scatter(BATCH - 1)
            scatter_pick(1)
            ffn_pool(pool)

        def ipa_k_hi(act):
            act.wait_ge(ipa_mm, 1)
            act.activation(kipa_s[:, 0].rearrange("p m b i -> p (m b i)"), ps_s[:, 0, :], ACT.Copy,
                           scale=1 / WSCALE).then_inc(ipa_hi, 1)

        def ipa_v_hi(act):
            act.wait_ge(ipa_mm, 2)
            act.activation(vipa_s[:, 0, :], ps_s[0:BATCH * IPA, 1:3, :].rearrange("p c n -> p (c n)"), ACT.Copy,
                           scale=1 / WSCALE).then_inc(ipa_hi, 1)

        @block.scalar
        def _(act):
            def split_job(n):
                j, slot = jobs[n], n % SLOTS
                if j in lora_jobs:
                    act.wait_ge(lora_add, 4 * lora_jobs.index(j) + 4)
                else:
                    act.wait_ge(pst_in[slot], 32 * (n // SLOTS + 1))
                scale = WSCALE
                if n in POOL_JOBS:
                    for rows, lo, hi in job_parts(j):
                        last = act.activation(stage[slot][0:rows, lo:hi], stage[slot][0:rows, lo:hi], ACT.Copy,
                                              scale=WSCALE)
                    last.then_inc(w_scaled, 1)
                    act.wait_ge(w_scaled, POOL_JOBS.index(n) + 1)
                    scale = 1.0
                for rows, lo, hi in job_parts(j):
                    last = act.activation(dst_flat(j, 0)[0:rows, lo:hi], stage[slot][0:rows, lo:hi], ACT.Copy,
                                          scale=scale)
                last.then_inc(w_hi, 1)

            def hi_of(dst, src, scale, ready, n, done):
                act.wait_ge(ready, n)
                act.activation(dst, src, ACT.Copy, scale=scale).then_inc(done, 1)

            def xt(b):
                hi_of(xt_s[:, 0].rearrange("p k n -> p (k n)"), ps_b[:, 1, :], 1.0, xt_mm, b + 1, xt_hi)

            def q(b, k):
                hi_of(q_s[:, 0, 2 * k:2 * k + 2, :].rearrange("p m n -> p (m n)"), ps_a[:, k % 3, :],
                      1 / WSCALE, q_mm, 4 * b + k + 1, q_hi)

            def k_(b, k):
                act.wait_ge(k_mm, 2 * b + k + 1)
                for half in (0, 1):
                    o = half * DH
                    last = act.activation(
                        kbd[o:o + DH, 0, 4 * k:4 * k + 4, half * CTX:half * CTX + ORG],
                        ps_b[o:o + DH, 1 - k, 0:4 * ORG].rearrange("p (m j) -> p m j", m=4), ACT.Copy,
                        scale=1 / WSCALE)
                last.then_inc(k_hi, 1)

            def put_kipa(b):
                for half in (0, 1):
                    o = half * DH
                    last = act.activation(
                        kbd[o:o + DH, :, :, half * CTX + ORG:half * CTX + CTX].rearrange("p a m j -> p (a m) j"),
                        kipa_s[o:o + DH, :, :, bass.ds(b, 1), :].rearrange("p a m b j -> p (a m) (b j)"), ACT.Copy)
                last.then_inc(kipa_put, 1)

            def v(b, k):
                hi_of(v_s[0:ORG, 0, k * 512:k * 512 + 512], ps_b[0:ORG, 1 - k, :], 1 / WSCALE, v_mm,
                      2 * b + k + 1, v_hi)

            def copy_scores(b, t):
                act.wait_ge(s_mm, 2 * b + t + 1)
                for c in range(3):
                    w = min(3, PAIRS - 3 * c) * 2 * CTX
                    last = act.activation(prob[:, t, c * 6 * CTX:c * 6 * CTX + w], ps_s[:, c, 0:w], ACT.Copy)
                last.then_inc(s_copied, 1)

            def exp(b, t):
                act.wait_ge(shifted, 2 * b + t + 1)
                if t == 0:
                    act.wait_ge(shifted_half, b + 1)
                act.activation(prob[:, t, :], prob[:, t, :], ACT.Exp, scale=DH ** -0.5).then_inc(exp_done, 1)

            def pt(b, k):
                t, h = k // 4, HPB * (k % 4)
                hi_of(pt_s[0:CTX, 0, h:h + HPB, t * P:t * P + P],
                      probs_bank(k)[0:CTX, :].rearrange("p (h n) -> p h n", h=HPB), PSCALE, t_mm, 8 * b + k + 1,
                      pt_hi)

            def ot(b, k):
                hi_of(ot_s[:, 0, 2 * k:2 * k + 2, :].rearrange("p m n -> p (m n)"), heads_bank(k),
                      1 / (PSCALE), pv_mm, 4 * b + k + 1, ot_hi)

            def std_2(b):
                act.wait_ge(var2, b + 1)
                act.activation(ln2_s[:, 1, :], ln2_s[:, 0, :], ACT.Sqrt).then_inc(std2, 1)

            def row_high(b):
                act.wait_ge(x2n_done, b + 1)
                act.wait_ge(scattered, 64 * b + 16)
                act.activation(row[:, :, 0:DM], x2n[:], ACT.Copy).then_inc(row_hi, 1)

            def x2t_copy(b):
                act.wait_ge(x2_mm, b + 1)
                act.activation(x2t[:].rearrange("p k n -> p (k n)"), ps_a[:, 2, :], ACT.Copy).then_inc(x2_copied, 1)

            def gap_e(b):
                act.wait_ge(gap_done, b + 1)
                act.activation(gap_exp[:], gap[:], ACT.Exp).then_inc(gap_expd, 1)

            def body(b, first, last):
                copy_scores(b, 0)
                if not last:
                    xt(b + 1)
                copy_scores(b, 1)
                exp(b, 0)
                if not last:
                    q(b + 1, 0)
                    q(b + 1, 1)
                    q(b + 1, 2)
                exp(b, 1)
                if first:
                    act.wait_ge(pt_zeroed, 1)
                pt(b, 0)
                if not last:
                    q(b + 1, 3)
                pt(b, 1)
                if not first:
                    std_2(b - 1)
                pt(b, 2)
                pt(b, 3)
                if not last:
                    k_(b + 1, 0)
                    k_(b + 1, 1)
                    put_kipa(b + 1)
                for k in range(4, 8):
                    pt(b, k)
                    if k == 4 and not first:
                        row_high(b - 1)
                if not first:
                    x2t_copy(b - 1)
                act.wait_ge(fw_in, 16 * b + 16)
                act.activation(wstage[:], wstage[:], ACT.Copy, scale=WSCALE).then_inc(fw_scaled, 1)
                act.wait_ge(fw_scaled, b + 1)
                act.activation(ffnw[:, 0, bass.ds(b, 1), :].rearrange("p e n -> p (e n)"), wstage[:], ACT.Copy
                               ).then_inc(fw_hi, 1)
                for k in range(4):
                    ot(b, k)
                if not first:
                    gap_e(b - 1)
                if not last:
                    v(b + 1, 0)
                    v(b + 1, 1)

            split_job(0)
            split_job(1)
            for kk, rows in enumerate((P, CDR)):
                act.wait_ge(ctx_in[kk], 16)
                act.activation(ctx_s[0:rows, 0, kk, :], cstage[kk][0:rows, 0:BATCH * CTX], ACT.Copy).then_inc(c_hi, 1)
            split_job(2)
            split_job(3)
            split_job(4)
            act.wait_ge(ln_var, 1)
            act.activation(ln_std[:], ln_tmp[:, 5, :], ACT.Sqrt).then_inc(ln_sqrt, 1)
            xt(0)
            q(0, 0)
            q(0, 1)
            q(0, 2)
            q(0, 3)
            split_job(5)
            act.wait_ge(zeroed, 2)
            k_(0, 0)
            k_(0, 1)
            ipa_k_hi(act)
            ipa_v_hi(act)
            act.wait_ge(ipa_split, 4)
            put_kipa(0)
            v(0, 0)
            v(0, 1)
            body(0, True, False)
            with act.Fori(1, BATCH - 1) as b:
                body(b, False, False)
            body(BATCH - 1, False, True)
            std_2(BATCH - 1)
            row_high(BATCH - 1)
            x2t_copy(BATCH - 1)
            gap_e(BATCH - 1)
            ffn_act(act)

        @block.vector
        def _(dve):
            links = [0]

            def link(ins):
                links[0] += 1
                ins.then_inc(ln_link, 1)
                dve.wait_ge(ln_link, links[0])

            def layer_stats(n):
                me, mo, cve, cvo = (stats[:, :, c] for c in (1, 4, 2, 5))
                tmp = [ln_tmp[:, c, :] for c in range(6)]
                link(dve.tensor_tensor(tmp[0], me, mo, ALU.add))
                link(dve.tensor_tensor(tmp[1], me, mo, ALU.subtract))
                link(dve.tensor_tensor(tmp[2], cve, cvo, ALU.add))
                link(dve.tensor_scalar(ln_mean[:], tmp[0], 0.5, None, ALU.mult))
                link(dve.tensor_tensor(tmp[3], tmp[1], tmp[1], ALU.mult))
                link(dve.tensor_scalar(tmp[4], tmp[2], 1.0 / DM, LN_EPS, ALU.mult, ALU.add))
                dve.scalar_tensor_tensor(out=tmp[5], in0=tmp[3], scalar=0.25, in1=tmp[4], op0=ALU.mult,
                                         op1=ALU.add).then_inc(ln_var, 1)
                dve.wait_ge(ln_sqrt, n)
                link(dve.reciprocal(ln_rstd[:], ln_std[:]))

            def lo_of(dst, src, scale, hi, ready, n, done):
                dve.wait_ge(ready, n)
                dve.scalar_tensor_tensor(out=dst, in0=src, scalar=scale, in1=hi, op0=ALU.mult, op1=ALU.subtract
                                         ).then_inc(done, 1)

            def scale_down(n):
                dve.wait_ge(lora_in[n], 48)
                dve.tensor_scalar(downs[lora_jobs[n]], downs[lora_jobs[n]], alphas[:, n:n + 1], 1.0 / RANK, ALU.mult,
                                  ALU.mult).then_inc(downs_ok, 1)

            def job_adds(n, between=None):
                j, slot = jobs[n], n % SLOTS
                dve.wait_ge(pst_in[slot], 32 * (n // SLOTS + 1))
                li = lora_jobs.index(j)
                for u in range(4):
                    rows = P if u < 2 or j in ("q", "o") else CDR
                    dve.wait_ge(lora_mm, 4 * li + u + 1)
                    piece = stage[slot][0:rows, u * 512:u * 512 + 512]
                    dve.tensor_tensor(piece, ps_s[0:rows, (4 * li + u) % 3, :], piece, ALU.add
                                      ).then_inc(lora_add, 1)
                    if between:
                        between(u)

            def job_lo(n):
                j, slot = jobs[n], n % SLOTS
                dve.wait_ge(w_hi, n + 1)
                for rows, lo, hi in job_parts(j):
                    last = dve.scalar_tensor_tensor(
                        out=dst_flat(j, 1)[0:rows, lo:hi], in0=stage[slot][0:rows, lo:hi], scalar=WSCALE,
                        in1=dst_flat(j, 0)[0:rows, lo:hi], op0=ALU.mult, op1=ALU.subtract)
                last.then_inc(w_split, 1)

            dve.memset(hold[:], 0.0).then_inc(slots, 1)
            dve.memset(gap[:], 0.0).then_inc(row_lo, 1)
            for w in (wk_s, wv_s, kipaw, vipaw, ctx_s):
                for part in (0, 1):
                    last = dve.memset(w[CDR:P, part, 1, :].bitcast(F32), 0.0)
            last.then_inc(rows_zeroed, 1)
            def bn(first, count):
                for t in range(first, first + count):
                    if t % 8 == 0:
                        dve.wait_ge(x_in[t // 8], 16)
                    dve.bn_stats(stats[:, t, :], x_sb[:, t, :]).then_inc(st_done, 1)

            def normalise_x(b):
                for t in range(TPB):
                    tile = b * TPB + t
                    last = dve.tensor_scalar(
                        xn[:, t, :], x_sb[:, bass.ds(tile, 1), :].rearrange("p t d -> p (t d)"),
                        ln_mean[:, bass.ds(tile, 1)], ln_rstd[:, bass.ds(tile, 1)], ALU.subtract, ALU.mult)
                last.then_inc(xn_done, 1)

            def xt(b):
                lo_of(xt_s[:, 1].rearrange("p k n -> p (k n)"), ps_b[:, 1, :], 1.0,
                      xt_s[:, 0].rearrange("p k n -> p (k n)"), xt_hi, b + 1, xt_split)

            def q(b, k):
                lo_of(q_s[:, 1, 2 * k:2 * k + 2, :].rearrange("p m n -> p (m n)"), ps_a[:, k % 3, :], 1 / WSCALE,
                      q_s[:, 0, 2 * k:2 * k + 2, :].rearrange("p m n -> p (m n)"), q_hi, 4 * b + k + 1, q_split)

            def k_(b, k):
                dve.wait_ge(k_hi, 2 * b + k + 1)
                for half in (0, 1):
                    o = half * DH
                    last = dve.scalar_tensor_tensor(
                        out=kbd[o:o + DH, 1, 4 * k:4 * k + 4, half * CTX:half * CTX + ORG],
                        in0=ps_b[o:o + DH, 1 - k, 0:4 * ORG].rearrange("p (m j) -> p m j", m=4), scalar=1 / WSCALE,
                        in1=kbd[o:o + DH, 0, 4 * k:4 * k + 4, half * CTX:half * CTX + ORG], op0=ALU.mult,
                        op1=ALU.subtract)
                last.then_inc(k_split, 1)

            def v(b, k):
                lo_of(v_s[0:ORG, 1, k * 512:k * 512 + 512], ps_b[0:ORG, 1 - k, :], 1 / WSCALE,
                      v_s[0:ORG, 0, k * 512:k * 512 + 512], v_hi, 2 * b + k + 1, v_split)

            def keys(t):
                vw = prob[:, t, :].rearrange("p (h j) -> p h j", j=CTX)
                return [(vw[:, :, 0:ORG], 0), (vw[:, :, ORG:CTX], 1)]

            def maxima(b, t):
                dve.wait_ge(s_copied, 2 * b + t + 1)
                for vw, w in keys(t):
                    last = dve.tensor_reduce(mx[:, t, w, :], vw, AX, ALU.max)
                last.then_inc(mx_done, 1)

            def shift_half(b):
                dve.wait_ge(mx_done, 2 * b + 1)
                half = HEADS // 2
                for vw, w in keys(0):
                    n = ORG if w == 0 else IPA
                    last = dve.tensor_tensor(
                        vw[:, half:HEADS, :], vw[:, half:HEADS, :],
                        mx[:, 0, w, half:HEADS].unsqueeze(2).to_broadcast([P, half, n]), ALU.subtract)
                last.then_inc(shifted_half, 1)

            def sums(b, t):
                dve.wait_ge(exp_done, 2 * b + t + 1)
                for vw, w in keys(t):
                    last = dve.tensor_reduce(sm[:, t, w, :], vw, AX, ALU.add)
                last.then_inc(sum_done, 1)
                dve.wait_ge(sum_done, 2 * b + t + 1)
                dve.reciprocal(rc[:, t], sm[:, t]).then_inc(rc_done, 1)

            def pt(b, k):
                t, h = k // 4, HPB * (k % 4)
                lo_of(pt_s[0:CTX, 1, h:h + HPB, t * P:t * P + P],
                      probs_bank(k)[0:CTX, :].rearrange("p (h n) -> p h n", h=HPB), PSCALE,
                      pt_s[0:CTX, 0, h:h + HPB, t * P:t * P + P], pt_hi, 8 * b + k + 1, pt_split)

            def ot(b, k):
                lo_of(ot_s[:, 1, 2 * k:2 * k + 2, :].rearrange("p m n -> p (m n)"), heads_bank(k),
                      1 / (PSCALE), ot_s[:, 0, 2 * k:2 * k + 2, :].rearrange("p m n -> p (m n)"), ot_hi,
                      4 * b + k + 1, ot_split)

            def residual(b):
                dve.wait_ge(wo_mm, b + 1)
                dve.wait_ge(bo_added, b + 1)
                xb = x_sb[:, bass.ds(b * TPB, TPB), :].rearrange("p t d -> p (t d)")
                dve.scalar_tensor_tensor(out=xb, in0=ps_b[:, 0, :], scalar=1 / WSCALE, in1=xb, op0=ALU.mult,
                                         op1=ALU.add).then_inc(x1_done, 1)
                dve.wait_ge(x1_done, b + 1)
                dve.memset(hold[:], 0.0)
                for t in range(TPB):
                    tile = b * TPB + t
                    last = dve.bn_stats(st2[:, t, :], x_sb[:, bass.ds(tile, 1), :].rearrange("p t d -> p (t d)"))
                last.then_inc(st2_done, 1)
                dve.wait_ge(st2_done, b + 1)
                dve.memset(hold[:], 0.0)
                for t in range(TPB):
                    last = dve.bn_aggr(ln2[:, t, :], st2[:, t, :])
                last.then_inc(ag2_done, 1)
                dve.wait_ge(ag2_done, b + 1)
                dve.tensor_scalar(ln2_s[:, 0, :], ln2[:, :, 1], LN_EPS, None, ALU.add).then_inc(var2, 1)

            def normalise_2(b):
                dve.wait_ge(std2, b + 1)
                dve.reciprocal(ln2_s[:, 2, :], ln2_s[:, 1, :]).then_inc(rstd2, 1)
                dve.wait_ge(rstd2, b + 1)
                for t in range(TPB):
                    last = dve.tensor_scalar(
                        x2n[:, t, :], x_sb[:, bass.ds(b * TPB + t, 1), :].rearrange("p t d -> p (t d)"),
                        ln2[:, t, 0:1], ln2_s[:, 2, t:t + 1], ALU.subtract, ALU.mult)
                last.then_inc(x2n_done, 1)

            class Chain:

                def __init__(self, b, per):
                    self.b, self.per, self.n = b, per, 0

                def step(self, ins):
                    self.n += 1
                    ins.then_inc(route, 1)
                    dve.wait_ge(route, self.b * self.per + self.n)

            ROUTE = 13

            def pick_experts(b):
                c = Chain(b, ROUTE)
                dve.wait_ge(lg_mm, b + 1)
                c.step(dve.tensor_copy(lg[:].rearrange("p t e -> p (t e)"), ps_s[:, 2, 0:TPB * EXPERTS]))
                dve.memset(hold[:], 0.0)
                for t in range(TPB):
                    last = dve.max(top[:, t, :], lg[:, t, :])
                c.step(last)
                dve.tensor_tensor(gap[:], top[:, :, 1], top[:, :, 0], ALU.subtract).then_inc(gap_done, 1)
                for t in range(TPB):
                    last = dve.max_index(top_i[:, t, :], top[:, t, :], lg[:, t, :])
                c.step(last)
                c.step(dve.tensor_copy(top_f[:], top_i[:]))
                io = iota8[:].unsqueeze(1).to_broadcast([P, TPB, EXPERTS])
                for pick in range(TOPK):
                    last = dve.tensor_tensor(
                        picks[:, pick], io, top_f[:, :, pick:pick + 1].to_broadcast([P, TPB, EXPERTS]), ALU.is_equal)
                c.step(last)
                dve.tensor_tensor(both[:], picks[:, 0], picks[:, 1], ALU.add).then_inc(both_done, 1)
                return c

            def weigh_and_place(b, c):
                dve.wait_ge(rank_mm, b + 1)
                rank = ps_a[:, 0, 0:TPB * EXPERTS].rearrange("p (t e) -> p t e", t=TPB)
                base = counts[:].unsqueeze(1).to_broadcast([P, TPB, EXPERTS])
                c.step(dve.tensor_tensor(place[:], rank, base, ALU.add))
                c.step(dve.tensor_tensor(place[:], place[:], reg0[:].unsqueeze(1).to_broadcast([P, TPB, EXPERTS]),
                                         ALU.add))
                dve.tensor_tensor(counts[:], ps_a[:, 0, TPB * EXPERTS:(TPB + 1) * EXPERTS], counts[:], ALU.add)
                for pick in range(TOPK):
                    last = dve.tensor_tensor(picked[:, pick], picks[:, pick], place[:], ALU.mult)
                c.step(last)
                c.step(dve.tensor_reduce(slot_f[:].rearrange("p k t -> p (k t)"),
                                         picked[:].rearrange("p k t e -> p (k t) e"), AX, ALU.add))
                dve.tensor_copy(slot_i[:], slot_f[:]).then_inc(slots, 1)
                dve.wait_ge(gap_expd, b + 1)
                c.step(dve.tensor_scalar(w_sum[:], gap_exp[:], 1.0, None, ALU.add))
                meta = row[:, :, META:META + 8].bitcast(F32)
                dve.wait_ge(scattered, 64 * b + 16)
                c.step(dve.reciprocal(w_a[:], w_sum[:]))
                c.step(dve.tensor_tensor(meta[:, :, 3], w_a[:], gap_exp[:], ALU.mult))
                dve.tensor_tensor(meta[:, :, 2], w_a[:], meta[:, :, 3], ALU.subtract)
                dve.tensor_copy(meta[:, :, 1], top_f[:, :, 0])
                dve.tensor_copy(row[:, :, META:META + 8].bitcast(I32)[:, :, 0], tok[:, bass.ds(b * TPB, TPB)]
                                ).then_inc(row_meta, 1)
                c.step(dve.memset(hold[:], 0.0))
                assert c.n == ROUTE, c.n

            def body(b, first, last, x_left):
                maxima(b, 0)
                shift_half(b)
                if not last:
                    xt(b + 1)
                maxima(b, 1)
                sums(b, 0)
                if not last:
                    q(b + 1, 0)
                if not first:
                    residual(b - 1)
                if not last:
                    q(b + 1, 1)
                    q(b + 1, 2)
                sums(b, 1)
                pt(b, 0)
                if not last:
                    q(b + 1, 3)
                pt(b, 1)
                if not first:
                    normalise_2(b - 1)
                pt(b, 2)
                pt(b, 3)
                if not last:
                    k_(b + 1, 0)
                for k in range(4, 8):
                    pt(b, k)
                if not last:
                    k_(b + 1, 1)
                if not first:
                    chain = pick_experts(b - 1)
                if x_left:
                    dve.wait_ge(row_lo, b + 1)
                    normalise_x(b + 2)
                for k in range(4):
                    ot(b, k)
                if not first:
                    weigh_and_place(b - 1, chain)
                if not last:
                    v(b + 1, 0)
                    v(b + 1, 1)

            scale_down(0)
            scale_down(1)
            job_adds(0)
            scale_down(2)
            job_lo(0)
            job_adds(1, lambda u: bn(2 * u, 2))
            scale_down(3)
            job_lo(1)
            for kk, rows in enumerate((P, CDR)):
                lo_of(ctx_s[0:rows, 1, kk, :], cstage[kk][0:rows, 0:BATCH * CTX], 1.0, ctx_s[0:rows, 0, kk, :],
                      c_hi, kk + 1, c_split)
            job_adds(3, lambda u: bn(8 + 4 * u, 4))
            job_lo(3)
            job_adds(5, lambda u: bn(24 + 2 * u, 2))
            dve.wait_ge(st_done, TILES)
            layer_stats(1)
            normalise_x(0)
            xt(0)
            for k in range(4):
                q(0, k)
            k_(0, 0)
            k_(0, 1)
            dve.wait_ge(ipa_hi, 1)
            dve.scalar_tensor_tensor(
                out=kipa_s[:, 1].rearrange("p m b i -> p (m b i)"), in0=ps_s[:, 0, :], scalar=1 / WSCALE,
                in1=kipa_s[:, 0].rearrange("p m b i -> p (m b i)"), op0=ALU.mult, op1=ALU.subtract
            ).then_inc(ipa_split, 2)
            dve.wait_ge(ipa_hi, 2)
            dve.scalar_tensor_tensor(
                out=vipa_s[:, 1, :], in0=ps_s[0:BATCH * IPA, 1:3, :].rearrange("p c n -> p (c n)"),
                scalar=1 / WSCALE, in1=vipa_s[:, 0, :], op0=ALU.mult, op1=ALU.subtract
            ).then_inc(ipa_split, 2)
            normalise_x(1)
            v(0, 0)
            v(0, 1)
            body(0, True, False, True)
            with dve.Fori(1, BATCH - 2) as b:
                body(b, False, False, True)
            body(BATCH - 2, False, False, False)
            body(BATCH - 1, False, True, False)
            residual(BATCH - 1)
            normalise_2(BATCH - 1)
            weigh_and_place(BATCH - 1, pick_experts(BATCH - 1))
            ffn_dve(dve)

        THREE = ((0, 0), (0, 1), (1, 0))

        @block.tensor
        def _(pe):
            def product(o, lhs, rhs, terms):
                steps = [(n, a, c) for n in range(terms) for a, c in THREE]
                for i, (n, a, c) in enumerate(steps):
                    last = pe.matmul(o, lhs(a, n), rhs(c, n), start=(i == 0), stop=(i == len(steps) - 1))
                return last

            def lora_products(j):
                li = lora_jobs.index(j)
                for u in range(4):
                    if 4 * li + u >= 3:
                        pe.wait_ge(lora_add, 4 * li + u - 2)
                    bank = (4 * li + u) % 3
                    if j == "o":
                        for c in (0, 1):
                            p = 2 * u + c
                            last = pe.matmul(ps_s[:, bank, c * DM:c * DM + DM], downs[j][:, p * P:p * P + P], ups[j],
                                             start=True, stop=True)
                    else:
                        kk, n = u // 2, u % 2
                        rows = P if kk == 0 or j == "q" else CDR
                        last = pe.matmul(ps_s[0:rows, bank, :], downs[j][:, kk * P:kk * P + rows],
                                         ups[j][:, n * 512:n * 512 + 512], start=True, stop=True)
                    last.then_inc(lora_mm, 1)

            def transpose_x(b):
                pe.wait_ge(xn_done, b + 1)
                for kk in range(KD):
                    for t in range(TPB):
                        c = kk * SEQ + t * P
                        last = pe.transpose(ps_b[:, 1, c:c + P], xn[:, t, kk * P:kk * P + P], ident[:])
                last.then_inc(xt_mm, 1)

            def queries(b, k):
                for m in (2 * k, 2 * k + 1):
                    o = (m % 2) * SEQ
                    last = product(ps_a[:, k % 3, o:o + SEQ], lambda a, n: wq_s[:, a, n, m * P:m * P + P],
                                   lambda a, n: xt_s[:, a, n, :], KD)
                last.then_inc(q_mm, 1)

            def context(part, kk, b):
                return ctx_s[:, part, kk, bass.ds(b * ORG, ORG)]

            def new_keys(b, k):
                for m in range(4 * k, 4 * k + 4):
                    o = (m % 4) * ORG
                    last = product(ps_b[:, 1 - k, o:o + ORG], lambda a, n: wk_s[:, a, n, m * P:m * P + P],
                                   lambda a, n: context(a, n, b), KD)
                last.then_inc(k_mm, 1)

            def new_values(b, k):
                product(ps_b[0:ORG, 1 - k, :], lambda a, n: context(a, n, b),
                        lambda a, n: wv_s[:, a, n, k * 512:k * 512 + 512], KD).then_inc(v_mm, 1)

            def scores(b, t):
                pe.wait_ge(s_copied, 2 * b + t)
                if t == 0:
                    pe.wait_ge(q_split, 4 * b + 4)
                    pe.wait_ge(k_split, 2 * b + 2)
                    pe.wait_ge(kipa_put, b + 1)
                for p in range(PAIRS):
                    o = (p % 3) * 2 * CTX
                    last = product(ps_s[:, p // 3, o:o + 2 * CTX], lambda a, n: q_s[:, a, p, t * P:t * P + P],
                                   lambda a, n: kbd[:, a, p, :], 1)
                last.then_inc(s_mm, 1)

            def transpose_probs(b, k):
                t, h = k // 4, HPB * (k % 4)
                if k % 4 == 0:
                    pe.wait_ge(p_ready, 2 * b + t + 1)
                for c in range(HPB):
                    last = pe.transpose(probs_bank(k)[0:CTX, c * P:c * P + P],
                                        prob[:, t, (h + c) * CTX:(h + c + 1) * CTX], ident[:])
                last.then_inc(t_mm, 1)

            def attend(b, k):
                for p in (2 * k, 2 * k + 1):
                    o = (p % 2) * SEQ
                    for i, (a, c) in enumerate(THREE):
                        for half in (0, 1):
                            h = 2 * p + half
                            last = pe.matmul(heads_bank(k)[half * DH:half * DH + DH, o:o + SEQ],
                                             v_s[:, a, h * DH:h * DH + DH], pt_s[:, c, h, :],
                                             start=(i == 0), stop=(i == 2))
                last.then_inc(pv_mm, 1)

            def project(b, t):
                pe.wait_ge(ot_split, 4 * b + 4)
                last = product(ps_b[:, 0, t * DM:t * DM + DM], lambda a, n: ot_s[:, a, n, t * P:t * P + P],
                               lambda a, n: wo_s[:, a, n, :], PAIRS)
                if t == TPB - 1:
                    last.then_inc(wo_mm, 1)

            pe.wait_ge(consts, 3)
            pe.wait_ge(consts2, 11)
            for n, j in enumerate(lora_jobs):
                pe.wait_ge(downs_ok, n + 1)
                lora_products(j)
            transpose_x(0)
            pe.wait_ge(w_split, 1)
            pe.wait_ge(xt_split, 1)
            for k in range(4):
                if k == 3:
                    pe.wait_ge(q_split, 1)
                queries(0, k)
            pe.wait_ge(rows_zeroed, 1)
            pe.wait_ge(c_split, 2)
            pe.wait_ge(w_split, 2)
            new_keys(0, 0)
            new_keys(0, 1)
            pe.wait_ge(w_split_p, 1)
            pe.wait_ge(lora_add, 16)
            for m in range(PAIRS):
                last = product(ps_s[:, 0, m * 64:m * 64 + 64], lambda a, n: kipaw[:, a, n, m * P:m * P + P],
                               lambda a, n: ctx_s[:, a, n, BATCH * ORG:BATCH * CTX], KD)
            last.then_inc(ipa_mm, 1)
            pe.wait_ge(w_split_p, 2)
            for c in (0, 1):
                last = product(ps_s[0:BATCH * IPA, 1 + c, :], lambda a, n: ctx_s[:, a, n, BATCH * ORG:BATCH * CTX],
                               lambda a, n: vipaw[:, a, n, c * 512:c * 512 + 512], KD)
            last.then_inc(ipa_mm, 1)
            pe.wait_ge(w_split, 3)
            pe.wait_ge(k_split, 1)
            new_values(0, 0)
            pe.wait_ge(k_split, 2)
            new_values(0, 1)
            pe.wait_ge(ipa_split, 4)

            def transpose_2(b):
                pe.wait_ge(x2n_done, b + 1)
                for kk in range(KD):
                    for t in range(TPB):
                        c = kk * SEQ + t * P
                        last = pe.transpose(ps_a[:, 2, c:c + P], x2n[:, t, kk * P:kk * P + P], ident[:])
                last.then_inc(x2_mm, 1)

            def router(b):
                pe.wait_ge(x2_copied, b + 1)
                for t in range(TPB):
                    c = t * EXPERTS
                    for kk in range(KD):
                        last = pe.matmul(ps_s[:, 2, c:c + EXPERTS], x2t[:, kk, t * P:t * P + P], gate_f[:, kk, :],
                                         start=(kk == 0), stop=(kk == KD - 1))
                last.then_inc(lg_mm, 1)

            def rank(b):
                pe.wait_ge(both_done, b + 1)
                bank = ps_a[:, 0, :]
                pe.matmul(bank[:, 0:8], before[:], both[:, 0, :], start=True, stop=True)
                pe.matmul(bank[:, 8:16], before[:], both[:, 1, :], start=True, stop=False)
                pe.matmul(bank[:, 8:16], ones[:], both[:, 0, :], start=False, stop=True)
                pe.matmul(bank[:, 16:24], ones[:], both[:, 0, :], start=True, stop=False)
                pe.matmul(bank[:, 16:24], ones[:], both[:, 1, :], start=False, stop=True).then_inc(rank_mm, 1)

            def body(b, first, last):
                if not first:
                    pe.wait_ge(ot_split, 4 * b)
                scores(b, 0)
                if not last:
                    pe.wait_ge(v_split, 2 * b + 1)
                    transpose_x(b + 1)
                scores(b, 1)
                if not first:
                    pe.wait_ge(v_split, 2 * b + 2)
                    project(b - 1, 0)
                    project(b - 1, 1)
                if not last:
                    pe.wait_ge(xt_split, b + 2)
                    if not first:
                        pe.wait_ge(slots, b)
                    pe.wait_ge(pt_split, 8 * b)
                    queries(b + 1, 0)
                    queries(b + 1, 1)
                    queries(b + 1, 2)
                else:
                    pe.wait_ge(slots, b)
                    pe.wait_ge(pt_split, 8 * b)
                pe.wait_ge(s_copied, 2 * b + 2)
                transpose_probs(b, 0)
                transpose_probs(b, 1)
                if not last:
                    pe.wait_ge(q_split, 4 * b + 5)
                    queries(b + 1, 3)
                    pe.wait_ge(q_split, 4 * b + 6)
                transpose_probs(b, 2)
                if not last:
                    pe.wait_ge(q_split, 4 * b + 7)
                transpose_probs(b, 3)
                if not last:
                    new_keys(b + 1, 0)
                    if first:
                        pe.wait_ge(v_split, 2)
                    new_keys(b + 1, 1)
                    pe.wait_ge(q_split, 4 * b + 8)
                for k in range(4, 8):
                    if k >= 5:
                        pe.wait_ge(pt_split, 8 * b + k - 4)
                    transpose_probs(b, k)
                if not first:
                    pe.wait_ge(pt_split, 8 * b + 4)
                    transpose_2(b - 1)
                    router(b - 1)
                pe.wait_ge(pt_split, 8 * b + 8)
                pe.wait_ge(v_split, 2 * b + 2)
                pe.wait_ge(vipa_in, 16 * b + 16)
                if first:
                    pe.wait_ge(w_split_p, 3)
                for k in range(4):
                    if k < 2 and not last:
                        pe.wait_ge(k_split, 2 * b + 3 + k)
                    attend(b, k)
                if not first:
                    rank(b - 1)
                if not last:
                    for k in (0, 1):
                        pe.wait_ge(ot_split, 4 * b + 1 + k)
                        new_values(b + 1, k)

            body(0, True, False)
            with pe.Fori(1, BATCH - 1) as b:
                body(b, False, False)
            body(BATCH - 1, False, True)
            for t in range(TPB):
                project(BATCH - 1, t)
            transpose_2(BATCH - 1)
            router(BATCH - 1)
            rank(BATCH - 1)
            ffn_pe(pe, product)



def kernel(**inputs):
    import numpy as _np
    import concourse.bacc as _bacc
    from concourse.bass_utils import run_bass_kernel_spmd as _run

    i = {n.replace("L0_xattn_", "").replace("L0_ffn_", ""): _np.asarray(a) for n, a in inputs.items()}
    c = i["ctx_768"]
    ctx_t = _np.concatenate([c[:, :ORG].reshape(-1, CD), c[:, ORG:].reshape(-1, CD)]).T
    w1 = i["w1"].reshape(EXPERTS, KD, P, DFF).transpose(0, 2, 1, 3).reshape(EXPERTS, 1, P, FW)
    w2 = i["w2"].reshape(EXPERTS, DFF // P, P, DM).transpose(0, 2, 1, 3).reshape(EXPERTS, 1, P, FW)
    ffn_w = _np.concatenate([w1, w2], axis=1).reshape(2 * EXPERTS, P, FW)
    laid = {
        "x": i["x"], "ctx_t": ctx_t, "wq": i["Wq"], "wk": i["Wk"], "wv": i["Wv"], "wo": i["Wo"], "bo": i["bo"],
        "q_down_t": i["q_down"].T, "q_up": i["q_up"], "q_alpha": i["q_alpha"],
        "k_down_t": i["k_down"].T, "k_up": i["k_up"], "k_alpha": i["k_alpha"],
        "v_down_t": i["v_down"].T, "v_up": i["v_up"], "v_alpha": i["v_alpha"],
        "o_down_t": i["o_down"].T, "o_up": i["o_up"], "o_alpha": i["o_alpha"],
        "wk_ipa": i["Wk_ipa"], "wv_ipa": i["Wv_ipa"], "gate_w": i["gate_w"], "ffn_w": ffn_w,
    }
    nc = _bacc.Bacc("TRN2", target_bir_lowering=False, num_devices=1)
    arrays, args = {}, {}
    for name, a in laid.items():
        a = _np.ascontiguousarray(a)
        arrays[f"in_{name}"] = a
        args[name] = nc.dram_tensor(f"in_{name}", a.shape, mybir.dt.from_np(a.dtype), kind="ExternalInput").ap()
    args["out"] = nc.dram_tensor("out_x", (BATCH, SEQ, DM), F32, kind="ExternalOutput").ap()
    build(nc, **args)
    return _run(nc, [arrays], core_ids=[0]).results[0]["out_x"]
```
